# Optimizing a Trainium2 kernel written in Bass

```python
import numpy as np
import jax
import jax.numpy as jnp

def _softmax(x, axis=-1):
    return jax.nn.softmax(x, axis=axis)

def _gelu(x):
    return jax.nn.gelu(x, approximate=True)

def _silu(x):
    return jax.nn.silu(x)

def _sigmoid(x):
    return jax.nn.sigmoid(x)

def _layernorm(x, axis=-1, eps=1e-05):
    m = jnp.mean(x, axis=axis, keepdims=True)
    v = jnp.var(x, axis=axis, keepdims=True)
    return (x - m) / jnp.sqrt(v + eps)

def _scatter_add(tgt, idx, src, axis=0):
    return tgt.at[idx].add(src)

def _segment_sum(src, seg, n):
    return jax.ops.segment_sum(src, seg, n)
kernel_name = 'mk_decoder_preln_d2_seqx_r8_11ed19'

def setup_inputs(seed: int=0):
    np.random.seed(seed)
    _w = jnp.asarray

    def _rec_inputs():
        import jax
        import jax.numpy as jnp
        _rk = jax.random.key(seed)
        x = -0.0002928 + 1 * jax.random.normal(jax.random.fold_in(_rk, 1), (8, 256, 128), jnp.float32)
        _lenS = 256 - jax.random.randint(jax.random.fold_in(_rk, 7), (8,), 0, max(1, 256 // 4) + 1, jnp.int32)
        _lenS2 = 256 - jax.random.randint(jax.random.fold_in(_rk, 8), (8,), 0, max(1, 256 // 4) + 1, jnp.int32)
        _ctx_1024P = jax.random.normal(jax.random.fold_in(_rk, 11), (8, 16, 128), jnp.float32)
        _ctx_1024c = jax.random.dirichlet(jax.random.fold_in(_rk, 511), 0.3 * jnp.ones((16,), jnp.float32), (8, 256))
        _ctx_1024t = jnp.einsum('bsk,bkd->bsd', _ctx_1024c, _ctx_1024P)
        _ctx_1024t = _ctx_1024t * jax.lax.rsqrt(jnp.mean(jnp.square(_ctx_1024t)) + 1e-12) * 0.953939
        ctx_1024 = -1.39393e-06 + 0.999914 * (_ctx_1024t + 0.3 * jax.random.normal(jax.random.fold_in(_rk, 611), (8, 256, 128), jnp.float32))
        return (x, ctx_1024)
    x, ctx_1024 = _rec_inputs()

    def _L0_attn_setup():
        import jax, jax.numpy as jnp
        import numpy as np
        B, T, D_MODEL, D_SSM = (8, 256, 128, 128)
        key = jax.random.key(seed)
        ks = jax.random.split(key, 7)
        sc_in = 1.0 / np.sqrt(D_MODEL)
        sc_ssm = 1.0 / np.sqrt(D_SSM)
        return {'x': jax.random.normal(ks[0], (B, T, D_MODEL), dtype=jnp.float32), 'Wp': jax.random.uniform(ks[1], (D_MODEL, 3 * D_SSM), jnp.float32, -sc_in, sc_in), 'bp': jax.random.uniform(ks[2], (3 * D_SSM,), jnp.float32, -sc_in, sc_in), 'Wu': jax.random.uniform(ks[3], (D_MODEL, D_SSM), jnp.float32, -sc_in, sc_in), 'bu': jax.random.uniform(ks[4], (D_SSM,), jnp.float32, -sc_in, sc_in), 'Wo': jax.random.uniform(ks[5], (D_SSM, D_MODEL), jnp.float32, -sc_ssm, sc_ssm), 'bo': jax.random.uniform(ks[6], (D_MODEL,), jnp.float32, -sc_ssm, sc_ssm)}
    _L0_attn_all = _L0_attn_setup()
    _L0_attn_in = {k: v for k, v in _L0_attn_all.items() if k in ('Wp', 'bp', 'Wu', 'bu', 'Wo', 'bo')}
    del _L0_attn_all

    def _L0_xattn_setup():
        import jax, jax.numpy as jnp
        import numpy as np
        B, S, E, NH = (2, 256, 128, 4)
        HD = E // NH

        def _mlstm_head(q, k, v, ig, fg, eps=1e-06):
            s, dh = q.shape
            log_f = jax.nn.log_sigmoid(fg)
            cs = jnp.concatenate([jnp.zeros((1, 1), log_f.dtype), jnp.cumsum(log_f, axis=0)], axis=0)
            neg = jnp.asarray(-0.7 * jnp.finfo(cs.dtype).max, cs.dtype)
            log_d = jnp.where(jnp.tri(s, dtype=bool), (cs - cs.T)[1:, 1:] + ig.T, neg)
            m = jnp.max(log_d, axis=-1, keepdims=True)
            d = jnp.exp(log_d - m)
            c = q @ (k.T / jnp.sqrt(dh)) * d
            n = jnp.maximum(jnp.sum(c, axis=-1, keepdims=True), jnp.exp(-m))
            return c / (n + eps) @ v
        key = jax.random.key(seed)
        ks = jax.random.split(key, 8)
        return {'q': jax.random.normal(ks[0], (B, S, E), jnp.float32), 'k': jax.random.normal(ks[1], (B, S, E), jnp.float32), 'v': jax.random.normal(ks[2], (B, S, E), jnp.float32), 'igate_kernel': jax.random.normal(ks[3], (3 * E, NH), jnp.float32) * 0.02, 'igate_bias': jax.random.normal(ks[4], (NH,), jnp.float32) * 0.1, 'fgate_kernel': jax.random.normal(ks[5], (3 * E, NH), jnp.float32) * 0.02, 'fgate_bias': jnp.linspace(3.0, 6.0, NH, dtype=jnp.float32), 'rms_scale': jax.random.normal(ks[6], (HD,), jnp.float32) * 0.02}
    _L0_xattn_all = _L0_xattn_setup()
    _L0_xattn_in = {k: v for k, v in _L0_xattn_all.items() if k in ('igate_kernel', 'igate_bias', 'fgate_kernel', 'fgate_bias', 'rms_scale')}
    del _L0_xattn_all

    def _L0_ffn_setup():
        import jax, jax.numpy as jnp
        import numpy as np
        B, S, D, E, F = (4, 256, 128, 8, 512)
        MIN_CAPACITY = 4

        def _make_waff():
            g = D // E
            scale = E / D
            w = np.zeros((E, D), np.float32)
            for i in range(E):
                w[i, i * g:(i + 1) * g] = scale
            return jnp.asarray(w)
        key = jax.random.key(seed)
        ks = jax.random.split(key, 6)
        inputs = jax.random.normal(ks[0], (B, S, D), dtype=jnp.float32)
        W1 = jax.random.normal(ks[1], (E, D, F), dtype=jnp.float32) * (1.0 / np.sqrt(D))
        b1 = jnp.zeros((E, F), dtype=jnp.float32)
        W2 = jax.random.normal(ks[2], (E, F, D), dtype=jnp.float32) * (1.0 / np.sqrt(F))
        b2 = jnp.zeros((E, D), dtype=jnp.float32)
        return {'inputs': inputs, 'waff': _make_waff(), 'W1': W1, 'b1': b1, 'W2': W2, 'b2': b2, 'affinity_threshold': jnp.float32(0.5)}
    _L0_ffn_all = _L0_ffn_setup()
    _L0_ffn_in = {k: v for k, v in _L0_ffn_all.items() if k in ('waff', 'W1', 'b1', 'W2', 'b2', 'affinity_threshold')}
    del _L0_ffn_all

    def _L1_attn_setup():
        import jax, jax.numpy as jnp
        import numpy as np
        B, S, D = (4, 512, 128)

        def _scan_causal(x_scan, a):

            def step(h, inp):
                a_t, x_t = inp
                h = a_t * h + x_t
                return (h, h)
            h0 = jnp.zeros(x_scan.shape[::2], dtype=x_scan.dtype)
            xs = (jnp.swapaxes(a, 0, 1), jnp.swapaxes(x_scan, 0, 1))
            _, out = jax.lax.scan(step, h0, xs)
            return jnp.swapaxes(out, 0, 1)
        key = jax.random.key(seed)
        ks = jax.random.split(key, 4)
        scale = 1.0 / np.sqrt(D)
        x = jax.random.normal(ks[0], (B, S, D), dtype=jnp.float32)
        Wg = jax.random.normal(ks[1], (D, D), dtype=jnp.float32) * scale
        Wv = jax.random.normal(ks[2], (D, D), dtype=jnp.float32) * scale
        Wd = jax.random.normal(ks[3], (D, D), dtype=jnp.float32) * scale
        bg = jnp.zeros((D,), dtype=jnp.float32)
        bv = jnp.zeros((D,), dtype=jnp.float32)
        bd = jnp.ones((D,), dtype=jnp.float32)
        return {'x': x, 'Wg': Wg, 'bg': bg, 'Wv': Wv, 'bv': bv, 'Wd': Wd, 'bd': bd}
    _L1_attn_all = _L1_attn_setup()
    _L1_attn_in = {k: v for k, v in _L1_attn_all.items() if k in ('Wg', 'bg', 'Wv', 'bv', 'Wd', 'bd')}
    del _L1_attn_all

    def _L1_xattn_setup():
        import jax, jax.numpy as jnp
        import numpy as np
        B, S, E, H = (2, 256, 128, 16)
        HD = E // H
        key = jax.random.key(seed)
        ks = jax.random.split(key, 7)
        mk = lambda k, shp: jax.random.normal(k, shp, dtype=jnp.float32) * 0.02
        return {'q': jax.random.normal(ks[0], (B, S, E), dtype=jnp.float32), 'k': jax.random.normal(ks[1], (B, S, E), dtype=jnp.float32), 'v': jax.random.normal(ks[2], (B, S, E), dtype=jnp.float32), 'wq': mk(ks[3], (E, E)), 'wk': mk(ks[4], (E, E)), 'wv': mk(ks[5], (E, E)), 'wo': mk(ks[6], (E, E)), 'autoregressive_mask': 1}
    _L1_xattn_all = _L1_xattn_setup()
    _L1_xattn_in = {k: v for k, v in _L1_xattn_all.items() if k in ('wq', 'wk', 'wv', 'wo')}
    del _L1_xattn_all

    def _L1_ffn_setup():
        import jax, jax.numpy as jnp
        import numpy as np
        TOP_K = 2
        key = jax.random.key(seed)
        k1, k2, k3, k4 = jax.random.split(key, 4)
        B, T, D, H, E = (2, 256, 128, 256, 8)
        x = jax.random.normal(k1, (B, T, D), dtype=jnp.float32)
        w12 = jax.random.normal(k2, (E, 2 * H, D), dtype=jnp.float32) * D ** (-0.5)
        w3 = jax.random.normal(k3, (E, D, H), dtype=jnp.float32) * H ** (-0.5)
        gate_w = jax.random.normal(k4, (E, D), dtype=jnp.float32) * D ** (-0.5)
        return {'x': x, 'w12': w12, 'w3': w3, 'gate_w': gate_w}
    _L1_ffn_all = _L1_ffn_setup()
    _L1_ffn_in = {k: v for k, v in _L1_ffn_all.items() if k in ('w12', 'w3', 'gate_w')}
    del _L1_ffn_all
    return {'x': x, 'ctx_1024': ctx_1024, 'L0_attn_Wp': _L0_attn_in['Wp'], 'L0_attn_bp': _L0_attn_in['bp'], 'L0_attn_Wu': _L0_attn_in['Wu'], 'L0_attn_bu': _L0_attn_in['bu'], 'L0_attn_Wo': _L0_attn_in['Wo'], 'L0_attn_bo': _L0_attn_in['bo'], 'L0_xattn_igate_kernel': _L0_xattn_in['igate_kernel'], 'L0_xattn_igate_bias': _L0_xattn_in['igate_bias'], 'L0_xattn_fgate_kernel': _L0_xattn_in['fgate_kernel'], 'L0_xattn_fgate_bias': _L0_xattn_in['fgate_bias'], 'L0_xattn_rms_scale': _L0_xattn_in['rms_scale'], 'L0_ffn_waff': _L0_ffn_in['waff'], 'L0_ffn_W1': _L0_ffn_in['W1'], 'L0_ffn_b1': _L0_ffn_in['b1'], 'L0_ffn_W2': _L0_ffn_in['W2'], 'L0_ffn_b2': _L0_ffn_in['b2'], 'L0_ffn_affinity_threshold': _L0_ffn_in['affinity_threshold'], 'L1_attn_Wg': _L1_attn_in['Wg'], 'L1_attn_bg': _L1_attn_in['bg'], 'L1_attn_Wv': _L1_attn_in['Wv'], 'L1_attn_bv': _L1_attn_in['bv'], 'L1_attn_Wd': _L1_attn_in['Wd'], 'L1_attn_bd': _L1_attn_in['bd'], 'L1_xattn_wq': _L1_xattn_in['wq'], 'L1_xattn_wk': _L1_xattn_in['wk'], 'L1_xattn_wv': _L1_xattn_in['wv'], 'L1_xattn_wo': _L1_xattn_in['wo'], 'L1_ffn_w12': _L1_ffn_in['w12'], 'L1_ffn_w3': _L1_ffn_in['w3'], 'L1_ffn_gate_w': _L1_ffn_in['gate_w']}

def reference(x, ctx_1024, L0_attn_Wp, L0_attn_bp, L0_attn_Wu, L0_attn_bu, L0_attn_Wo, L0_attn_bo, L0_xattn_igate_kernel, L0_xattn_igate_bias, L0_xattn_fgate_kernel, L0_xattn_fgate_bias, L0_xattn_rms_scale, L0_ffn_waff, L0_ffn_W1, L0_ffn_b1, L0_ffn_W2, L0_ffn_b2, L0_ffn_affinity_threshold, L1_attn_Wg, L1_attn_bg, L1_attn_Wv, L1_attn_bv, L1_attn_Wd, L1_attn_bd, L1_xattn_wq, L1_xattn_wk, L1_xattn_wv, L1_xattn_wo, L1_ffn_w12, L1_ffn_w3, L1_ffn_gate_w):
    import jax
    import jax.numpy as jnp

    def _L0_attn_ref(x, Wp, bp, Wu, bu, Wo, bo):
        import jax, jax.numpy as jnp
        import numpy as np
        B, T, D_MODEL, D_SSM = (8, 256, 128, 128)
        Bb, Tt, _ = x.shape
        d_ssm = Wu.shape[1]
        params = x @ Wp + bp
        params = params.reshape(Bb, Tt, 3, d_ssm)
        u = x @ Wu + bu
        w = params[:, :, 0]
        k = params[:, :, 1]

        def step(s, inp):
            w_t, k_t, u_t = inp
            gate = jax.nn.sigmoid(w_t)
            s = gate * (s * jnp.tanh(k_t) + u_t) + (1.0 - gate) * s
            return (s, s)
        s0 = jnp.zeros((Bb, d_ssm), dtype=x.dtype)
        xs = (w.transpose(1, 0, 2), k.transpose(1, 0, 2), u.transpose(1, 0, 2))
        _, ys = jax.lax.scan(step, s0, xs)
        y = ys.transpose(1, 0, 2)
        return y @ Wo + bo

    def _L0_xattn_ref(q, k, v, igate_kernel, igate_bias, fgate_kernel, fgate_bias, rms_scale):
        import jax, jax.numpy as jnp
        import numpy as np
        B, S, E, NH = (2, 256, 128, 4)
        HD = E // NH

        def _mlstm_head(q, k, v, ig, fg, eps=1e-06):
            s, dh = q.shape
            log_f = jax.nn.log_sigmoid(fg)
            cs = jnp.concatenate([jnp.zeros((1, 1), log_f.dtype), jnp.cumsum(log_f, axis=0)], axis=0)
            neg = jnp.asarray(-0.7 * jnp.finfo(cs.dtype).max, cs.dtype)
            log_d = jnp.where(jnp.tri(s, dtype=bool), (cs - cs.T)[1:, 1:] + ig.T, neg)
            m = jnp.max(log_d, axis=-1, keepdims=True)
            d = jnp.exp(log_d - m)
            c = q @ (k.T / jnp.sqrt(dh)) * d
            n = jnp.maximum(jnp.sum(c, axis=-1, keepdims=True), jnp.exp(-m))
            return c / (n + eps) @ v
        b, s, e = q.shape
        nh = igate_kernel.shape[1]
        hd = e // nh
        gate_in = jnp.concatenate((q, k, v), axis=-1)
        ig = (gate_in @ igate_kernel + igate_bias).swapaxes(-1, -2)[..., None]
        fg = (gate_in @ fgate_kernel + fgate_bias).swapaxes(-1, -2)[..., None]
        qh = q.reshape(b, s, nh, hd).swapaxes(1, 2)
        kh = k.reshape(b, s, nh, hd).swapaxes(1, 2)
        vh = v.reshape(b, s, nh, hd).swapaxes(1, 2)
        h = jax.vmap(jax.vmap(_mlstm_head))(qh, kh, vh, ig, fg)
        var = jnp.mean(jnp.square(h.astype(jnp.float32)), axis=-1, keepdims=True)
        h = (h * jax.lax.rsqrt(var + 1e-06)).astype(h.dtype) * (1.0 + rms_scale)
        return h.swapaxes(1, 2).reshape(b, s, e)

    def _L0_ffn_ref(inputs, waff, W1, b1, W2, b2, affinity_threshold):
        import jax, jax.numpy as jnp
        import numpy as np
        B, S, D, E, F = (4, 256, 128, 8, 512)
        MIN_CAPACITY = 4

        def _make_waff():
            g = D // E
            scale = E / D
            w = np.zeros((E, D), np.float32)
            for i in range(E):
                w[i, i * g:(i + 1) * g] = scale
            return jnp.asarray(w)
        num = jnp.einsum('bsd,ed->bse', inputs, waff)
        x_norm = jnp.linalg.norm(inputs, axis=-1, keepdims=True)
        w_norm = jnp.linalg.norm(waff, axis=-1)
        aff = num / (x_norm * w_norm[None, None, :] + 1e-09)
        router_probs = jax.nn.softmax(aff, axis=-1)
        cap = jnp.floor(S * jax.nn.sigmoid(aff.mean() - affinity_threshold)).astype(jnp.int32)
        cap = jnp.minimum(jnp.maximum(cap, MIN_CAPACITY), S)
        tcr = jax.nn.one_hot(jnp.argmax(router_probs, axis=-1), E, dtype=inputs.dtype)
        order = jnp.argsort(-aff, axis=1)
        ranks = jnp.argsort(order, axis=1)
        ecr = (ranks < cap).astype(inputs.dtype)
        dispatch = tcr * ecr
        masks = jnp.moveaxis(dispatch, -1, 0)

        def body(acc, expert):
            W1e, b1e, W2e, b2e, me = expert
            xi = inputs * me[..., None]
            h = jax.nn.gelu(xi @ W1e + b1e, approximate=False)
            return (acc + (h @ W2e + b2e), None)
        out, _ = jax.lax.scan(body, jnp.zeros_like(inputs), (W1, b1, W2, b2, masks))
        return out

    def _L1_attn_ref(x, Wg, bg, Wv, bv, Wd, bd):
        import jax, jax.numpy as jnp
        import numpy as np
        B, S, D = (4, 512, 128)

        def _scan_causal(x_scan, a):

            def step(h, inp):
                a_t, x_t = inp
                h = a_t * h + x_t
                return (h, h)
            h0 = jnp.zeros(x_scan.shape[::2], dtype=x_scan.dtype)
            xs = (jnp.swapaxes(a, 0, 1), jnp.swapaxes(x_scan, 0, 1))
            _, out = jax.lax.scan(step, h0, xs)
            return jnp.swapaxes(out, 0, 1)
        g = jnp.einsum('bsd,ed->bse', x, Wg) + bg
        v = jnp.einsum('bsd,ed->bse', x, Wv) + bv
        d = jnp.einsum('bsd,ed->bse', x, Wd) + bd
        x_scan = jax.nn.sigmoid(g) * jnp.tanh(v)
        a = 0.001 + 0.998 * jax.nn.sigmoid(d)
        return _scan_causal(x_scan, a)

    def _L1_xattn_ref(q, k, v, wq, wk, wv, wo, autoregressive_mask):
        import jax, jax.numpy as jnp
        import numpy as np
        B, S, E, H = (2, 256, 128, 16)
        HD = E // H
        scale = 1.0 / np.sqrt(HD).astype(np.float32)
        qp = (q @ wq.T).reshape(-1, H, S, HD)
        kp = (k @ wk.T).reshape(-1, H, S, HD)
        vp = (v @ wv.T).reshape(-1, H, S, HD)
        scores = jnp.einsum('bhqd,bhkd->bhqk', qp, kp) * scale
        if autoregressive_mask:
            causal = jnp.tril(jnp.ones((S, S), dtype=bool))
            scores = jnp.where(causal, scores, jnp.float32(-1000000000.0))
        attn = jax.nn.softmax(scores, axis=-1)
        out = jnp.einsum('bhqk,bhkd->bhqd', attn, vp).reshape(-1, S, E)
        return out @ wo.T

    def _L1_ffn_ref(x, w12, w3, gate_w):
        import jax, jax.numpy as jnp
        import numpy as np
        TOP_K = 2
        E = gate_w.shape[0]
        H = w3.shape[-1]
        scores = jnp.einsum('btd,ed->bte', x, gate_w)
        topk_scores, topk_idx = jax.lax.top_k(scores, TOP_K)
        topk_probs = jax.nn.softmax(topk_scores, axis=-1)
        total_probs = jnp.sum(jax.nn.one_hot(topk_idx, E, dtype=topk_probs.dtype) * topk_probs[..., None], axis=-2)
        h12 = jnp.einsum('btd,ehd->bteh', x, w12)
        h1, h2 = (h12[..., :H], h12[..., H:])
        hidden = jax.nn.silu(h1) * h2
        expert_out = jnp.einsum('bteh,edh->bted', hidden, w3)
        y = jnp.sum(total_probs[..., None] * expert_out, axis=-2)
        return y
    x = x + _L0_attn_ref(_layernorm(x, axis=-1), L0_attn_Wp, L0_attn_bp, L0_attn_Wu, L0_attn_bu, L0_attn_Wo, L0_attn_bo)
    x = x + _L0_xattn_ref(_layernorm(x, axis=-1), ctx_1024, ctx_1024, L0_xattn_igate_kernel, L0_xattn_igate_bias, L0_xattn_fgate_kernel, L0_xattn_fgate_bias, L0_xattn_rms_scale)
    x = x + _L0_ffn_ref(_layernorm(x, axis=-1), L0_ffn_waff, L0_ffn_W1, L0_ffn_b1, L0_ffn_W2, L0_ffn_b2, L0_ffn_affinity_threshold)
    x = x + _L1_attn_ref(_layernorm(x, axis=-1), L1_attn_Wg, L1_attn_bg, L1_attn_Wv, L1_attn_bv, L1_attn_Wd, L1_attn_bd)
    x = x + _L1_xattn_ref(_layernorm(x, axis=-1), ctx_1024, ctx_1024, L1_xattn_wq, L1_xattn_wk, L1_xattn_wv, L1_xattn_wo, 1)
    x = x + _L1_ffn_ref(_layernorm(x, axis=-1), L1_ffn_w12, L1_ffn_w3, L1_ffn_gate_w)
    return x

_drawn_inputs = setup_inputs


def setup_inputs(seed=0):
    import zlib

    import numpy as np

    out = dict(_drawn_inputs(seed))
    spreads = {'L0_ffn_b1': (0.0, 0.1),
     'L0_ffn_b2': (0.0, 0.1),
     'L1_attn_bg': (0.0, 0.344),
     'L1_attn_bv': (0.0, 0.1),
     'L1_attn_bd': (1.0, 0.2)}
    factors = {'L0_xattn_igate_bias': 64.0,
     'L1_xattn_wq': 8.0,
     'L1_xattn_wk': 8.0,
     'L1_xattn_wv': 3.846,
     'L1_xattn_wo': 4.465}
    for name, (base, spread) in spreads.items():
        noise = np.random.default_rng([zlib.crc32(name.encode()), seed]).standard_normal(out[name].shape)
        drawn = base * np.exp(spread * noise) if base else spread * noise
        out[name] = jnp.asarray(drawn.astype(out[name].dtype))
    for name, factor in factors.items():
        out[name] = (out[name] * factor).astype(out[name].dtype)
    return out
```

```python
from contextlib import ExitStack

import numpy as np
import concourse.bass as bass
from concourse import mybir


F32 = mybir.dt.float32
BF16 = mybir.dt.bfloat16
ALU = mybir.AluOpType
ACT = mybir.ActivationFunctionType
AX = mybir.AxisListType

B, S, D = 8, 256, 128
P = 128
T = B * S // P
C = 4
CT = T // C
CW = CT * P
BC = CW // S
NH = 4
HD = D // NH
R = B * NH
E = 8
FK = 4
GH = 2
NA = 16
AD = 8
NP = B * NA
CUT = 2 * P + P
SL = 64
OW = 32
OG = P // OW
NEG = -1.0e30
LN_EPS = 1e-5

COLS = {}


def _pack_columns():
    at = 0
    for name, width in (("bw", 1), ("bk", 1), ("bu", 1), ("bg", 1), ("bv", 1), ("bd", 1), ("b1", E * FK),
                        ("gq", 8), ("gk", 8), ("gv", 8), ("gbias", 1), ("thr", 1), ("rms", HD), ("bo", D),
                        ("waffT", E), ("gateT", E), ("b2", D), ("prio", E)):
        COLS[name] = (at, width)
        at += width
    return at


NCOLS = _pack_columns()

CONST = {"ident": (0, P), "neg_ji": (P, P), "neg_ij": (2 * P, P), "before": (3 * P, 2 * S), "after": (3 * P + 2 * S, 2 * S)}
NCONST = 3 * P + 4 * S


def build(nc, x, ctx_in, ctxT_in, small_in, const_in, wp_in, wu_in, wo_in, w1_in, w2_in, lw_in, aw_in, w12_in, w3_in, out):
    es = ExitStack()
    with es:
        def sb(name, shape, dt=F32):
            return es.enter_context(nc.sbuf_tensor(name, shape, dt))

        def sem(name):
            return es.enter_context(nc.semaphore(name))

        X = sb("X", [P, T, D])
        XN = sb("XN", [P, T, D])
        XNT = [sb(f"XNT{i}", [P, T * P]) for i in range(2)]
        small = sb("small", [P, NCOLS])
        const = sb("const", [P, NCONST])
        ctxT = sb("ctxT", [P, T * P])
        ones = sb("ones", [P, P])
        zeros_b = sb("zeros_b", [P, SL], BF16)
        ident_b = sb("ident_b", [P, P], BF16)
        neg_ji_b = sb("neg_ji_b", [P, P], BF16)
        neg_ij_b = sb("neg_ij_b", [P, P], BF16)
        wp = sb("wp", [P, 3 * D])
        wu = sb("wu", [P, D])
        wo = sb("wo", [P, D])
        lw = sb("lw", [P, 3 * D])
        aw = sb("aw", [P, 4 * D])
        stats = sb("stats", [P, T, 6])
        mv = sb("mv", [P, T, 2])
        vareps = sb("vareps", [P, T])
        rstd = sb("rstd", [P, T])
        power = sb("power", [P, 2])

        scan_room = sb("scan_room", [P, 5, 2 * CW])
        gate, tnh, decay, drive, state = (scan_room[:, i, :].rearrange("p (n c) -> p n c", n=2) for i in range(5))

        zpad = sb("zpad", [P, 2, 68 * B])
        gkv = sb("gkv", [P, 8])
        sel_room = sb("sel_room", [P, R * P])
        sel = sel_room[0:R, :].rearrange("p (r m) -> p r m", m=P)
        g_i = sb("g_i", [R, S])
        g_f = sb("g_f", [R, S])
        g_n = sb("g_n", [R, S])
        g_l = sb("g_l", [R, S])
        g_e = sb("g_e", [R, S])
        g_cs = sb("g_cs", [R, S])
        g_b = sb("g_b", [R, S])
        g_g = sb("g_g", [R, S])
        g_m = sb("g_m", [R, S])
        bT = sb("bT", [P, 2, 2, R])
        v_room = sb("v_room", [P, 2 * NP * (AD + 1) + OW])
        vaug = v_room[:, 0:T * NH * (HD + 1)].rearrange("p (t h d) -> p t h d", t=T, h=NH)
        score_room = sb("score_room", [P, 2 * OG * CUT])
        dec = score_room[:, 0:3 * CUT].rearrange("p (n c) -> p n c", n=3)
        cT = score_room[:, 3 * CUT:6 * CUT].rearrange("p (n c) -> p n c", n=3)
        hn = sb("hn", [P, 2 * NH])
        hr = sb("hr", [P, 2 * NH])
        hh = sb("hh", [P, 2 * NH, HD])
        hq = sb("hq", [P, 2 * NH, HD])
        hv = sb("hv", [P, 2 * NH])
        hv2 = sb("hv2", [P, 2 * NH])
        rms1 = sb("rms1", [P, HD])

        w_room = sb("w_room", [P, 2 * E * FK * P])
        w1 = w_room[:, 0:E * FK * P].rearrange("p (e f) -> p e f", e=E)
        w2 = w_room[:, E * FK * P:].rearrange("p (e k d) -> p e k d", e=E, k=FK)
        h_room = sb("h_room", [P, 2 * FK * CW])
        hT = h_room[:].rearrange("p (n k c) -> p n k c", n=2, k=FK)
        gb1 = sb("gb1", [P, E * FK])
        gz = sb("gz", [P, E, FK, E])
        G0 = sb("G0", [E, D])
        wsq = sb("wsq", [P, E])
        wsum = sb("wsum", [P, E])
        wn = sb("wn", [P, E])
        xsq = sb("xsq", [P, T])
        xnm = sb("xnm", [P, T])
        sqj = sb("sqj", [P, D])
        den = sb("den", [P, T, E])
        rden = sb("rden", [P, T, E])
        aff = sb("aff", [P, T, E])
        amax = sb("amax", [P, T])
        eq = sb("eq", [P, T, E])
        pri = sb("pri", [P, T, E])
        pm = sb("pm", [P, T])
        oh = sb("oh", [P, T, E])
        ohT = h_room[0:E, 0:T * P]
        affT = h_room[0:E, T * P:2 * T * P]
        ndT = sel_room[0:E, 0:T * P]
        asum = sb("asum", [P, 1])
        zc = sb("zc", [P, 1])
        sg = sb("sg", [P, 1])
        cap = sb("cap", [P, 1])
        cnt = sb("cnt", [P, 2, T])
        cj = sb("cj", [P, 2, S])
        rank1 = sb("rank1", [P, T])
        keep = sb("keep", [P, T])
        disp = sb("disp", [P, T, E])
        ndisp = sb("ndisp", [P, T, E])

        kv_tm = sb("kv_tm", [P, 2, 2, 2 * D])
        Qs = sb("Qs", [P, 2, 2 * NA, AD])
        q1 = sb("q1", [P, 2 * NA, AD])
        q2 = sb("q2", [P, 2 * NA, AD])
        mx3 = sb("mx3", [P, 2, NA, 3])
        mx = sb("mx", [P, 2, NA])
        mr = sb("mr", [P, 2, NA])
        mr2 = sb("mr2", [P, 2, NA])
        pT = score_room[:].rearrange("p (n c) -> p n c", n=2 * OG)
        orec = sb("orec", [P, 2, OG])
        Os = sb("Os", [P, 2, 2 * NA, AD])
        Otm = sb("Otm", [P, 2, 2, D])
        OT = sb("OT", [P, 2, 2 * P])
        w12 = scan_room[:, 0:4, :].rearrange("p a (n c) -> p (a n) c", n=2)
        w3 = ctxT[:].rearrange("p (e k d) -> p e k d", e=E, k=GH)
        f_m2 = sb("f_m2", [P, T])
        f_z = sb("f_z", [P, T])
        f_e = sb("f_e", [P, T])
        f_p = sb("f_p", [P, T])
        Ks = sb("Ks", [P, 2, 2 * NA, AD])
        r1 = sb("r1", [P, 2 * NA, AD])
        r2 = sb("r2", [P, 2 * NA, AD])
        KK = h_room[:, 0:2048].bitcast(BF16).rearrange("p (n i a s) -> p n i a s", n=2, i=2, s=SL)
        QQ = h_room[:, 2048:4096].bitcast(BF16).rearrange("p (n i a s) -> p n i a s", n=2, i=2, s=SL)
        KT = w_room[:].bitcast(BF16).rearrange("p (q s) -> p q s", s=S)
        QT = sel_room[:].bitcast(BF16).rearrange("p (v n q s) -> p v n q s", v=2, n=2, s=S)
        Va = v_room[:, 0:2 * NP * (AD + 1)].rearrange("p (n d) -> p n d", d=AD + 1)
        OV = sb("OV", [P, 2, S])

        ps = [es.enter_context(nc.psum_tensor(f"bank{i}", [P, 512], F32)) for i in range(8)]
        ps_b = [bank[:].bitcast(BF16) for bank in ps]

        kv_d = nc.dram_tensor("kv_rows", (2, B, 2, P, D), F32, kind="Internal").ap()
        q_d = nc.dram_tensor("q_rows", (T, P, D), F32, kind="Internal").ap()
        o_d = nc.dram_tensor("o_rows", (T, P, D), F32, kind="Internal").ap()

        def problems(rows):
            return rows.rearrange("i p (g d) -> (i p g) d", d=AD).rearrange("(n p) d -> p n d", p=P)

        def col(name):
            a, w = COLS[name]
            return small[:, a:a + w]

        def cst(name):
            a, w = CONST[name]
            return const[:, a:a + w]

        ident = cst("ident")

        s_x = sem("s_x")
        s_small = sem("s_small")
        s_const = sem("s_const")
        s_wa = sem("s_wa")
        s_ctxT = sem("s_ctxT")
        s_ctx = sem("s_ctx")
        s_lw = sem("s_lw")
        s_aw = sem("s_aw")
        s_w1 = sem("s_w1")
        s_w2 = sem("s_w2")
        s_out = sem("s_out")
        dve_seq = sem("dve_seq")
        pool_seq = sem("pool_seq")
        act_seq = sem("act_seq")
        var_ready = sem("var_ready")
        rstd_ready = sem("rstd_ready")
        pow_asked = sem("pow_asked")
        pow_done = sem("pow_done")
        xn_ready = sem("xn_ready")
        xnt_turned = sem("xnt_turned")
        xnt_ready = sem("xnt_ready")
        a_proj = sem("a_proj")
        a_gate = sem("a_gate")
        a_drive = sem("a_drive")
        a_scan = sem("a_scan")
        a_out = sem("a_out")
        a_add = sem("a_add")
        a_bias = sem("a_bias")
        pool_const = sem("pool_const")
        b_gates = sem("b_gates")
        b_pad = sem("b_pad")
        b_exp = sem("b_exp")
        b_dve = sem("b_dve")
        b_turn = sem("b_turn")
        b_turned = sem("b_turned")
        b_sc = sem("b_sc")
        b_dec = sem("b_dec")
        b_ct = sem("b_ct")
        b_pv = sem("b_pv")
        b_num = sem("b_num")
        c_sq = sem("c_sq")
        c_gb = sem("c_gb")
        c_num = sem("c_num")
        c_wn = sem("c_wn")
        c_wsq = sem("c_wsq")
        c_sum = sem("c_sum")
        c_mean = sem("c_mean")
        c_z = sem("c_z")
        c_sig = sem("c_sig")
        c_oh = sem("c_oh")
        c_turn = sem("c_turn")
        c_turned = sem("c_turned")
        c_row = sem("c_row")
        c_cnt = sem("c_cnt")
        c_nd = sem("c_nd")
        c_g0 = sem("c_g0")
        c_g0c = sem("c_g0c")
        c_base = sem("c_base")
        c_badd = sem("c_badd")
        c_h = sem("c_h")
        c_act = sem("c_act")
        c_y = sem("c_y")
        c_acc = sem("c_acc")
        d_proj = sem("d_proj")
        d_act = sem("d_act")
        d_scan = sem("d_scan")
        d_turn = sem("d_turn")
        d_add = sem("d_add")

        e_fill = sem("e_fill")
        e_kv = sem("e_kv")
        e_kvc = sem("e_kvc")
        e_kvd = [sem(f"e_kvd{i}") for i in range(2)]
        e_ks = [sem(f"e_ks{i}") for i in range(2)]
        e_va = sem("e_va")
        e_kpart = sem("e_kpart")
        e_qpart = sem("e_qpart")
        e_kk = sem("e_kk")
        e_kt = sem("e_kt")
        e_ktc = sem("e_ktc")
        e_q = sem("e_q")
        e_qc = sem("e_qc")
        e_qd = [sem(f"e_qd{i}") for i in range(C)]
        e_qs = [sem(f"e_qs{i}") for i in range(2)]
        e_qq = sem("e_qq")
        e_mq = sem("e_mq")
        e_turn = sem("e_turn")
        e_turned = sem("e_turned")
        e_i = sem("e_i")
        e_max = sem("e_max")
        e_j = sem("e_j")
        e_p = sem("e_p")
        e_pv = sem("e_pv")
        e_ov = sem("e_ov")
        e_rec = sem("e_rec")
        e_read = sem("e_read")
        e_o = sem("e_o")
        e_od = [sem(f"e_od{i}") for i in range(2)]
        e_ot = [sem(f"e_ot{i}") for i in range(2)]
        e_y = sem("e_y")
        e_add = sem("e_add")
        s_w12 = sem("s_w12")
        s_w3 = sem("s_w3")
        f_sc = sem("f_sc")
        f_d = sem("f_d")
        f_ex = sem("f_ex")
        f_h = sem("f_h")
        f_silu = sem("f_silu")
        f_mul = sem("f_mul")
        f_y = sem("f_y")
        f_acc = sem("f_acc")

        LAG_J = NA + 4
        FIRST = -NA - 4
        LAST = NP + 2 * NA + 20

        def batch_at(step, offset):
            b, left = divmod(step - offset, NA)
            return b if left == 0 and 0 <= b < B else None

        def group_at(step, offset):
            g, left = divmod(step - offset, OG)
            return g if left == 0 and 0 <= g < NP // OG else None

        AT_LOAD, AT_SPLIT, AT_TURN, AT_MAX, AT_TURN2 = -NA - 4, -10, -6, NA, NA + 2
        AT_PV = LAG_J + OG
        AT_GROUP = AT_PV + 2
        AT_STORE, AT_OUT, AT_Y = LAG_J + NA + 3, LAG_J + NA + 11, LAG_J + NA + 13

        def split_parts(eng, part_done, count, src, left1, left2, hi, mid, lo):
            for ins in (lambda: eng.tensor_copy(hi, src),
                        lambda: eng.tensor_tensor(left1, src, hi, ALU.subtract),
                        lambda: eng.tensor_copy(mid, left1),
                        lambda: eng.tensor_tensor(left2, left1, mid, ALU.subtract),
                        lambda: eng.tensor_copy(lo, left2)):
                ins().then_inc(part_done, 1)
                count += 1
                eng.wait_ge(part_done, count)
            return count

        fills = []
        for step in range(FIRST, LAST):
            for kind, which, n in (("q", batch_at(step, AT_TURN), 2), ("q2", batch_at(step, AT_TURN2), 2),
                                   ("group", group_at(step, AT_GROUP), 1), ("out", batch_at(step, AT_OUT), 1),
                                   ("y", batch_at(step, AT_Y), 1)):
                if which is not None:
                    fills += [(kind, which, k) for k in range(n)]
        fill_of = {f: n for n, f in enumerate(fills)}
        by_dve = ("group", "y")

        def read_count(f):
            mine = fills[f][0] in by_dve
            return sum((kind in by_dve) == mine for kind, _, _ in fills[:f + 1])

        def wait_read(eng, f):
            eng.wait_ge(e_read if fills[f][0] in by_dve else e_turned, read_count(f))

        block = es.enter_context(nc.Block())

        @block.sync
        def _(sp):
            sp.dma_start(X[:], x.rearrange("(t p) d -> p t d", p=P)).then_inc(s_x, 16)
            sp.dma_start(const[:], const_in).then_inc(s_const, 16)
            sp.dma_start(wp[:], wp_in).then_inc(s_wa, 16)
            sp.dma_start(wu[:], wu_in).then_inc(s_wa, 16)
            sp.dma_start(wo[:], wo_in).then_inc(s_wa, 16)
            sp.dma_start(ctxT[:], ctxT_in).then_inc(s_ctxT, 16)
            for h in range(NH):
                sp.dma_start(vaug[:, :, h, 0:HD],
                             ctx_in.rearrange("(t p) (h d) -> p t h d", p=P, h=NH)[:, :, h, :]).then_inc(s_ctx, 16)
            sp.dma_start(w1, w1_in).then_inc(s_w1, 16)
            sp.dma_start(w2, w2_in).then_inc(s_w2, 16)
            sp.dma_start(lw[:], lw_in).then_inc(s_lw, 16)
            sp.dma_start(aw[:], aw_in).then_inc(s_aw, 16)
            for b in range(B):
                k = b % 2
                sp.wait_ge(e_kvc, b + 1)
                for n in range(2):
                    sp.dma_start(kv_d[n, b].rearrange("i p d -> p i d"), kv_tm[:, k, :, n * D:(n + 1) * D]).then_inc(e_kvd[k], 16)

            def load_keys(b):
                if b >= 2:
                    sp.wait_ge(e_kk, b - 1)
                sp.dma_start(Ks[:, b % 2], problems(kv_d[0, b])).then_inc(e_ks[b % 2], 16)

            for k in range(2):
                sp.wait_ge(e_kvd[k], 32 * B // 2)
            for b in range(2):
                load_keys(b)
            for b in range(B):
                sp.dma_start(Va[:, b * 2 * NA:(b + 1) * 2 * NA, 0:AD], problems(kv_d[1, b])).then_inc(e_va, 16)
            sp.wait_ge(d_add, C)
            sp.dma_start(w12, w12_in).then_inc(s_w12, 16)
            sp.dma_start(w3, w3_in).then_inc(s_w3, 16)
            for c in range(C):
                sp.wait_ge(e_qc, c + 1)
                sp.dma_start(q_d[c * CT:(c + 1) * CT].rearrange("t p d -> p t d"), XN[:, c * CT:(c + 1) * CT, :]).then_inc(e_qd[c], 16)
            for b in range(2, B):
                load_keys(b)
            for step in range(FIRST, LAST):
                b = batch_at(step, AT_LOAD)
                if b is not None:
                    sp.wait_ge(e_qd[b // BC], 16)
                    if b >= 2:
                        sp.wait_ge(e_qq, b - 1)
                    sp.dma_start(Qs[:, b % 2], problems(q_d[2 * b:2 * b + 2])).then_inc(e_qs[b % 2], 16)
            sp.wait_ge(f_acc, E * C)
            sp.dma_start(out.rearrange("(t p) d -> p t d", p=P), X[:]).then_inc(s_out, 16)
            sp.wait_ge(s_out, 16)

        @block.gpsimd
        def _(pool):
            pool.memset(ones[:], 1.0)
            pool.memset(power[:, 0:1], -0.5)
            pool.memset(power[:, 1:2], 0.5).then_inc(pool_seq, 1)
            pool.memset(zpad[:], 0.0)
            pool.memset(gz[:], 0.0)
            pool.memset(vaug[:, :, :, HD:HD + 1], 1.0).then_inc(pool_const, 1)
            ln_count = [0]

            def rstd_of(c):
                ln_count[0] += 1
                pool.wait_ge(var_ready, ln_count[0])
                t0, t1 = c * CT, (c + 1) * CT
                pool.tensor_tensor(rstd[:, t0:t1], vareps[:, t0:t1], power[:, 0:1].to_broadcast([P, CT]), ALU.pow).then_inc(rstd_ready, 1)

            pool.wait_ge(pool_seq, 1)
            pool.wait_ge(s_small, 16)
            rstd_of(0)
            for c in range(C):
                if c + 1 < C:
                    rstd_of(c + 1)
                pool.wait_ge(xn_ready, c + 1)
                if c == 0:
                    pool.wait_ge(s_x, 16)
                ch = X[:, c * CT:(c + 1) * CT, :]
                pool.tensor_tensor(ch, ch, col("bo").unsqueeze(1).to_broadcast([P, CT, D]), ALU.add).then_inc(a_bias, 1)
            pool.wait_ge(s_const, 16)
            pool.wait_ge(s_small, 16)
            pool.tensor_scalar(sel, ident[0:R, 0:R].unsqueeze(2).to_broadcast([R, R, P]), -1.0, None, ALU.mult)
            pool.tensor_tensor(gkv[:], col("gk"), col("gv"), ALU.add).then_inc(pool_seq, 1)
            pool.wait_ge(pool_seq, 2)
            for n, g in enumerate((col("gq"), gkv[:])):
                z = zpad[:, n, :].rearrange("p (b s) -> p b s", s=68)
                for k in range(2):
                    last = pool.tensor_copy(z[:, :, 32 * k:32 * k + 4],
                                            g[:, 4 * k:4 * k + 4].unsqueeze(1).to_broadcast([P, B, 4]))
            last.then_inc(b_pad, 1)
            for c in range(C):
                rstd_of(c)
            for b in range(B):
                pool.wait_ge(pow_asked, b + 1)
                pool.tensor_tensor(hv[:], hv2[:], power[:, 0:1].to_broadcast([P, 2 * NH]), ALU.pow).then_inc(pow_done, 1)
            for c in range(C):
                rstd_of(c)
            pool.wait_ge(c_wn, 1)
            pool.wait_ge(pow_asked, B + 1)
            pool.tensor_tensor(wn[:], wsum[:], power[:, 1:2].to_broadcast([P, E]), ALU.pow)
            pool.wait_ge(c_sq, T)
            pool.tensor_tensor(xnm[:], xsq[:], power[:, 1:2].to_broadcast([P, T]), ALU.pow).then_inc(pow_done, 1)
            for c in range(C):
                rstd_of(c)
            pool.wait_ge(c_y, E * C)
            for n in range(2):
                pool.memset(KK[:, n, :, :, 6 * AD:SL], 0.0)
                pool.memset(QQ[:, n, :, :, 6 * AD:SL], 0.0)
            pool.memset(v_room[:, 2 * NP * (AD + 1):], 0.0)
            pool.memset(Va[:, :, AD:AD + 1], 1.0).then_inc(e_fill, 1)
            pool.wait_ge(e_fill, 1)
            for n in range(2):
                last = pool.memset(KK[:, n, :, :, 6 * AD:6 * AD + 3], 1.0)
            last.then_inc(e_fill, 1)
            for c in range(C):
                rstd_of(c)
            parts = 0
            for b in range(B):
                pool.wait_ge(e_ks[b % 2], 16 * (b // 2 + 1))
                if b >= 2:
                    pool.wait_ge(e_kt, 2 * (b - 1))
                src = Ks[:, b % 2].rearrange("p (a i) d -> p i a d", i=2)
                va, vb = (v[:].rearrange("p (a i) d -> p i a d", i=2) for v in (r1, r2))
                slot = [KK[:, b % 2, :, :, AD * j:AD * (j + 1)] for j in range(6)]
                parts = split_parts(pool, e_kpart, parts, src, va, vb, slot[0], slot[2], slot[4])
                pool.tensor_copy(slot[1], slot[0])
                pool.tensor_copy(slot[3], slot[0])
                pool.tensor_copy(slot[5], slot[2]).then_inc(e_kk, 1)
            for step in range(FIRST, LAST):
                b = batch_at(step, AT_STORE)
                if b is not None:
                    pool.wait_ge(e_o, NA // OG * (b + 1))
                    pool.dma_start(problems(o_d[2 * b:2 * b + 2]), Os[:, b % 2]).then_inc(e_od[b % 2], 16)
                    pool.wait_ge(e_od[b % 2], 16 * (b // 2 + 1))
                    if b >= 2:
                        pool.wait_ge(e_turn, fill_of["out", b - 2, 0] + 1)
                    pool.dma_start(Otm[:, b % 2], o_d[2 * b:2 * b + 2].rearrange("i p d -> p i d")).then_inc(e_ot[b % 2], 16)
            for c in range(C):
                rstd_of(c)

        @block.scalar
        def _(act):
            act.dma_start(small[:], small_in).then_inc(s_small, 16)
            ln_count = [0]

            def copy_xnt(layer):
                def one(c):
                    n = ln_count[0]
                    act.wait_ge(xnt_turned, n + 1)
                    act.activation(XNT[layer % 2][:, c * CW:(c + 1) * CW], ps[n % 2][:], ACT.Copy).then_inc(xnt_ready, 1)
                    ln_count[0] += 1
                return one

            cp = copy_xnt(0)
            act.wait_ge(s_small, 16)
            for c in range(C):
                cp(c)
                act.wait_ge(a_proj, c + 1)
                if c >= 2:
                    act.wait_ge(a_drive, c - 1)
                act.activation(gate[:, c % 2, :], ps[2][:], ACT.Sigmoid, bias=col("bw"))
                act.activation(tnh[:, c % 2, :], ps[3][:], ACT.Tanh, bias=col("bk")).then_inc(a_gate, 1)

            cp = copy_xnt(1)
            for c in range(C):
                cp(c)
            act.wait_ge(b_dve, 1)
            act.activation(g_e[:], g_n[:], ACT.Exp).then_inc(act_seq, 1)
            act.wait_ge(act_seq, 1)
            act.activation(g_n[:], g_e[:], ACT.Ln, bias=1.0).then_inc(b_exp, 1)
            act.wait_ge(b_dve, 2)
            act.activation(g_e[:], g_m[:], ACT.Exp, scale=-1.0).then_inc(b_exp, 1)
            act.wait_ge(b_turn, 1)
            act.activation(bT[:], ps[2][:, 0:4 * R], ACT.Copy).then_inc(b_turned, 1)
            act.wait_ge(b_turned, 1)
            for r in range(R):
                b, h = divmod(r, NH)
                act.wait_ge(b_sc, r + 1)
                if r >= 3:
                    act.wait_ge(b_ct, r - 2)
                act.activation(dec[:, r % 3, 0:S], ps[2 + r % 2][:, 0:S], ACT.Exp, bias=bT[:, 0, 0, r:r + 1])
                act.activation(dec[:, r % 3, S:CUT], ps[2 + r % 2][:, S:CUT], ACT.Exp,
                               bias=bT[:, 0, 1, r:r + 1]).then_inc(b_dec, 1)

            act.wait_ge(pool_const, 1)
            for e in range(E):
                last = act.activation(gz[:, e, :, e], small[:, COLS["b1"][0] + FK * e:COLS["b1"][0] + FK * e + FK], ACT.Gelu)
            last.then_inc(c_gb, 1)
            cp = copy_xnt(2)
            for c in range(C):
                cp(c)
                for t in range(c * CT, (c + 1) * CT):
                    act.activation(sqj[:], XN[:, t, :], ACT.Square, accum_out=xsq[:, t:t + 1]).then_inc(c_sq, 1)
                    act.wait_ge(c_sq, t + 1)
            for c in range(C):
                act.wait_ge(c_turn, c + 1)
                act.activation(affT[:, c * CW:(c + 1) * CW], ps[2 + 2 * (c % 2)][0:E, :], ACT.Copy)
                act.activation(ohT[:, c * CW:(c + 1) * CW], ps[3 + 2 * (c % 2)][0:E, :], ACT.Copy).then_inc(c_turned, 1)
            act.wait_ge(c_z, 1)
            act.activation(sg[:], zc[:], ACT.Sigmoid).then_inc(c_sig, 1)
            for c in range(C):
                act.wait_ge(c_turn, C + c + 1)
                act.activation(ndT[:, c * CW:(c + 1) * CW], ps[2 + c % 2][0:E, :], ACT.Copy).then_inc(c_turned, 1)
            for n in range(E * C):
                e, c = divmod(n, C)
                if n >= 2:
                    act.wait_ge(c_y, n - 1)
                for k in range(FK):
                    act.wait_ge(c_h, FK * n + k + 1)
                    b1 = COLS["b1"][0] + FK * e + k
                    act.activation(hT[:, n % 2, k, :], ps[2 + k][:], ACT.Gelu, bias=small[:, b1:b1 + 1]).then_inc(c_act, 1)

            cp = copy_xnt(3)
            for c in range(C):
                cp(c)
                act.wait_ge(d_proj, c + 1)
                if c >= 2:
                    act.wait_ge(d_scan, c - 1)
                act.activation(gate[:, c % 2, :], ps[2][:], ACT.Sigmoid, bias=col("bg"))
                act.activation(tnh[:, c % 2, :], ps[3][:], ACT.Tanh, bias=col("bv"))
                act.activation(state[:, c % 2, :], ps[4][:], ACT.Sigmoid, bias=col("bd")).then_inc(d_act, 1)

            for b in range(B):
                act.wait_ge(e_kv, b + 1)
                if b >= 2:
                    act.wait_ge(e_kvd[b % 2], 32 * (b // 2))
                act.activation(kv_tm[:, b % 2].rearrange("p i d -> p (i d)"), ps[6 + b % 2][:], ACT.Copy).then_inc(e_kvc, 1)
            cp = copy_xnt(4)
            for c in range(C):
                cp(c)
                act.wait_ge(e_q, c + 1)
                act.activation(XN[:, c * CT:(c + 1) * CT, :].rearrange("p t d -> p (t d)"), ps[2 + c % 2][:], ACT.Copy).then_inc(e_qc, 1)
            for n in range(2 * B):
                act.wait_ge(e_kt, n + 1)
                act.activation(KT[:, 4 * n:4 * n + 4, :].rearrange("p q s -> p (q s)"), ps_b[n % 2], ACT.Copy).then_inc(e_ktc, 1)

            def copy_turned(kind, b, dst):
                for k, d in enumerate(dst):
                    f = fill_of[kind, b, k]
                    act.wait_ge(e_turn, f + 1)
                    src = ps[f % 2][:, 0:2 * P] if kind == "out" else ps_b[f % 2]
                    act.activation(d, src, ACT.Copy).then_inc(e_turned, 1)

            for step in range(FIRST, LAST):
                b = batch_at(step, AT_TURN)
                if b is not None:
                    if b >= 2:
                        act.wait_ge(e_i, NA * (b - 1))
                    copy_turned("q", b, [QT[:, 0, b % 2, 4 * k:4 * k + 4, :].rearrange("p q s -> p (q s)") for k in range(2)])
                b = batch_at(step, AT_TURN2)
                if b is not None:
                    if b >= 2:
                        act.wait_ge(e_j, NA * (b - 1))
                    copy_turned("q2", b, [QT[:, 1, b % 2, 4 * k:4 * k + 4, :].rearrange("p q s -> p (q s)") for k in range(2)])
                b = batch_at(step, AT_OUT)
                if b is not None:
                    if b >= 2:
                        act.wait_ge(e_turn, fill_of["y", b - 2, 0] + 1)
                    copy_turned("out", b, [OT[:, b % 2, :]])
                g = group_at(step, AT_GROUP - 1)
                if g is not None:
                    act.wait_ge(e_pv, g + 1)
                    if g >= 2:
                        act.wait_ge(e_turn, fill_of["group", g - 2, 0] + 1)
                    act.activation(OV[:, g % 2, :], ps[6 + g % 2][:, 0:S], ACT.Copy).then_inc(e_ov, 1)
                n = step - LAG_J
                if 0 <= n < NP:
                    act.wait_ge(e_j, n + 1)
                    if n >= 2 * OG:
                        act.wait_ge(e_pv, n // OG - 1)
                    act.activation(pT[:, n % (2 * OG), :], ps[4 + n % 2][:, 0:CUT], ACT.Exp, scale=float(AD) ** -0.5).then_inc(e_p, 1)

            cp = copy_xnt(5)
            for c in range(C):
                cp(c)
            act.wait_ge(f_d, 1)
            act.activation(f_e[:], f_z[:], ACT.Exp).then_inc(f_ex, 1)
            for n in range(E * C):
                if n >= 2:
                    act.wait_ge(f_y, n - 1)
                for k in range(GH):
                    act.wait_ge(f_h, 2 * GH * n + k + 1)
                    act.activation(hT[:, n % 2, k, :], ps[2 + k][:], ACT.Silu).then_inc(f_silu, 1)

        @block.tensor
        def _(pe):
            ln_count = [0]

            def turn_xn(c):
                n = ln_count[0]
                pe.wait_ge(xn_ready, n + 1)
                if n >= 2:
                    pe.wait_ge(xnt_ready, n - 1)
                for i in range(CT):
                    last = pe.transpose(ps[n % 2][:, i * P:(i + 1) * P], XN[:, c * CT + i, :], ident)
                last.then_inc(xnt_turned, 1)
                ln_count[0] += 1

            pe.wait_ge(s_const, 16)
            xt = XNT[0]

            def a_project(c):
                pe.wait_ge(xnt_ready, c + 1)
                if c == 0:
                    pe.wait_ge(s_wa, 48)
                if c >= 1:
                    pe.wait_ge(a_gate, c)
                    pe.wait_ge(a_drive, c)
                mov = xt[:, c * CW:(c + 1) * CW]
                pe.matmul(ps[2][:], wp[:, 0:D], mov, start=True, stop=True)
                pe.matmul(ps[3][:], wp[:, D:2 * D], mov, start=True, stop=True)
                pe.matmul(ps[4][:], wu[:], mov, start=True, stop=True).then_inc(a_proj, 1)

            def a_output(c):
                pe.wait_ge(a_scan, c + 1)
                if c >= 1:
                    pe.wait_ge(a_add, c)
                for i in range(CT):
                    last = pe.matmul(ps[5][:, i * P:(i + 1) * P], state[:, c % 2, i * P:(i + 1) * P], wo[:], start=True, stop=True)
                last.then_inc(a_out, 1)

            for c in range(C + 1):
                if c < C:
                    turn_xn(c)
                    a_project(c)
                if c >= 1:
                    a_output(c - 1)

            xt = XNT[1]
            pe.wait_ge(b_pad, 1)
            pe.wait_ge(s_ctxT, 16)
            for b in range(B):
                pe.matmul(ps[6][0:2 * R, 0:S], zpad[:, 1, b * 64:b * 64 + 64], ctxT[:, b * S:(b + 1) * S], start=(b == 0), stop=False)
            for c in range(C):
                turn_xn(c)
            for b in range(B):
                pe.wait_ge(xnt_ready, C + b // BC + 1)
                last = pe.matmul(ps[6][0:2 * R, 0:S], zpad[:, 0, b * 64:b * 64 + 64], xt[:, b * S:(b + 1) * S], start=False, stop=(b == B - 1))
            last.then_inc(b_gates, 1)
            pe.wait_ge(b_dve, 2)
            pe.wait_ge(b_exp, 2)
            for n, src in enumerate((g_b, g_e)):
                for i in range(2):
                    at = (2 * n + i) * R
                    last = pe.transpose(ps[2][:, at:at + R], src[:, i * P:(i + 1) * P], ident[0:R, 0:R])
            last.then_inc(b_turn, 1)

            def b_scores(r):
                b, h = divmod(r, NH)
                row = slice(HD * h, HD * h + HD)
                i0 = b * S
                if r == 0:
                    pe.wait_ge(b_turned, 1)
                    pe.wait_ge(pool_seq, 1)
                if r >= 2:
                    pe.wait_ge(b_dec, r - 1)
                    pe.wait_ge(b_ct, r - 1)
                dk, sk = ps[2 + r % 2], ps[4 + r % 2]
                pe.matmul(dk[:, 0:S], sel[:, r, :], g_g[:], start=True, stop=False)
                pe.matmul(dk[:, 0:P], ident_b[:], neg_ji_b[:], start=False, stop=True)
                pe.matmul(dk[:, S:CUT], sel[:, r, :], g_g[:, P:S], start=True, stop=False)
                pe.matmul(dk[:, S:CUT], ident_b[:], neg_ji_b[:], start=False, stop=True)
                pe.matmul(sk[:, 0:S], ctxT[row, i0:i0 + P], xt[row, i0:i0 + S], start=True, stop=True)
                pe.matmul(sk[:, S:CUT], ctxT[row, i0 + P:i0 + S], xt[row, i0 + P:i0 + S], start=True, stop=True).then_inc(b_sc, 1)

            def b_values(r):
                b, h = divmod(r, NH)
                pe.wait_ge(b_ct, r + 1)
                if h == 0 and b >= 2:
                    pe.wait_ge(b_num, 2 * (b - 1) - 1)
                if r == 0:
                    pe.wait_ge(s_ctx, 16 * NH)
                    pe.wait_ge(pool_const, 1)
                o = ps[6 + b % 2][:, 0:2 * NH * (HD + 1)].rearrange("p (i h d) -> p i h d", i=2, h=NH)
                ct = cT[:, r % 3, :]
                pe.matmul(o[:, 0, h, :], ct[:, 0:P], vaug[:, 2 * b, h, :], start=True, stop=True)
                pe.matmul(o[:, 1, h, :], ct[:, P:S], vaug[:, 2 * b, h, :], start=True, stop=False)
                pe.matmul(o[:, 1, h, :], ct[:, S:CUT], vaug[:, 2 * b + 1, h, :], start=False, stop=True).then_inc(b_pv, 1)

            for r in range(R + 1):
                if r < R:
                    b_scores(r)
                if r >= 1:
                    b_values(r - 1)

            xt = XNT[0]
            pe.wait_ge(c_wsq, 1)
            pe.matmul(ps[3][:, 0:E], ones[:], wsq[:], start=True, stop=True).then_inc(c_wn, 1)
            for c in range(C):
                turn_xn(c)
                pe.wait_ge(xnt_ready, 2 * C + c + 1)
                for t in range(c * CT, (c + 1) * CT):
                    last = pe.matmul(ps[2][:, t * E:(t + 1) * E], xt[:, t * P:(t + 1) * P], col("waffT"), start=True, stop=True)
            last.then_inc(c_num, 1)
            pe.wait_ge(c_gb, 1)
            pe.wait_ge(s_w2, 16)
            for e in range(E):
                for k in range(FK):
                    last = pe.matmul(ps[6][0:E, 0:D], gz[:, e, k, :], w2[:, e, k, :], start=(e == 0 and k == 0),
                                     stop=(e == E - 1 and k == FK - 1))
            last.then_inc(c_g0, 1)
            pe.wait_ge(c_sum, 1)
            pe.matmul(ps[7][:, 0:1], ones[:], asum[:], start=True, stop=True).then_inc(c_mean, 1)
            pe.wait_ge(c_oh, 1)
            for c in range(C):
                if c >= 2:
                    pe.wait_ge(c_turned, c - 1)
                for src, bank in ((aff, 2 + 2 * (c % 2)), (oh, 3 + 2 * (c % 2))):
                    for i in range(CT):
                        last = pe.transpose(ps[bank][0:E, i * P:(i + 1) * P], src[:, c * CT + i, :], ident)
                last.then_inc(c_turn, 1)
            for t in range(T):
                if t == 0:
                    pe.wait_ge(c_turned, C)
                if t >= 2:
                    pe.wait_ge(c_cnt, t - 1)
                q0 = (t // 2) * S
                pe.matmul(ps[4 + t % 2][:, 0:S], ohT[:, t * P:(t + 1) * P], affT[:, q0:q0 + S], start=True, stop=True).then_inc(c_row, 1)
            pe.wait_ge(c_nd, 1)
            for c in range(C):
                if c >= 2:
                    pe.wait_ge(c_turned, C + c - 1)
                for i in range(CT):
                    last = pe.transpose(ps[2 + c % 2][0:E, i * P:(i + 1) * P], ndisp[:, c * CT + i, :], ident)
                last.then_inc(c_turn, 1)
            pe.wait_ge(c_g0c, 1)
            for c in range(C):
                pe.wait_ge(c_turned, C + c + 1)
                if c >= 2:
                    pe.wait_ge(c_badd, c - 1)
                for i in range(CT):
                    o = ps[6 + c % 2][:, i * P:(i + 1) * P]
                    t = c * CT + i
                    pe.matmul(o, ndT[:, t * P:(t + 1) * P], G0[:], start=True, stop=False)
                    last = pe.matmul(o, ones[0:E, :], col("b2")[0:E, :], start=False, stop=True)
                last.then_inc(c_base, 1)

            def c_hidden(n):
                e, c = divmod(n, C)
                if n == 0:
                    pe.wait_ge(s_w1, 16)
                    pe.wait_ge(c_turned, 2 * C)
                for k in range(FK):
                    if n >= 1:
                        pe.wait_ge(c_act, FK * (n - 1) + k + 1)
                    if n == 0:
                        pe.wait_ge(c_cnt, T)
                    pe.matmul(ps[2 + k][:], w1[:, e, k * P:(k + 1) * P], xt[:, c * CW:(c + 1) * CW], start=True, stop=True).then_inc(c_h, 1)

            def c_down(n):
                e, c = divmod(n, C)
                pe.wait_ge(c_act, FK * (n + 1))
                if n < 2:
                    pe.wait_ge(c_badd, C)
                else:
                    pe.wait_ge(c_acc, n - 1)
                for i in range(CT):
                    for k in range(FK):
                        last = pe.matmul(ps[6 + n % 2][:, i * P:(i + 1) * P], hT[:, n % 2, k, i * P:(i + 1) * P], w2[:, e, k, :],
                                         start=(k == 0), stop=(k == FK - 1))
                last.then_inc(c_y, 1)

            for n in range(E * C + 1):
                if n < E * C:
                    c_hidden(n)
                if n >= 1:
                    c_down(n - 1)

            xt = XNT[1]
            pe.wait_ge(s_lw, 16)

            def d_project(c):
                pe.wait_ge(xnt_ready, 3 * C + c + 1)
                if c >= 1:
                    pe.wait_ge(d_act, c)
                mov = xt[:, c * CW:(c + 1) * CW]
                for k in range(3):
                    last = pe.matmul(ps[2 + k][:], lw[:, k * D:(k + 1) * D], mov, start=True, stop=True)
                last.then_inc(d_proj, 1)

            def d_output(c):
                pe.wait_ge(d_scan, c + 1)
                if c >= 1:
                    pe.wait_ge(d_add, c)
                for i in range(CT):
                    last = pe.transpose(ps[5][:, i * P:(i + 1) * P], drive[:, c % 2, i * P:(i + 1) * P], ident)
                last.then_inc(d_turn, 1)

            for c in range(C + 1):
                if c < C:
                    turn_xn(c)
                    d_project(c)
                if c >= 1:
                    d_output(c - 1)

            xt = XNT[0]
            pe.wait_ge(s_aw, 16)
            pe.wait_ge(c_acc, E * C)
            for b in range(B):
                if b >= 2:
                    pe.wait_ge(e_kvc, b - 1)
                for i in range(2):
                    t = 2 * b + i
                    last = pe.matmul(ps[6 + b % 2][:, i * 2 * D:(i + 1) * 2 * D], ctxT[:, t * P:(t + 1) * P], aw[:, D:3 * D], start=True, stop=True)
                last.then_inc(e_kv, 1)
            for c in range(C):
                turn_xn(c)
                pe.wait_ge(xnt_ready, 4 * C + c + 1)
                if c >= 2:
                    pe.wait_ge(e_qc, c - 1)
                for i in range(CT):
                    t = c * CT + i
                    last = pe.matmul(ps[2 + c % 2][:, i * P:(i + 1) * P], xt[:, t * P:(t + 1) * P], aw[:, 0:D], start=True, stop=True)
                last.then_inc(e_q, 1)
            pe.wait_ge(xnt_ready, 5 * C)
            for b in range(B):
                pe.wait_ge(e_kk, b + 1)
                for k in range(2):
                    n = 2 * b + k
                    if n >= 2:
                        pe.wait_ge(e_ktc, n - 1)
                    for q in range(4):
                        for i in range(2):
                            last = pe.transpose(ps_b[n % 2][:, (2 * q + i) * P:(2 * q + i + 1) * P],
                                                KK[:, b % 2, i, 8 * k + 2 * q:8 * k + 2 * q + 2, :].rearrange("p a s -> p (a s)"), ident_b[:])
                    last.then_inc(e_kt, 1)
            pe.wait_ge(e_ktc, 2 * B)
            pe.wait_ge(e_qc, C)
            pe.wait_ge(e_kvc, B)
            pe.wait_ge(e_va, 16 * B)

            def next_fill(kind, which, k):
                f = fill_of[kind, which, k]
                if f >= 2:
                    wait_read(pe, f - 2)
                return f

            def turn_queries(kind, b):
                for k in range(2):
                    f = next_fill(kind, b, k)
                    for q in range(4):
                        for i in range(2):
                            last = pe.transpose(ps_b[f % 2][:, (2 * q + i) * P:(2 * q + i + 1) * P],
                                                QQ[:, b % 2, i, 8 * k + 2 * q:8 * k + 2 * q + 2, :].rearrange("p a s -> p (a s)"), ident_b[:])
                    last.then_inc(e_turn, 1)

            for step in range(FIRST, LAST):
                b = batch_at(step, AT_TURN)
                if b is not None:
                    pe.wait_ge(e_qq, b + 1)
                    turn_queries("q", b)
                b = batch_at(step, AT_TURN2)
                if b is not None:
                    pe.wait_ge(e_mq, b + 1)
                    turn_queries("q2", b)
                n = step
                if 0 <= n < NP:
                    b, a = divmod(n, NA)
                    rows = slice(SL * (a % 2), SL * (a % 2) + 6 * AD)
                    qt, kt = QT[rows, 0, b % 2, a // 2, :], KT[rows, n // 2, :]
                    if a % 8 == 0:
                        wait_read(pe, fill_of["q", b, a // 8])
                    if n >= 2:
                        pe.wait_ge(e_max, n - 1)
                    o = ps[2 + n % 2]
                    pe.matmul(o[:, 0:P], qt[:, 0:P], kt[:, 0:P], start=True, stop=False)
                    pe.matmul(o[:, 0:P], ident_b[:], neg_ij_b[:], start=False, stop=True)
                    pe.matmul(o[:, P:CUT], qt[:, P:S], kt[:, 0:S], start=True, stop=False)
                    pe.matmul(o[:, S:CUT], ident_b[:], neg_ij_b[:], start=False, stop=True).then_inc(e_i, 1)
                n = step - LAG_J
                if 0 <= n < NP:
                    b, a = divmod(n, NA)
                    rows = slice(SL * (a % 2), SL * (a % 2) + 6 * AD + 3)
                    qt, kt = QT[rows, 1, b % 2, a // 2, :], KT[rows, n // 2, :]
                    if a % 8 == 0:
                        wait_read(pe, fill_of["q2", b, a // 8])
                    if n >= 2:
                        pe.wait_ge(e_p, n - 1)
                    o = ps[4 + n % 2]
                    pe.matmul(o[:, 0:S], kt[:, 0:P], qt[:, 0:S], start=True, stop=False)
                    pe.matmul(o[:, 0:P], ident_b[:], neg_ji_b[:], start=False, stop=True)
                    pe.matmul(o[:, S:CUT], kt[:, P:S], qt[:, P:S], start=True, stop=False)
                    pe.matmul(o[:, S:CUT], ident_b[:], neg_ji_b[:], start=False, stop=True).then_inc(e_j, 1)
                g = group_at(step, AT_PV)
                if g is not None:
                    pe.wait_ge(e_p, OG * (g + 1))
                    if g >= 2:
                        pe.wait_ge(e_ov, g - 1)
                    for i in range(2):
                        for j in range(OG):
                            n = g * OG + j
                            o = ps[6 + g % 2][OW * j:OW * (j + 1), i * P:S]
                            v = v_room[:, (2 * n + i) * (AD + 1):(2 * n + i) * (AD + 1) + OW]
                            last = pe.matmul(o, v, pT[:, n % (2 * OG), i * S:CUT if i else S], start=(i == 0), stop=(i == 1))
                    last.then_inc(e_pv, 1)
                g = group_at(step, AT_GROUP)
                if g is not None:
                    f = next_fill("group", g, 0)
                    pe.wait_ge(e_ov, g + 1)
                    for i in range(2):
                        last = pe.transpose(ps[f % 2][:, i * P:(i + 1) * P], OV[:, g % 2, i * P:(i + 1) * P], ident)
                    last.then_inc(e_turn, 1)
                b = batch_at(step, AT_OUT)
                if b is not None:
                    f = next_fill("out", b, 0)
                    pe.wait_ge(e_ot[b % 2], 16 * (b // 2 + 1))
                    for i in range(2):
                        last = pe.transpose(ps[f % 2][:, i * P:(i + 1) * P], Otm[:, b % 2, i, :], ident)
                    last.then_inc(e_turn, 1)
                b = batch_at(step, AT_Y)
                if b is not None:
                    f = next_fill("y", b, 0)
                    wait_read(pe, fill_of["out", b, 0])
                    for i in range(2):
                        last = pe.matmul(ps[f % 2][:, i * P:(i + 1) * P], OT[:, b % 2, i * P:(i + 1) * P], aw[:, 3 * D:4 * D], start=True, stop=True)
                    last.then_inc(e_turn, 1)

            xt = XNT[1]
            wait_read(pe, len(fills) - 1)
            wait_read(pe, fill_of["out", B - 1, 0])
            for c in range(C):
                turn_xn(c)
                pe.wait_ge(xnt_ready, 5 * C + c + 1)
                if c == 0:
                    pe.wait_ge(e_max, NP)
                    pe.wait_ge(e_p, NP)
                for t in range(c * CT, (c + 1) * CT):
                    last = pe.matmul(ps[2][:, t * E:(t + 1) * E], xt[:, t * P:(t + 1) * P], col("gateT"), start=True, stop=True)
            last.then_inc(f_sc, 1)
            pe.wait_ge(s_w12, 16)
            pe.wait_ge(s_w3, 16)
            pe.wait_ge(f_d, 1)
            pe.wait_ge(e_add, B)

            def f_hidden(n):
                e, c = divmod(n, C)
                for k in range(2 * GH):
                    if n >= 1:
                        if k < GH:
                            pe.wait_ge(f_silu, GH * (n - 1) + k + 1)
                        else:
                            pe.wait_ge(f_mul, GH * (n - 1) + k - GH + 1)
                    pe.matmul(ps[2 + k][:], w12[:, e, k * P:(k + 1) * P], xt[:, c * CW:(c + 1) * CW], start=True, stop=True).then_inc(f_h, 1)

            def f_down(n):
                e, c = divmod(n, C)
                pe.wait_ge(f_mul, GH * (n + 1))
                if n >= 2:
                    pe.wait_ge(f_acc, n - 1)
                for i in range(CT):
                    for k in range(GH):
                        last = pe.matmul(ps[6 + n % 2][:, i * P:(i + 1) * P], hT[:, n % 2, 2 + k, i * P:(i + 1) * P], w3[:, e, k, :],
                                         start=(k == 0), stop=(k == GH - 1))
                last.then_inc(f_y, 1)

            for n in range(E * C + 1):
                if n < E * C:
                    f_hidden(n)
                if n >= 1:
                    f_down(n - 1)

        @block.vector
        def _(dve):
            chain = [0]
            ln_count = [0]

            def link(ins):
                chain[0] += 1
                ins.then_inc(dve_seq, 1)
                dve.wait_ge(dve_seq, chain[0])

            def layer_norm(c):
                t0, t1 = c * CT, (c + 1) * CT
                for t in range(t0, t1):
                    last = dve.bn_stats(stats[:, t, :], X[:, t, :])
                link(last)
                for t in range(t0, t1):
                    last = dve.bn_aggr(mv[:, t, :], stats[:, t, :])
                link(last)
                dve.tensor_scalar(vareps[:, t0:t1], mv[:, t0:t1, 1], LN_EPS, None, ALU.add).then_inc(var_ready, 1)
                ln_count[0] += 1
                dve.wait_ge(rstd_ready, ln_count[0])
                for t in range(t0, t1):
                    last = dve.tensor_scalar(XN[:, t, :], X[:, t, :], mv[:, t, 0:1], rstd[:, t:t + 1], ALU.subtract, ALU.mult)
                last.then_inc(xn_ready, 1)

            dve.wait_ge(s_x, 16)

            def a_scan_chunk(c):
                k = c % 2
                dve.wait_ge(s_small, 16)
                dve.wait_ge(a_gate, c + 1)
                if c >= 2:
                    dve.wait_ge(a_out, c - 1)
                dve.scalar_tensor_tensor(out=drive[:, k, :], in0=ps[4][:], scalar=col("bu"), in1=gate[:, k, :], op0=ALU.add, op1=ALU.mult)
                link(dve.scalar_tensor_tensor(out=decay[:, k, :], in0=tnh[:, k, :], scalar=-1.0, in1=gate[:, k, :], op0=ALU.add, op1=ALU.mult))
                link(dve.tensor_scalar(decay[:, k, :], decay[:, k, :], 1.0, None, ALU.add))
                for b in range(BC):
                    sl = slice(b * S, (b + 1) * S)
                    last = dve.tensor_tensor_scan(state[:, k, sl], decay[:, k, sl], drive[:, k, sl], 0.0, ALU.mult, ALU.add)
                    if b == 0:
                        last.then_inc(a_drive, 1)
                last.then_inc(a_scan, 1)

            def a_residual(c):
                dve.wait_ge(a_out, c + 1)
                dve.wait_ge(a_bias, c + 1)
                ch = X[:, c * CT:(c + 1) * CT, :]
                ins = dve.tensor_tensor(ch, ps[5][:].rearrange("p (t d) -> p t d", d=D), ch, ALU.add)
                ins.then_inc(a_add, 1)

            layer_norm(0)
            for c in range(C):
                if c + 1 < C:
                    layer_norm(c + 1)
                if c == 0:
                    dve.wait_ge(s_const, 16)
                    dve.tensor_copy(ident_b[:], ident)
                    dve.tensor_copy(neg_ji_b[:], cst("neg_ji"))
                    dve.tensor_copy(neg_ij_b[:], cst("neg_ij"))
                a_scan_chunk(c)
                if c >= 1:
                    a_residual(c - 1)
            a_residual(C - 1)

            for c in range(C):
                dve.wait_ge(a_add, c + 1)
                layer_norm(c)
            dve.tensor_scalar(rms1[:], col("rms"), 1.0, None, ALU.add)
            dve.wait_ge(b_gates, 1)
            gb = col("gbias")
            dve.tensor_scalar(g_i[:], ps[6][0:R, 0:S], gb[0:R, :], None, ALU.add)
            link(dve.tensor_scalar(g_f[:], ps[6][R:2 * R, 0:S], gb[R:2 * R, :], None, ALU.add))
            dve.tensor_scalar(g_l[:], g_f[:], 0.0, None, ALU.min)
            dve.scalar_tensor_tensor(out=g_n[:], in0=g_f[:], scalar=-1.0, in1=g_f[:], op0=ALU.mult, op1=ALU.min).then_inc(b_dve, 1)
            dve.wait_ge(b_dve, 1)
            dve.wait_ge(b_exp, 1)
            link(dve.tensor_tensor(g_l[:], g_l[:], g_n[:], ALU.subtract))
            dve.wait_ge(pool_const, 1)
            link(dve.tensor_tensor_scan(g_cs[:], ones[0:R, 0:1].to_broadcast([R, S]), g_l[:], 0.0, ALU.mult, ALU.add))
            link(dve.tensor_tensor(g_b[:], g_i[:], g_cs[:], ALU.subtract))
            link(dve.tensor_tensor_scan(g_g[:], g_b[:], g_b[:], -3.0e38, ALU.max, ALU.max))
            dve.tensor_tensor(g_m[:], g_cs[:], g_g[:], ALU.add).then_inc(b_dve, 1)

            def b_norm(b):
                o = ps[6 + b % 2][:, 0:2 * NH * (HD + 1)].rearrange("p (g d) -> p g d", d=HD + 1)
                dve.wait_ge(b_pv, NH * (b + 1))
                em = bT[:, 1, :, NH * b:NH * b + NH]
                link(dve.tensor_tensor(hn[:].rearrange("p (i h) -> p i h", i=2),
                                       o[:, :, HD].rearrange("p (i h) -> p i h", i=2), em, ALU.max))
                link(dve.tensor_scalar(hn[:], hn[:], 1e-6, None, ALU.add))
                link(dve.reciprocal(hr[:], hn[:]))
                dve.tensor_tensor(hh[:], o[:, :, 0:HD], hr[:].unsqueeze(2).to_broadcast([P, 2 * NH, HD]), ALU.mult).then_inc(b_num, 1)
                dve.wait_ge(b_num, 2 * b + 1)
                link(dve.tensor_tensor(hq[:], hh[:], hh[:], ALU.mult))
                link(dve.tensor_reduce(hv[:], hq[:], AX.X, ALU.add))
                dve.tensor_scalar(hv2[:], hv[:], 1.0 / HD, 1e-6, ALU.mult, ALU.add).then_inc(pow_asked, 1)
                dve.wait_ge(pow_done, b + 1)
                link(dve.tensor_tensor(hq[:], hh[:], hv[:].unsqueeze(2).to_broadcast([P, 2 * NH, HD]), ALU.mult))
                link(dve.tensor_tensor(hh[:], hq[:], rms1[:].unsqueeze(1).to_broadcast([P, 2 * NH, HD]), ALU.mult))
                xx = X[:, 2 * b:2 * b + 2, :].rearrange("p t (h d) -> p (t h) d", h=NH)
                dve.tensor_tensor(xx, xx, hh[:], ALU.add).then_inc(b_num, 1)

            for r in range(R):
                b, h = divmod(r, NH)
                dve.wait_ge(b_dec, r + 1)
                if r >= 3:
                    dve.wait_ge(b_pv, r - 2)
                dve.scalar_tensor_tensor(out=cT[:, r % 3, :], in0=ps[4 + r % 2][:, 0:CUT], scalar=float(HD) ** -0.5,
                                         in1=dec[:, r % 3, :], op0=ALU.mult, op1=ALU.mult).then_inc(b_ct, 1)
                if h == 0 and b >= 1:
                    b_norm(b - 1)
            b_norm(B - 1)

            dve.tensor_tensor(wsq[:], col("waffT"), col("waffT"), ALU.mult).then_inc(c_wsq, 1)
            for c in range(C):
                dve.wait_ge(b_num, 2 * BC * (c + 1))
                layer_norm(c)
            dve.wait_ge(c_wn, 1)
            dve.tensor_copy(wsum[:], ps[3][:, 0:E]).then_inc(pow_asked, 1)
            dve.wait_ge(pow_done, B + 1)
            link(dve.tensor_tensor(den[:], xnm[:].unsqueeze(2).to_broadcast([P, T, E]),
                                   wn[:].unsqueeze(1).to_broadcast([P, T, E]), ALU.mult))
            link(dve.tensor_scalar(den[:], den[:], 1e-9, None, ALU.add))
            link(dve.reciprocal(rden[:], den[:]))
            dve.wait_ge(c_num, 1)
            link(dve.tensor_tensor(aff[:], ps[2][:, 0:T * E].rearrange("p (t e) -> p t e", e=E), rden[:], ALU.mult))
            dve.tensor_reduce(asum[:], aff[:], AX.XY, ALU.add).then_inc(c_sum, 1)
            link(dve.tensor_reduce(amax[:], aff[:], AX.X, ALU.max))

            def first_max(dst, scores, best):
                link(dve.tensor_tensor(eq[:], scores, best[:].unsqueeze(2).to_broadcast([P, T, E]), ALU.is_equal))
                link(dve.tensor_tensor(pri[:], eq[:], col("prio").unsqueeze(1).to_broadcast([P, T, E]), ALU.mult))
                link(dve.tensor_reduce(pm[:], pri[:], AX.X, ALU.max))
                return dve.tensor_tensor(dst[:], pri[:], pm[:].unsqueeze(2).to_broadcast([P, T, E]), ALU.is_equal)

            first_max(oh, aff[:], amax).then_inc(c_oh, 1)
            dve.wait_ge(c_mean, 1)
            dve.scalar_tensor_tensor(out=zc[:], in0=ps[7][:, 0:1], scalar=1.0 / (T * P * E), in1=col("thr"),
                                     op0=ALU.mult, op1=ALU.subtract).then_inc(c_z, 1)
            dve.wait_ge(c_g0, 1)
            dve.tensor_copy(G0[:], ps[6][0:E, 0:D]).then_inc(c_g0c, 1)
            dve.wait_ge(c_sig, 1)
            link(dve.tensor_scalar(cap[:], sg[:], float(S), 4.0, ALU.mult, ALU.max))
            link(dve.tensor_scalar(cap[:], cap[:], float(S), None, ALU.min))
            for t in range(T):
                dve.wait_ge(c_row, t + 1)
                m = (t % 2) * S
                row = ps[4 + t % 2][:, 0:S]
                if t >= 1:
                    dve.wait_ge(c_cnt, t)
                own = amax[:, t:t + 1]
                dve.scalar_tensor_tensor(out=cj[:, 0, :], in0=row, scalar=own, in1=cst("before")[:, m:m + S],
                                         op0=ALU.is_ge, op1=ALU.mult, accum_out=cnt[:, 0, t:t + 1])
                dve.scalar_tensor_tensor(out=cj[:, 1, :], in0=row, scalar=own, in1=cst("after")[:, m:m + S],
                                         op0=ALU.is_gt, op1=ALU.mult, accum_out=cnt[:, 1, t:t + 1]).then_inc(c_cnt, 1)
            dve.wait_ge(c_cnt, T)
            link(dve.scalar_tensor_tensor(out=rank1[:], in0=cnt[:, 0, :], scalar=1.0, in1=cnt[:, 1, :], op0=ALU.add, op1=ALU.add))
            link(dve.tensor_scalar(keep[:], rank1[:], cap[:], None, ALU.is_le))
            link(dve.tensor_tensor(disp[:], oh[:], keep[:].unsqueeze(2).to_broadcast([P, T, E]), ALU.mult))
            dve.tensor_scalar(ndisp[:], disp[:], -1.0, 1.0, ALU.mult, ALU.add).then_inc(c_nd, 1)
            for c in range(C):
                dve.wait_ge(c_base, c + 1)
                ch = X[:, c * CT:(c + 1) * CT, :]
                dve.tensor_tensor(ch, ps[6 + c % 2][:].rearrange("p (t d) -> p t d", d=D), ch, ALU.add).then_inc(c_badd, 1)
            for n in range(E * C):
                e, c = divmod(n, C)
                dve.wait_ge(c_y, n + 1)
                if e == 0:
                    dve.wait_ge(c_badd, c + 1)
                else:
                    dve.wait_ge(c_acc, n - C + 1)
                for i in range(CT):
                    t = c * CT + i
                    last = dve.scalar_tensor_tensor(out=X[:, t, :], in0=ps[6 + n % 2][:, i * P:(i + 1) * P],
                                                    scalar=disp[:, t, e:e + 1], in1=X[:, t, :], op0=ALU.mult, op1=ALU.add)
                last.then_inc(c_acc, 1)

            def d_scan_chunk(c):
                k = c % 2
                dve.wait_ge(d_act, c + 1)
                if c >= 2:
                    dve.wait_ge(d_turn, c - 1)
                dve.tensor_scalar(decay[:, k, :], state[:, k, :], 0.998, 0.001, ALU.mult, ALU.add)
                link(dve.tensor_tensor(gate[:, k, :], gate[:, k, :], tnh[:, k, :], ALU.mult))
                for b in range(BC):
                    sl = slice(b * S, (b + 1) * S)
                    last = dve.tensor_tensor_scan(drive[:, k, sl], decay[:, k, sl], gate[:, k, sl], 0.0, ALU.mult, ALU.add)
                last.then_inc(d_scan, 1)

            def d_residual(c):
                dve.wait_ge(d_turn, c + 1)
                ch = X[:, c * CT:(c + 1) * CT, :]
                dve.tensor_tensor(ch, ps[5][:].rearrange("p (t d) -> p t d", d=D), ch, ALU.add).then_inc(d_add, 1)

            for c in range(C):
                dve.wait_ge(c_acc, (E - 1) * C + c + 1)
                layer_norm(c)
                if c >= 1:
                    d_scan_chunk(c - 1)
                if c >= 2:
                    d_residual(c - 2)
            d_scan_chunk(C - 1)
            d_residual(C - 2)
            d_residual(C - 1)

            for c in range(C):
                dve.wait_ge(d_add, c + 1)
                layer_norm(c)
            parts = 0
            for step in range(FIRST, LAST):
                b = batch_at(step, AT_SPLIT)
                if b is not None:
                    k = b % 2
                    dve.wait_ge(e_fill, 2)
                    dve.wait_ge(e_qs[k], 16 * (b // 2 + 1))
                    if b >= 2:
                        dve.wait_ge(e_turn, fill_of["q2", b - 2, 1] + 1)
                    src = Qs[:, k].rearrange("p (a i) d -> p i a d", i=2)
                    va, vb = (v[:].rearrange("p (a i) d -> p i a d", i=2) for v in (q1, q2))
                    slot = [QQ[:, k, :, :, AD * j:AD * (j + 1)] for j in range(6)]
                    parts = split_parts(dve, e_qpart, parts, src, va, vb, slot[0], slot[1], slot[3])
                    dve.tensor_copy(slot[2], slot[0])
                    dve.tensor_copy(slot[4], slot[0])
                    dve.tensor_copy(slot[5], slot[1]).then_inc(e_qq, 1)
                b = batch_at(step, AT_MAX)
                if b is not None:
                    k = b % 2
                    dve.wait_ge(e_max, NA * (b + 1))
                    dve.tensor_scalar(mx[:, 0, :], mx3[:, k, :, 0], -1.0, None, ALU.mult)
                    link(dve.tensor_tensor(mr[:, 0, :], mx3[:, k, :, 1], mx3[:, k, :, 2], ALU.max))
                    link(dve.tensor_scalar(mx[:, 1, :], mr[:, 0, :], -1.0, None, ALU.mult))
                    top = [QQ[:, k, :, :, 6 * AD + j] for j in range(3)]
                    parts = split_parts(dve, e_qpart, parts, mx[:], mr[:], mr2[:], *top)
                    dve.sem_inc(e_mq, 1)
                g = group_at(step, AT_GROUP)
                if g is not None:
                    b, a = divmod(g * OG, NA)
                    f = fill_of["group", g, 0]
                    dve.wait_ge(e_turn, f + 1)
                    if a == 0 and b >= 2:
                        dve.wait_ge(e_od[b % 2], 16 * (b // 2))
                    o = ps[f % 2][:, 0:2 * P].rearrange("p (i a d) -> p i a d", i=2, d=OW)
                    dve.reciprocal(orec[:], o[:, :, :, AD]).then_inc(e_rec, 1)
                    dve.wait_ge(e_rec, g + 1)
                    dst = Os[:, b % 2, 2 * a:2 * (a + OG), :].rearrange("p (a i) d -> p i a d", i=2)
                    dve.tensor_tensor(dst, o[:, :, :, 0:AD], orec[:].unsqueeze(3).to_broadcast([P, 2, OG, AD]), ALU.mult).then_inc(e_read, 1)
                    dve.wait_ge(e_read, read_count(f))
                    dve.sem_inc(e_o, 1)
                n = step
                if 0 <= n < NP:
                    b, a = divmod(n, NA)
                    dve.wait_ge(e_i, n + 1)
                    dve.tensor_reduce(mx3[:, b % 2, a, :], ps[2 + n % 2][:, 0:CUT].rearrange("p (g j) -> p g j", g=3), AX.X, ALU.max).then_inc(e_max, 1)
                b = batch_at(step, AT_Y)
                if b is not None:
                    f = fill_of["y", b, 0]
                    dve.wait_ge(e_turn, f + 1)
                    xx = X[:, 2 * b:2 * b + 2, :]
                    dve.tensor_tensor(xx, ps[f % 2][:, 0:2 * P].rearrange("p (t d) -> p t d", d=D), xx, ALU.add).then_inc(e_read, 1)
                    dve.wait_ge(e_read, read_count(f))
                    dve.sem_inc(e_add, 1)

            for c in range(C):
                dve.wait_ge(e_add, BC * (c + 1))
                layer_norm(c)
            dve.wait_ge(f_sc, 1)
            link(dve.tensor_copy(aff[:], ps[2][:, 0:T * E].rearrange("p (t e) -> p t e", e=E)))
            link(dve.tensor_reduce(amax[:], aff[:], AX.X, ALU.max))
            link(first_max(oh, aff[:], amax))
            link(dve.scalar_tensor_tensor(out=rden[:], in0=oh[:], scalar=-3.0e38, in1=aff[:], op0=ALU.mult, op1=ALU.add))
            link(dve.tensor_reduce(f_m2[:], rden[:], AX.X, ALU.max))
            dve.tensor_tensor(f_z[:], f_m2[:], amax[:], ALU.subtract).then_inc(f_d, 1)
            link(first_max(ndisp, rden[:], f_m2))
            dve.wait_ge(f_ex, 1)
            link(dve.tensor_scalar(f_p[:], f_e[:], 1.0, None, ALU.add))
            link(dve.reciprocal(f_m2[:], f_p[:]))
            link(dve.tensor_tensor(f_p[:], f_e[:], f_m2[:], ALU.mult))
            link(dve.tensor_tensor(disp[:], oh[:], f_m2[:].unsqueeze(2).to_broadcast([P, T, E]), ALU.mult))
            link(dve.tensor_tensor(ndisp[:], ndisp[:], f_p[:].unsqueeze(2).to_broadcast([P, T, E]), ALU.mult))
            link(dve.tensor_tensor(disp[:], disp[:], ndisp[:], ALU.add))

            def f_hidden_mul(n):
                for k in range(GH):
                    dve.wait_ge(f_h, 2 * GH * n + GH + k + 1)
                    dve.wait_ge(f_silu, GH * n + k + 1)
                    if n >= 2:
                        dve.wait_ge(f_y, n - 1)
                    dve.tensor_tensor(hT[:, n % 2, 2 + k, :], ps[2 + GH + k][:], hT[:, n % 2, k, :], ALU.mult).then_inc(f_mul, 1)

            def f_accumulate(n):
                e, c = divmod(n, C)
                dve.wait_ge(f_y, n + 1)
                if e >= 1:
                    dve.wait_ge(f_acc, n - C + 1)
                for i in range(CT):
                    t = c * CT + i
                    last = dve.scalar_tensor_tensor(out=X[:, t, :], in0=ps[6 + n % 2][:, i * P:(i + 1) * P],
                                                    scalar=disp[:, t, e:e + 1], in1=X[:, t, :], op0=ALU.mult, op1=ALU.add)
                last.then_inc(f_acc, 1)

            for n in range(E * C + 1):
                if n < E * C:
                    f_hidden_mul(n)
                if n >= 1:
                    f_accumulate(n - 1)


def _constants():
    c = np.zeros((P, NCONST), np.float32)
    i = np.arange(P)
    c[:, 0:P] = np.eye(P, dtype=np.float32)
    c[:, P:2 * P] = np.where(i[:, None] > i[None, :], NEG, 0.0)
    c[:, 2 * P:3 * P] = np.where(i[None, :] > i[:, None], NEG, 0.0)
    s = np.arange(S)
    for h in range(2):
        before = (s[None, :] < (h * P + i)[:, None]).astype(np.float32)
        c[:, 3 * P + h * S:3 * P + (h + 1) * S] = before
        c[:, 3 * P + 2 * S + h * S:3 * P + 2 * S + (h + 1) * S] = 1.0 - before
    return c


def kernel(**inputs):
    import concourse.bacc as _bacc
    from concourse import mybir as _mybir
    from concourse.bass_utils import run_bass_kernel_spmd as _run

    g = {k: np.asarray(v) for k, v in inputs.items()}
    small = np.zeros((P, NCOLS), np.float32)

    def put(name, a):
        at, w = COLS[name]
        small[0:a.shape[0], at:at + w] = a

    bp = g["L0_attn_bp"].reshape(3, D)
    put("bw", bp[0][:, None])
    put("bk", bp[1][:, None])
    put("bu", g["L0_attn_bu"][:, None])
    put("bg", g["L1_attn_bg"][:, None])
    put("bv", g["L1_attn_bv"][:, None])
    put("bd", g["L1_attn_bd"][:, None])
    put("b1", g["L0_ffn_b1"].reshape(E * FK, P).T)
    gi, gf = g["L0_xattn_igate_kernel"].reshape(3, D, NH), g["L0_xattn_fgate_kernel"].reshape(3, D, NH)
    for n, name in enumerate(("gq", "gk", "gv")):
        put(name, np.concatenate([gi[n], gf[n]], axis=1))
    put("gbias", np.concatenate([np.tile(g["L0_xattn_igate_bias"], B), np.tile(g["L0_xattn_fgate_bias"], B)])[:, None])
    put("thr", np.broadcast_to(g["L0_ffn_affinity_threshold"].reshape(1, 1), (P, 1)))
    put("rms", np.broadcast_to(g["L0_xattn_rms_scale"][None, :], (P, HD)))
    put("bo", np.broadcast_to(g["L0_attn_bo"][None, :], (P, D)))
    put("waffT", g["L0_ffn_waff"].T)
    put("gateT", g["L1_ffn_gate_w"].T)
    put("b2", g["L0_ffn_b2"])
    put("prio", np.broadcast_to(np.arange(E, 0, -1, dtype=np.float32)[None, :], (P, E)))

    arrays = {
        "x": g["x"].reshape(B * S, D),
        "ctx": g["ctx_1024"].reshape(B * S, D),
        "ctxT": g["ctx_1024"].reshape(B * S, D).T,
        "small": small,
        "const": _constants(),
        "wp": g["L0_attn_Wp"],
        "wu": g["L0_attn_Wu"],
        "wo": g["L0_attn_Wo"],
        "w1": g["L0_ffn_W1"].transpose(1, 0, 2),
        "w2": g["L0_ffn_W2"].reshape(E, FK, P, D).transpose(2, 0, 1, 3),
        "lw": np.concatenate([g["L1_attn_Wg"].T, g["L1_attn_Wv"].T, g["L1_attn_Wd"].T], axis=1),
        "aw": np.concatenate([g["L1_xattn_wq"].T, g["L1_xattn_wk"].T, g["L1_xattn_wv"].T, g["L1_xattn_wo"].T], axis=1),
        "w12": g["L1_ffn_w12"].transpose(2, 0, 1),
        "w3": g["L1_ffn_w3"].reshape(E, D, GH, P).transpose(3, 0, 2, 1),
    }
    nc = _bacc.Bacc("TRN2", target_bir_lowering=False, num_devices=1)
    feed, args = {}, []
    for name, a in arrays.items():
        a = np.ascontiguousarray(a)
        feed[f"in_{name}"] = a
        args.append(nc.dram_tensor(f"in_{name}", a.shape, _mybir.dt.from_np(a.dtype), kind="ExternalInput").ap())
    args.append(nc.dram_tensor("out_x", (B * S, D), F32, kind="ExternalOutput").ap())
    build(nc, *args)
    r = _run(nc, [feed], core_ids=[0])
    return r.results[0]["out_x"].reshape(B, S, D)
```

```python
from contextlib import ExitStack

import numpy as np
import concourse.bass as bass
from concourse import mybir


F32 = mybir.dt.float32
BF16 = mybir.dt.bfloat16
I32 = mybir.dt.int32
ALU = mybir.AluOpType
ACT = mybir.ActivationFunctionType
AX = mybir.AxisListType

B, S, D = 8, 256, 128
P = 128
T = B * S // P
C = 4
CT = T // C
CW = CT * P
BC = CW // S
NH = 4
HD = D // NH
R = B * NH
E = 8
FK = 4
GH = 2
NA = 16
AD = 8
NP = B * NA
CUT = 2 * P + P
SL = 64
OW = 32
HW = 64
OG = P // OW
NEG = -1.0e30
LN_EPS = 1e-5

COLS = {}
C_SLOTS = T + E - 1
C_GROUPS = -(-C_SLOTS // CT)
C_ZERO = C_SLOTS * P


def _pack_columns():
    at = 0
    for name, width in (("bw", 1), ("bk", 1), ("bu", 1), ("bg", 1), ("bv", 1), ("bd", 1), ("b1", E * FK),
                        ("gq", 8), ("gk", 8), ("gv", 8), ("gbias", 1), ("thr", 1), ("rms", HD), ("bo", D),
                        ("waffT", E), ("gateT", E), ("b2", D), ("prio", E)):
        COLS[name] = (at, width)
        at += width
    return at


NCOLS = _pack_columns()

CONST = {"ident": (0, P), "neg_ji": (P, P), "neg_ij": (2 * P, P), "before": (3 * P, 2 * S), "after": (3 * P + 2 * S, 2 * S),
         "minus3": (3 * P + 4 * S, R), "earlier": (3 * P + 4 * S + R, P), "tile_sizes": (4 * P + 4 * S + R, T),
         "slot": (4 * P + 4 * S + R + T, C_SLOTS), "spare": (4 * P + 4 * S + R + T + C_SLOTS, T)}
NCONST = CONST["spare"][0] + T


def build(nc, x, ctx_in, ctxT_in, small_in, const_in, wp_in, wu_in, wo_in, w1_in, w2_in, lw_in, aw_in, w12_in, w3_in, out):
    es = ExitStack()
    with es:
        def sb(name, shape, dt=F32):
            return es.enter_context(nc.sbuf_tensor(name, shape, dt))

        def sem(name):
            return es.enter_context(nc.semaphore(name))

        X = sb("X", [P, T, D])
        XN = sb("XN", [P, T, D])
        XNT = [sb(f"XNT{i}", [P, T * P]) for i in range(2)]
        small = sb("small", [P, NCOLS])
        const = sb("const", [P, NCONST])
        ctxT = sb("ctxT", [P, T * P])
        ones = sb("ones", [P, P])
        zeros_b = sb("zeros_b", [P, SL], BF16)
        ident_b = sb("ident_b", [P, P], BF16)
        neg_ji_b = sb("neg_ji_b", [P, P], BF16)
        neg_ij_b = sb("neg_ij_b", [P, P], BF16)
        wp = sb("wp", [P, 3 * D])
        wu = sb("wu", [P, D])
        wo = sb("wo", [P, D])
        lw = sb("lw", [P, 3 * D])
        aw = sb("aw", [P, 4 * D])
        stats = sb("stats", [P, T, 6])
        mv = sb("mv", [P, T, 2])
        vareps = sb("vareps", [P, T])
        rstd = sb("rstd", [P, T])
        power = sb("power", [P, 2])

        scan_room = sb("scan_room", [P, 5, 2 * CW])
        gate, tnh, decay, drive, state = (scan_room[:, i, :].rearrange("p (n c) -> p n c", n=2) for i in range(5))

        zpad = sb("zpad", [P, 2, 68 * B])
        gkv = sb("gkv", [P, 8])
        sel_room = sb("sel_room", [P, R * P])
        sel = sel_room[0:3 * R, 0:R * P // 2].bitcast(BF16).rearrange("p (r m) -> p r m", m=P)
        gp = sb("gp", [3 * R, S], BF16)
        g_part = sb("g_part", [R, S], BF16)
        g_i = sb("g_i", [R, S])
        g_f = sb("g_f", [R, S])
        g_n = sb("g_n", [R, S])
        g_l = sb("g_l", [R, S])
        g_e = sb("g_e", [R, S])
        g_cs = sb("g_cs", [R, S])
        g_b = sb("g_b", [R, S])
        g_g = sb("g_g", [R, S])
        g_m = sb("g_m", [R, S])
        bT = sb("bT", [P, 2, 2, R])
        v_room = sb("v_room", [P, 2 * NP * (AD + 1) + OW])
        vaug = v_room[:, 0:T * NH * (HD + 1)].rearrange("p (t h d) -> p t h d", t=T, h=NH)
        score_room = sb("score_room", [P, 2 * OG * CUT])
        cT = score_room[:].rearrange("p (n c) -> p n c", n=2 * NH)
        hn = sb("hn", [P, 2 * NH])
        hr = sb("hr", [P, 2 * NH])
        hh = sb("hh", [P, 2 * NH, HD])
        hq = sb("hq", [P, 2 * NH, HD])
        hv = sb("hv", [P, 2 * NH])
        hv2 = sb("hv2", [P, 2 * NH])
        rms1 = sb("rms1", [P, HD])

        w_room = sb("w_room", [P, 2 * E * FK * P])
        w1 = w_room[:, 0:E * FK * P].rearrange("p (e f) -> p e f", e=E)
        w2 = w_room[:, E * FK * P:].rearrange("p (e k d) -> p e k d", e=E, k=FK)
        h_room = sb("h_room", [P, 2 * FK * CW])
        hS = h_room[:, 0:2 * FK * P].rearrange("p (n k c) -> p n k c", n=2, k=FK)
        hT = h_room[:].rearrange("p (n k c) -> p n k c", n=2, k=FK)
        dec = h_room[:, 0:3 * CUT].rearrange("p (n c) -> p n c", n=3)
        OB = h_room[:, 3 * CUT:3 * CUT + 2 * S]
        gb1 = sb("gb1", [P, E * FK])
        gz = sb("gz", [P, E, FK, E])
        G0 = sb("G0", [E, D])
        wsq = sb("wsq", [P, E])
        wsum = sb("wsum", [P, E])
        wn = sb("wn", [P, E])
        xsq = sb("xsq", [P, T])
        xnm = sb("xnm", [P, T])
        sqj = sb("sqj", [P, D])
        den = sb("den", [P, T, E])
        rden = sb("rden", [P, T, E])
        aff = sb("aff", [P, T, E])
        amax = sb("amax", [P, T])
        eq = sb("eq", [P, T, E])
        pri = sb("pri", [P, T, E])
        pm = sb("pm", [P, T])
        oh = sb("oh", [P, T, E])
        ohT = h_room[0:E, 0:T * P]
        affT = h_room[0:E, T * P:2 * T * P]
        ndT = sel_room[0:E, 0:T * P]
        asum = sb("asum", [P, 1])
        zc = sb("zc", [P, 1])
        sg = sb("sg", [P, 1])
        cap = sb("cap", [P, 1])
        cnt = sb("cnt", [P, 2, T])
        cj = scan_room[:, 3, 0:2 * S].rearrange("p (n s) -> p n s", n=2)
        rank1 = sb("rank1", [P, T])
        keep = sb("keep", [P, T])
        disp = sb("disp", [P, T, E])
        ndisp = sb("ndisp", [P, T, E])

        sums = scan_room[:, 2, :]
        total = sums[:, 0:E * T].rearrange("p (e t) -> p e t", e=E)
        running = sums[:, E * T:2 * E * T].rearrange("p (e t) -> p e t", e=E)
        size = sb("size", [P, E])
        over = sums[:, 2 * E * T:3 * E * T].rearrange("p (e t) -> p e t", e=E)
        tiles_of = sb("tiles_of", [P, E])
        tile_end = sb("tile_end", [P, E])
        shift = sb("shift", [P, E])
        place = sums[:, 3 * E * T:4 * E * T].rearrange("p (t e) -> p t e", t=T)
        row_of = sb("row_of", [P, T])
        unsent = sb("unsent", [P, T])
        to_row = sb("to_row", [P, T], I32)
        from_row = sb("from_row", [P, T], I32)
        passed = sums[:, 4 * E * T:4 * E * T + C_SLOTS * E].rearrange("p (n e) -> p n e", e=E)
        expert_f = sb("expert_f", [P, C_SLOTS])
        expert_of = sb("expert_of", [P, C_SLOTS], I32)
        w1_now = scan_room[:, 0, :].rearrange("p (n f) -> p n f", n=2)
        b1_now = scan_room[:, 1, 0:2 * FK].rearrange("p (n k) -> p n k", n=2)
        xg = score_room[:].rearrange("p (t d) -> p t d", d=P)
        xgT = XNT[0][:].rearrange("p (n c) -> p n c", n=C)
        yg = XNT[1][:].rearrange("p (n c) -> p n c", n=C)

        kv_tm = sb("kv_tm", [P, 2, 2, 2 * D])
        Qs = sb("Qs", [P, 2, 2 * NA, AD])
        q1 = sb("q1", [P, 2 * NA, AD])
        q2 = sb("q2", [P, 2 * NA, AD])
        mx3 = sb("mx3", [P, 2, NA, 3])
        mx = sb("mx", [P, 2, NA])
        mr = sb("mr", [P, 2, NA])
        mr2 = sb("mr2", [P, 2, NA])
        pT = score_room[:].rearrange("p (n c) -> p n c", n=2 * OG)
        orec = sb("orec", [P, 2, OG])
        Os = sb("Os", [P, 2, 2 * NA, AD])
        Otm = sb("Otm", [P, 2, 2, D])
        OT = sb("OT", [P, 2, 2 * P])
        w12 = scan_room[:, 0:4, :].rearrange("p a (n c) -> p (a n) c", n=2)
        w3 = ctxT[:].rearrange("p (e k d) -> p e k d", e=E, k=GH)
        f_m2 = sb("f_m2", [P, T])
        f_z = sb("f_z", [P, T])
        f_e = sb("f_e", [P, T])
        f_p = sb("f_p", [P, T])
        Ks = sb("Ks", [P, 2, 2 * NA, AD])
        r1 = sb("r1", [P, 2 * NA, AD])
        r2 = sb("r2", [P, 2 * NA, AD])
        KK = h_room[:, 0:2048].bitcast(BF16).rearrange("p (n i a s) -> p n i a s", n=2, i=2, s=SL)
        QQ = h_room[:, 2048:4096].bitcast(BF16).rearrange("p (n i a s) -> p n i a s", n=2, i=2, s=SL)
        KT = w_room[:].bitcast(BF16).rearrange("p (q s) -> p q s", s=S)
        QT = sel_room[:].bitcast(BF16).rearrange("p (v n q s) -> p v n q s", v=2, n=2, s=S)
        Va = v_room[:, 0:2 * NP * (AD + 1)].rearrange("p (n d) -> p n d", d=AD + 1)
        OV = sb("OV", [P, 2, S])
        zero_row = OV[:, 0, 0:P]

        ps = [es.enter_context(nc.psum_tensor(f"bank{i}", [P, 512], F32)) for i in range(8)]
        ps_b = [bank[:].bitcast(BF16) for bank in ps]

        kv_d = nc.dram_tensor("kv_rows", (2, B, 2, P, D), F32, kind="Internal").ap()
        q_d = nc.dram_tensor("q_rows", (T, P, D), F32, kind="Internal").ap()
        o_d = nc.dram_tensor("o_rows", (T, P, D), F32, kind="Internal").ap()

        xg_d = nc.dram_tensor("slot_rows", ((C_SLOTS + T) * P, D), F32, kind="Internal").ap()
        y_d = nc.dram_tensor("slot_outputs", ((C_SLOTS + 1) * P, D), F32, kind="Internal").ap()

        def problems(rows):
            return rows.rearrange("i p (g d) -> (i p g) d", d=AD).rearrange("(n p) d -> p n d", p=P)

        def col(name):
            a, w = COLS[name]
            return small[:, a:a + w]

        def cst(name):
            a, w = CONST[name]
            return const[:, a:a + w]

        ident = cst("ident")

        s_x = sem("s_x")
        s_small = sem("s_small")
        s_const = sem("s_const")
        s_wa = sem("s_wa")
        s_ctxT = sem("s_ctxT")
        s_ctx = sem("s_ctx")
        s_lw = sem("s_lw")
        s_aw = sem("s_aw")
        s_w1 = sem("s_w1")
        s_w2 = sem("s_w2")
        s_out = sem("s_out")
        dve_seq = sem("dve_seq")
        pool_seq = sem("pool_seq")
        act_seq = sem("act_seq")
        var_ready = sem("var_ready")
        rstd_ready = sem("rstd_ready")
        pow_asked = sem("pow_asked")
        pow_done = sem("pow_done")
        xn_ready = sem("xn_ready")
        xnt_turned = sem("xnt_turned")
        xnt_ready = sem("xnt_ready")
        a_proj = sem("a_proj")
        a_gate = sem("a_gate")
        a_drive = sem("a_drive")
        a_scan = sem("a_scan")
        a_out = sem("a_out")
        a_add = sem("a_add")
        a_bias = sem("a_bias")
        pool_const = sem("pool_const")
        b_gates = sem("b_gates")
        b_pad = sem("b_pad")
        b_exp = sem("b_exp")
        b_dve = sem("b_dve")
        b_turn = sem("b_turn")
        b_turned = sem("b_turned")
        b_sc = sem("b_sc")
        b_dec = sem("b_dec")
        b_ct = sem("b_ct")
        b_pv = sem("b_pv")
        b_ov = sem("b_ov")
        b_ot = sem("b_ot")
        b_num = sem("b_num")
        c_sq = sem("c_sq")
        c_gb = sem("c_gb")
        c_num = sem("c_num")
        c_wn = sem("c_wn")
        c_wsq = sem("c_wsq")
        c_sum = sem("c_sum")
        c_mean = sem("c_mean")
        c_z = sem("c_z")
        c_sig = sem("c_sig")
        c_oh = sem("c_oh")
        c_turn = sem("c_turn")
        c_turned = sem("c_turned")
        c_row = sem("c_row")
        c_cnt = sem("c_cnt")
        c_nd = sem("c_nd")
        c_g0 = sem("c_g0")
        c_g0c = sem("c_g0c")
        c_base = sem("c_base")
        c_badd = sem("c_badd")
        c_zero = sem("c_zero")
        c_totals = sem("c_totals")
        c_rows = sem("c_rows")
        c_expert = sem("c_expert")
        c_sent = sem("c_sent")
        c_load = [sem(f"c_load{g}") for g in range(C_GROUPS)]
        c_xt = sem("c_xt")
        c_xtc = sem("c_xtc")
        c_w = sem("c_w")
        c_h = sem("c_h")
        c_act = sem("c_act")
        c_y = sem("c_y")
        c_yc = sem("c_yc")
        c_stored = [sem(f"c_stored{g}") for g in range(C_GROUPS)]
        c_back = [sem(f"c_back{c}") for c in range(C)]
        c_acc = sem("c_acc")
        d_proj = sem("d_proj")
        d_act = sem("d_act")
        d_scan = sem("d_scan")
        d_turn = sem("d_turn")
        d_add = sem("d_add")

        e_fill = sem("e_fill")
        e_kv = sem("e_kv")
        e_kvc = sem("e_kvc")
        e_kvd = [sem(f"e_kvd{i}") for i in range(2)]
        e_ks = [sem(f"e_ks{i}") for i in range(2)]
        e_va = sem("e_va")
        e_kpart = sem("e_kpart")
        e_qpart = sem("e_qpart")
        e_kk = sem("e_kk")
        e_kt = sem("e_kt")
        e_ktc = sem("e_ktc")
        e_q = sem("e_q")
        e_qc = sem("e_qc")
        e_qd = [sem(f"e_qd{i}") for i in range(C)]
        e_qs = [sem(f"e_qs{i}") for i in range(2)]
        e_qq = sem("e_qq")
        e_mq = sem("e_mq")
        e_turn = sem("e_turn")
        e_turned = sem("e_turned")
        e_i = sem("e_i")
        e_max = sem("e_max")
        e_j = sem("e_j")
        e_p = sem("e_p")
        e_pv = sem("e_pv")
        e_ov = sem("e_ov")
        e_rec = sem("e_rec")
        e_read = sem("e_read")
        e_o = sem("e_o")
        e_od = [sem(f"e_od{i}") for i in range(2)]
        e_ot = [sem(f"e_ot{i}") for i in range(2)]
        e_y = sem("e_y")
        e_add = sem("e_add")
        s_w12 = sem("s_w12")
        s_w3 = sem("s_w3")
        f_sc = sem("f_sc")
        f_d = sem("f_d")
        f_ex = sem("f_ex")
        f_h = sem("f_h")
        f_silu = sem("f_silu")
        f_mul = sem("f_mul")
        f_y = sem("f_y")
        f_acc = sem("f_acc")

        LAG_J = NA + 4
        FIRST = -NA - 4
        LAST = NP + 2 * NA + 20

        def batch_at(step, offset):
            b, left = divmod(step - offset, NA)
            return b if left == 0 and 0 <= b < B else None

        def group_at(step, offset):
            g, left = divmod(step - offset, OG)
            return g if left == 0 and 0 <= g < NP // OG else None

        AT_LOAD, AT_SPLIT, AT_TURN, AT_MAX, AT_TURN2 = -NA - 4, -10, -6, NA, NA + 2
        AT_PV = LAG_J + OG
        AT_GROUP = AT_PV + 2
        AT_STORE, AT_OUT, AT_Y = LAG_J + NA + 3, LAG_J + NA + 11, LAG_J + NA + 13

        def split_parts(eng, part_done, count, src, left1, left2, hi, mid, lo):
            for ins in (lambda: eng.tensor_copy(hi, src),
                        lambda: eng.tensor_tensor(left1, src, hi, ALU.subtract),
                        lambda: eng.tensor_copy(mid, left1),
                        lambda: eng.tensor_tensor(left2, left1, mid, ALU.subtract),
                        lambda: eng.tensor_copy(lo, left2)):
                ins().then_inc(part_done, 1)
                count += 1
                eng.wait_ge(part_done, count)
            return count

        fills = []
        for step in range(FIRST, LAST):
            for kind, which, n in (("q", batch_at(step, AT_TURN), 2), ("q2", batch_at(step, AT_TURN2), 2),
                                   ("group", group_at(step, AT_GROUP), 1), ("out", batch_at(step, AT_OUT), 1),
                                   ("y", batch_at(step, AT_Y), 1)):
                if which is not None:
                    fills += [(kind, which, k) for k in range(n)]
        fill_of = {f: n for n, f in enumerate(fills)}
        by_dve = ("group", "y")

        def read_count(f):
            mine = fills[f][0] in by_dve
            return sum((kind in by_dve) == mine for kind, _, _ in fills[:f + 1])

        def wait_read(eng, f):
            eng.wait_ge(e_read if fills[f][0] in by_dve else e_turned, read_count(f))

        block = es.enter_context(nc.Block())

        @block.sync
        def _(sp):
            sp.dma_start(X[:], x.rearrange("(t p) d -> p t d", p=P)).then_inc(s_x, 16)
            sp.dma_start(const[:], const_in).then_inc(s_const, 16)
            sp.dma_start(wp[:], wp_in).then_inc(s_wa, 16)
            sp.dma_start(wu[:], wu_in).then_inc(s_wa, 16)
            sp.dma_start(wo[:], wo_in).then_inc(s_wa, 16)
            sp.dma_start(ctxT[:], ctxT_in).then_inc(s_ctxT, 16)
            for h in range(NH):
                sp.dma_start(vaug[:, :, h, 0:HD],
                             ctx_in.rearrange("(t p) (h d) -> p t h d", p=P, h=NH)[:, :, h, :]).then_inc(s_ctx, 16)
            sp.dma_start(w1, w1_in).then_inc(s_w1, 16)
            sp.dma_start(w2, w2_in).then_inc(s_w2, 16)
            sp.wait_ge(pool_const, 1)
            sp.dma_start(xg_d[0:C_SLOTS * P].rearrange("(t p) d -> p t d", p=P), zero_row.unsqueeze(1).to_broadcast([P, C_SLOTS, P])).then_inc(c_zero, 16)
            sp.dma_start(y_d[C_ZERO:C_ZERO + P], zero_row).then_inc(c_zero, 16)
            sp.dma_start(lw[:], lw_in).then_inc(s_lw, 16)
            def group_rows(g):
                return g * CT, min((g + 1) * CT, C_SLOTS)

            sp.wait_ge(c_sent, 16 * T)
            for g in range(C_GROUPS):
                t0, t1 = group_rows(g)
                sp.dma_start(xg[:, t0:t1, :], xg_d[t0 * P:t1 * P].rearrange("(t p) d -> p t d", p=P)).then_inc(c_load[g], 16)
            for g in range(C_GROUPS):
                t0, t1 = group_rows(g)
                sp.wait_ge(c_yc, g + 1)
                sp.dma_start(y_d[t0 * P:t1 * P].rearrange("(t p) d -> p t d", p=P),
                             yg[:, g % C, 0:(t1 - t0) * P].rearrange("p (t d) -> p t d", d=D)).then_inc(c_stored[g], 16)
            sp.dma_start(aw[:], aw_in).then_inc(s_aw, 16)
            for b in range(B):
                k = b % 2
                sp.wait_ge(e_kvc, b + 1)
                for n in range(2):
                    sp.dma_start(kv_d[n, b].rearrange("i p d -> p i d"), kv_tm[:, k, :, n * D:(n + 1) * D]).then_inc(e_kvd[k], 16)

            def load_keys(b):
                if b >= 2:
                    sp.wait_ge(e_kk, b - 1)
                sp.dma_start(Ks[:, b % 2], problems(kv_d[0, b])).then_inc(e_ks[b % 2], 16)

            for k in range(2):
                sp.wait_ge(e_kvd[k], 32 * B // 2)
            for b in range(2):
                load_keys(b)
            for b in range(B):
                sp.dma_start(Va[:, b * 2 * NA:(b + 1) * 2 * NA, 0:AD], problems(kv_d[1, b])).then_inc(e_va, 16)
            sp.wait_ge(d_add, C)
            sp.dma_start(w12, w12_in).then_inc(s_w12, 16)
            sp.dma_start(w3, w3_in).then_inc(s_w3, 16)
            for c in range(C):
                sp.wait_ge(e_qc, c + 1)
                sp.dma_start(q_d[c * CT:(c + 1) * CT].rearrange("t p d -> p t d"), XN[:, c * CT:(c + 1) * CT, :]).then_inc(e_qd[c], 16)
            for b in range(2, B):
                load_keys(b)
            for step in range(FIRST, LAST):
                b = batch_at(step, AT_LOAD)
                if b is not None:
                    sp.wait_ge(e_qd[b // BC], 16)
                    if b >= 2:
                        sp.wait_ge(e_qq, b - 1)
                    sp.dma_start(Qs[:, b % 2], problems(q_d[2 * b:2 * b + 2])).then_inc(e_qs[b % 2], 16)
            sp.wait_ge(f_acc, E * C)
            sp.dma_start(out.rearrange("(t p) d -> p t d", p=P), X[:]).then_inc(s_out, 16)
            sp.wait_ge(s_out, 16)

        @block.gpsimd
        def _(pool):
            pool.memset(ones[:], 1.0)
            pool.memset(power[:, 0:1], -0.5)
            pool.memset(power[:, 1:2], 0.5).then_inc(pool_seq, 1)
            pool.memset(zpad[:], 0.0)
            pool.memset(gz[:], 0.0)
            pool.memset(zero_row, 0.0)
            pool.memset(v_room[:, T * NH * (HD + 1):T * NH * (HD + 1) + HW], 0.0)
            pool.memset(vaug[:, :, :, HD:HD + 1], 1.0).then_inc(pool_const, 1)
            ln_count = [0]

            def rstd_of(c):
                ln_count[0] += 1
                pool.wait_ge(var_ready, ln_count[0])
                t0, t1 = c * CT, (c + 1) * CT
                pool.tensor_tensor(rstd[:, t0:t1], vareps[:, t0:t1], power[:, 0:1].to_broadcast([P, CT]), ALU.pow).then_inc(rstd_ready, 1)

            pool.wait_ge(pool_seq, 1)
            pool.wait_ge(s_small, 16)
            rstd_of(0)
            for c in range(C):
                if c + 1 < C:
                    rstd_of(c + 1)
                pool.wait_ge(xn_ready, c + 1)
                if c == 0:
                    pool.wait_ge(s_x, 16)
                ch = X[:, c * CT:(c + 1) * CT, :]
                pool.tensor_tensor(ch, ch, col("bo").unsqueeze(1).to_broadcast([P, CT, D]), ALU.add).then_inc(a_bias, 1)
            pool.wait_ge(s_const, 16)
            pool.wait_ge(s_small, 16)
            pool.wait_ge(a_bias, C)
            pool.tensor_copy(sel, cst("minus3")[0:3 * R, :].unsqueeze(2).to_broadcast([3 * R, R, P])).then_inc(pool_seq, 1)
            pool.wait_ge(pool_seq, 2)
            pool.tensor_tensor(gkv[:], col("gk"), col("gv"), ALU.add).then_inc(pool_seq, 1)
            pool.wait_ge(pool_seq, 3)
            for n, g in enumerate((col("gq"), gkv[:])):
                z = zpad[:, n, :].rearrange("p (b s) -> p b s", s=68)
                for k in range(2):
                    last = pool.tensor_copy(z[:, :, 32 * k:32 * k + 4],
                                            g[:, 4 * k:4 * k + 4].unsqueeze(1).to_broadcast([P, B, 4]))
            last.then_inc(b_pad, 1)
            for c in range(C):
                rstd_of(c)
            for b in range(B):
                pool.wait_ge(pow_asked, b + 1)
                pool.tensor_tensor(hv[:], hv2[:], power[:, 0:1].to_broadcast([P, 2 * NH]), ALU.pow).then_inc(pow_done, 1)
            for c in range(C):
                rstd_of(c)
            pool.wait_ge(c_wn, 1)
            pool.wait_ge(pow_asked, B + 1)
            pool.tensor_tensor(wn[:], wsum[:], power[:, 1:2].to_broadcast([P, E]), ALU.pow)
            pool.wait_ge(c_sq, T)
            pool.tensor_tensor(xnm[:], xsq[:], power[:, 1:2].to_broadcast([P, T]), ALU.pow).then_inc(pow_done, 1)
            pool.wait_ge(c_zero, 32)
            pool.wait_ge(c_rows, 1)
            for t in range(T):
                pool.indirect_dma_start(out=xg_d, out_offset=bass.IndirectOffsetOnAxis(ap=to_row[:, t:t + 1], axis=0),
                                        in_=XN[:, t, :], in_offset=None).then_inc(c_sent, 16)
            for g in range(C_GROUPS):
                pool.wait_ge(c_stored[g], 16)
            for t in range(T):
                pool.indirect_dma_start(out=XN[:, t, :], out_offset=None, in_=y_d,
                                        in_offset=bass.IndirectOffsetOnAxis(ap=from_row[:, t:t + 1], axis=0)).then_inc(c_back[t // CT], 16)
            for c in range(C):
                rstd_of(c)
            pool.wait_ge(c_y, C_SLOTS)
            for n in range(2):
                pool.memset(KK[:, n, :, :, 6 * AD:SL], 0.0)
                pool.memset(QQ[:, n, :, :, 6 * AD:SL], 0.0)
            pool.memset(v_room[:, 2 * NP * (AD + 1):], 0.0)
            pool.memset(Va[:, :, AD:AD + 1], 1.0).then_inc(e_fill, 1)
            pool.wait_ge(e_fill, 1)
            for n in range(2):
                last = pool.memset(KK[:, n, :, :, 6 * AD:6 * AD + 3], 1.0)
            last.then_inc(e_fill, 1)
            for c in range(C):
                rstd_of(c)
            parts = 0
            for b in range(B):
                pool.wait_ge(e_ks[b % 2], 16 * (b // 2 + 1))
                if b >= 2:
                    pool.wait_ge(e_kt, 2 * (b - 1))
                src = Ks[:, b % 2].rearrange("p (a i) d -> p i a d", i=2)
                va, vb = (v[:].rearrange("p (a i) d -> p i a d", i=2) for v in (r1, r2))
                slot = [KK[:, b % 2, :, :, AD * j:AD * (j + 1)] for j in range(6)]
                parts = split_parts(pool, e_kpart, parts, src, va, vb, slot[0], slot[2], slot[4])
                pool.tensor_copy(slot[1], slot[0])
                pool.tensor_copy(slot[3], slot[0])
                pool.tensor_copy(slot[5], slot[2]).then_inc(e_kk, 1)
            for step in range(FIRST, LAST):
                b = batch_at(step, AT_STORE)
                if b is not None:
                    pool.wait_ge(e_o, NA // OG * (b + 1))
                    pool.dma_start(problems(o_d[2 * b:2 * b + 2]), Os[:, b % 2]).then_inc(e_od[b % 2], 16)
                    pool.wait_ge(e_od[b % 2], 16 * (b // 2 + 1))
                    if b >= 2:
                        pool.wait_ge(e_turn, fill_of["out", b - 2, 0] + 1)
                    pool.dma_start(Otm[:, b % 2], o_d[2 * b:2 * b + 2].rearrange("i p d -> p i d")).then_inc(e_ot[b % 2], 16)
            for c in range(C):
                rstd_of(c)

        @block.scalar
        def _(act):
            act.dma_start(small[:], small_in).then_inc(s_small, 16)
            ln_count = [0]

            def copy_xnt(layer):
                def one(c):
                    n = ln_count[0]
                    act.wait_ge(xnt_turned, n + 1)
                    act.activation(XNT[layer % 2][:, c * CW:(c + 1) * CW], ps[n % 2][:], ACT.Copy).then_inc(xnt_ready, 1)
                    ln_count[0] += 1
                return one

            cp = copy_xnt(0)
            act.wait_ge(s_small, 16)
            for c in range(C):
                cp(c)
                act.wait_ge(a_proj, c + 1)
                if c >= 2:
                    act.wait_ge(a_drive, c - 1)
                act.activation(gate[:, c % 2, :], ps[2][:], ACT.Sigmoid, bias=col("bw"))
                act.activation(tnh[:, c % 2, :], ps[3][:], ACT.Tanh, bias=col("bk")).then_inc(a_gate, 1)

            cp = copy_xnt(1)
            for c in range(C):
                cp(c)
            act.wait_ge(b_dve, 1)
            act.activation(g_e[:], g_n[:], ACT.Exp).then_inc(act_seq, 1)
            act.wait_ge(act_seq, 1)
            act.activation(g_n[:], g_e[:], ACT.Ln, bias=1.0).then_inc(b_exp, 1)
            act.wait_ge(b_dve, 2)
            act.activation(g_e[:], g_m[:], ACT.Exp, scale=-1.0).then_inc(b_exp, 1)
            act.wait_ge(b_turn, 1)
            act.activation(bT[:], ps[2][:, 0:4 * R], ACT.Copy).then_inc(b_turned, 1)
            act.wait_ge(b_turned, 1)

            def copy_values(b):
                act.wait_ge(b_pv, b + 1)
                if b >= 1:
                    act.wait_ge(b_ot, b)
                act.activation(OB, ps[6][:], ACT.Copy).then_inc(b_ov, 1)

            for r in range(R):
                b, h = divmod(r, NH)
                act.wait_ge(b_sc, r + 1)
                if r >= 3:
                    act.wait_ge(b_ct, r - 2)
                if r % NH == 1 and r > NH:
                    copy_values(r // NH - 1)
                act.activation(dec[:, r % 3, 0:S], ps[2 + r % 2][:, 0:S], ACT.Exp, bias=bT[:, 0, 0, r:r + 1])
                act.activation(dec[:, r % 3, S:CUT], ps[2 + r % 2][:, S:CUT], ACT.Exp,
                               bias=bT[:, 0, 1, r:r + 1]).then_inc(b_dec, 1)
            copy_values(B - 1)

            act.wait_ge(pool_const, 1)
            for e in range(E):
                last = act.activation(gz[:, e, :, e], small[:, COLS["b1"][0] + FK * e:COLS["b1"][0] + FK * e + FK], ACT.Gelu)
            last.then_inc(c_gb, 1)
            cp = copy_xnt(2)
            for c in range(C):
                cp(c)
                for t in range(c * CT, (c + 1) * CT):
                    act.activation(sqj[:], XN[:, t, :], ACT.Square, accum_out=xsq[:, t:t + 1]).then_inc(c_sq, 1)
                    act.wait_ge(c_sq, t + 1)
            for c in range(C):
                act.wait_ge(c_turn, c + 1)
                act.activation(affT[:, c * CW:(c + 1) * CW], ps[2 + 2 * (c % 2)][0:E, :], ACT.Copy)
                act.activation(ohT[:, c * CW:(c + 1) * CW], ps[3 + 2 * (c % 2)][0:E, :], ACT.Copy).then_inc(c_turned, 1)
            act.wait_ge(c_z, 1)
            act.activation(sg[:], zc[:], ACT.Sigmoid).then_inc(c_sig, 1)
            for c in range(C):
                act.wait_ge(c_turn, C + c + 1)
                act.activation(ndT[:, c * CW:(c + 1) * CW], ps[2 + c % 2][0:E, :], ACT.Copy).then_inc(c_turned, 1)
            for n in range(C_SLOTS):
                if n % CT == 0:
                    g = n // CT
                    w = min(CT, C_SLOTS - n) * P
                    act.wait_ge(c_xt, g + 1)
                    if g >= C:
                        act.wait_ge(c_h, CT * (g - C + 1))
                    act.activation(xgT[:, g % C, 0:w], ps[g % 2][:, 0:w], ACT.Copy).then_inc(c_xtc, 1)
                if n >= 2:
                    act.wait_ge(c_y, n - 1)
                act.wait_ge(c_w, n + 1)
                act.wait_ge(c_h, n + 1)
                for k in range(FK):
                    last = act.activation(hS[:, n % 2, k, :], ps[2 + n % 2][:, k * P:(k + 1) * P], ACT.Gelu, bias=b1_now[:, n % 2, k:k + 1])
                last.then_inc(c_act, 1)

            cp = copy_xnt(3)
            for c in range(C):
                cp(c)
                act.wait_ge(d_proj, c + 1)
                if c >= 2:
                    act.wait_ge(d_scan, c - 1)
                act.activation(gate[:, c % 2, :], ps[2][:], ACT.Sigmoid, bias=col("bg"))
                act.activation(tnh[:, c % 2, :], ps[3][:], ACT.Tanh, bias=col("bv"))
                act.activation(state[:, c % 2, :], ps[4][:], ACT.Sigmoid, bias=col("bd")).then_inc(d_act, 1)

            for b in range(B):
                act.wait_ge(e_kv, b + 1)
                if b >= 2:
                    act.wait_ge(e_kvd[b % 2], 32 * (b // 2))
                act.activation(kv_tm[:, b % 2].rearrange("p i d -> p (i d)"), ps[6 + b % 2][:], ACT.Copy).then_inc(e_kvc, 1)
            cp = copy_xnt(4)
            for c in range(C):
                cp(c)
                act.wait_ge(e_q, c + 1)
                act.activation(XN[:, c * CT:(c + 1) * CT, :].rearrange("p t d -> p (t d)"), ps[2 + c % 2][:], ACT.Copy).then_inc(e_qc, 1)
            for n in range(2 * B):
                act.wait_ge(e_kt, n + 1)
                act.activation(KT[:, 4 * n:4 * n + 4, :].rearrange("p q s -> p (q s)"), ps_b[n % 2], ACT.Copy).then_inc(e_ktc, 1)

            def copy_turned(kind, b, dst):
                for k, d in enumerate(dst):
                    f = fill_of[kind, b, k]
                    act.wait_ge(e_turn, f + 1)
                    src = ps[f % 2][:, 0:2 * P] if kind == "out" else ps_b[f % 2]
                    act.activation(d, src, ACT.Copy).then_inc(e_turned, 1)

            for step in range(FIRST, LAST):
                b = batch_at(step, AT_TURN)
                if b is not None:
                    if b >= 2:
                        act.wait_ge(e_i, NA * (b - 1))
                    copy_turned("q", b, [QT[:, 0, b % 2, 4 * k:4 * k + 4, :].rearrange("p q s -> p (q s)") for k in range(2)])
                b = batch_at(step, AT_TURN2)
                if b is not None:
                    if b >= 2:
                        act.wait_ge(e_j, NA * (b - 1))
                    copy_turned("q2", b, [QT[:, 1, b % 2, 4 * k:4 * k + 4, :].rearrange("p q s -> p (q s)") for k in range(2)])
                b = batch_at(step, AT_OUT)
                if b is not None:
                    if b >= 2:
                        act.wait_ge(e_turn, fill_of["y", b - 2, 0] + 1)
                    copy_turned("out", b, [OT[:, b % 2, :]])
                g = group_at(step, AT_GROUP - 1)
                if g is not None:
                    act.wait_ge(e_pv, g + 1)
                    if g >= 2:
                        act.wait_ge(e_turn, fill_of["group", g - 2, 0] + 1)
                    act.activation(OV[:, g % 2, :], ps[6 + g % 2][:, 0:S], ACT.Copy).then_inc(e_ov, 1)
                n = step - LAG_J
                if 0 <= n < NP:
                    act.wait_ge(e_j, n + 1)
                    if n >= 2 * OG:
                        act.wait_ge(e_pv, n // OG - 1)
                    act.activation(pT[:, n % (2 * OG), :], ps[4 + n % 2][:, 0:CUT], ACT.Exp, scale=float(AD) ** -0.5).then_inc(e_p, 1)

            cp = copy_xnt(5)
            for c in range(C):
                cp(c)
            act.wait_ge(f_d, 1)
            act.activation(f_e[:], f_z[:], ACT.Exp).then_inc(f_ex, 1)
            for n in range(E * C):
                if n >= 2:
                    act.wait_ge(f_y, n - 1)
                for k in range(GH):
                    act.wait_ge(f_h, 2 * GH * n + k + 1)
                    act.activation(hT[:, n % 2, k, :], ps[2 + k][:], ACT.Silu).then_inc(f_silu, 1)

        @block.tensor
        def _(pe):
            ln_count = [0]

            def turn_xn(c):
                n = ln_count[0]
                pe.wait_ge(xn_ready, n + 1)
                if n >= 2:
                    pe.wait_ge(xnt_ready, n - 1)
                for i in range(CT):
                    last = pe.transpose(ps[n % 2][:, i * P:(i + 1) * P], XN[:, c * CT + i, :], ident)
                last.then_inc(xnt_turned, 1)
                ln_count[0] += 1

            pe.wait_ge(s_const, 16)
            xt = XNT[0]

            def a_project(c):
                pe.wait_ge(xnt_ready, c + 1)
                if c == 0:
                    pe.wait_ge(s_wa, 48)
                if c >= 1:
                    pe.wait_ge(a_gate, c)
                    pe.wait_ge(a_drive, c)
                mov = xt[:, c * CW:(c + 1) * CW]
                pe.matmul(ps[2][:], wp[:, 0:D], mov, start=True, stop=True)
                pe.matmul(ps[3][:], wp[:, D:2 * D], mov, start=True, stop=True)
                pe.matmul(ps[4][:], wu[:], mov, start=True, stop=True).then_inc(a_proj, 1)

            def a_output(c):
                pe.wait_ge(a_scan, c + 1)
                if c >= 1:
                    pe.wait_ge(a_add, c)
                for i in range(CT):
                    last = pe.matmul(ps[5][:, i * P:(i + 1) * P], state[:, c % 2, i * P:(i + 1) * P], wo[:], start=True, stop=True)
                last.then_inc(a_out, 1)

            for c in range(C + 1):
                if c < C:
                    turn_xn(c)
                    a_project(c)
                if c >= 1:
                    a_output(c - 1)

            xt = XNT[1]
            pe.wait_ge(b_pad, 1)
            pe.wait_ge(s_ctxT, 16)
            for b in range(B):
                pe.matmul(ps[6][0:2 * R, 0:S], zpad[:, 1, b * 64:b * 64 + 64], ctxT[:, b * S:(b + 1) * S], start=(b == 0), stop=False)
            for c in range(C):
                turn_xn(c)
            for b in range(B):
                pe.wait_ge(xnt_ready, C + b // BC + 1)
                last = pe.matmul(ps[6][0:2 * R, 0:S], zpad[:, 0, b * 64:b * 64 + 64], xt[:, b * S:(b + 1) * S], start=False, stop=(b == B - 1))
            last.then_inc(b_gates, 1)
            pe.wait_ge(b_dve, 2)
            pe.wait_ge(b_exp, 2)
            for n, src in enumerate((g_b, g_e)):
                for i in range(2):
                    at = (2 * n + i) * R
                    last = pe.transpose(ps[2][:, at:at + R], src[:, i * P:(i + 1) * P], ident[0:R, 0:R])
            last.then_inc(b_turn, 1)

            def b_scores(r):
                b, h = divmod(r, NH)
                row = slice(HD * h, HD * h + HD)
                i0 = b * S
                if r == 0:
                    pe.wait_ge(b_turned, 1)
                    pe.wait_ge(pool_seq, 3)
                    pe.wait_ge(b_dve, 3)
                if r >= 2:
                    pe.wait_ge(b_dec, r - 1)
                    pe.wait_ge(b_ct, r - 1)
                dk, sk = ps[2 + r % 2], ps[4 + r % 2]
                pe.matmul(dk[:, 0:S], sel[:, r, :], gp[:], start=True, stop=False)
                pe.matmul(dk[:, 0:P], ident_b[:], neg_ji_b[:], start=False, stop=True)
                pe.matmul(dk[:, S:CUT], sel[:, r, :], gp[:, P:S], start=True, stop=False)
                pe.matmul(dk[:, S:CUT], ident_b[:], neg_ji_b[:], start=False, stop=True)
                pe.matmul(sk[:, 0:S], ctxT[row, i0:i0 + P], xt[row, i0:i0 + S], start=True, stop=True)
                pe.matmul(sk[:, S:CUT], ctxT[row, i0 + P:i0 + S], xt[row, i0 + P:i0 + S], start=True, stop=True).then_inc(b_sc, 1)

            def b_values(b):
                pe.wait_ge(b_ct, NH * (b + 1))
                if b == 0:
                    pe.wait_ge(s_ctx, 16 * NH)
                    pe.wait_ge(pool_const, 1)
                else:
                    pe.wait_ge(b_ov, b)
                for q in range(2):
                    for i in range(2):
                        for f in range(2):
                            h = 2 * q + f
                            at = ((2 * b + i) * NH + h) * (HD + 1)
                            last = pe.matmul(ps[6][HW * f:HW * (f + 1), q * S + i * P:(q + 1) * S], v_room[:, at:at + HW],
                                             cT[:, (NH * b + h) % (2 * NH), i * S:CUT if i else S], start=(i == 0), stop=(i == 1))
                last.then_inc(b_pv, 1)

            def b_turn_values(b):
                pe.wait_ge(b_ov, b + 1)
                if b >= 1:
                    pe.wait_ge(b_num, 2 * b - 1)
                for n in range(4):
                    last = pe.transpose(ps[7][:, n * P:(n + 1) * P], OB[:, n * P:(n + 1) * P], ident)
                last.then_inc(b_ot, 1)

            for r in range(R):
                b_scores(r)
                if r % NH == 0 and r > 0:
                    b_values(r // NH - 1)
                if r % NH == 2 and r > NH:
                    b_turn_values(r // NH - 1)
            b_values(B - 1)
            b_turn_values(B - 1)

            xt = XNT[0]
            pe.wait_ge(c_wsq, 1)
            pe.matmul(ps[3][:, 0:E], ones[:], wsq[:], start=True, stop=True).then_inc(c_wn, 1)
            for c in range(C):
                turn_xn(c)
                pe.wait_ge(xnt_ready, 2 * C + c + 1)
                for t in range(c * CT, (c + 1) * CT):
                    last = pe.matmul(ps[2][:, t * E:(t + 1) * E], xt[:, t * P:(t + 1) * P], col("waffT"), start=True, stop=True)
            last.then_inc(c_num, 1)
            pe.wait_ge(c_gb, 1)
            pe.wait_ge(s_w2, 16)
            for e in range(E):
                for k in range(FK):
                    last = pe.matmul(ps[6][0:E, 0:D], gz[:, e, k, :], w2[:, e, k, :], start=(e == 0 and k == 0),
                                     stop=(e == E - 1 and k == FK - 1))
            last.then_inc(c_g0, 1)
            pe.wait_ge(c_sum, 1)
            pe.matmul(ps[7][:, 0:1], ones[:], asum[:], start=True, stop=True).then_inc(c_mean, 1)
            pe.wait_ge(c_oh, 1)
            for c in range(C):
                if c >= 2:
                    pe.wait_ge(c_turned, c - 1)
                for src, bank in ((aff, 2 + 2 * (c % 2)), (oh, 3 + 2 * (c % 2))):
                    for i in range(CT):
                        last = pe.transpose(ps[bank][0:E, i * P:(i + 1) * P], src[:, c * CT + i, :], ident)
                last.then_inc(c_turn, 1)
            for t in range(T):
                if t == 0:
                    pe.wait_ge(c_turned, C)
                if t >= 2:
                    pe.wait_ge(c_cnt, t - 1)
                q0 = (t // 2) * S
                pe.matmul(ps[4 + t % 2][:, 0:S], ohT[:, t * P:(t + 1) * P], affT[:, q0:q0 + S], start=True, stop=True).then_inc(c_row, 1)
            pe.wait_ge(c_nd, 1)
            sent = disp[:].rearrange("p t e -> p (t e)")
            pe.matmul(ps[4][:, 0:T * E], cst("earlier"), sent, start=True, stop=True)
            pe.matmul(ps[5][:, 0:T * E], ones[:], sent, start=True, stop=True).then_inc(c_totals, 1)
            for c in range(C):
                if c >= 2:
                    pe.wait_ge(c_turned, C + c - 1)
                for i in range(CT):
                    last = pe.transpose(ps[2 + c % 2][0:E, i * P:(i + 1) * P], ndisp[:, c * CT + i, :], ident)
                last.then_inc(c_turn, 1)
            pe.wait_ge(c_g0c, 1)
            for c in range(C):
                pe.wait_ge(c_turned, C + c + 1)
                if c >= 2:
                    pe.wait_ge(c_badd, c - 1)
                for i in range(CT):
                    o = ps[6 + c % 2][:, i * P:(i + 1) * P]
                    t = c * CT + i
                    pe.matmul(o, ndT[:, t * P:(t + 1) * P], G0[:], start=True, stop=False)
                    last = pe.matmul(o, ones[0:E, :], col("b2")[0:E, :], start=False, stop=True)
                last.then_inc(c_base, 1)

            def c_turn_group(g):
                pe.wait_ge(c_load[g], 16)
                if g >= 2:
                    pe.wait_ge(c_xtc, g - 1)
                for t in range(g * CT, min((g + 1) * CT, C_SLOTS)):
                    last = pe.transpose(ps[g % 2][:, (t % CT) * P:(t % CT + 1) * P], xg[:, t, :], ident)
                last.then_inc(c_xt, 1)

            def c_hidden(n):
                pe.wait_ge(c_xtc, n // CT + 1)
                pe.wait_ge(c_w, n + 1)
                if n >= 2:
                    pe.wait_ge(c_act, n - 1)
                for k in range(FK):
                    last = pe.matmul(ps[2 + n % 2][:, k * P:(k + 1) * P], w1_now[:, n % 2, k * P:(k + 1) * P],
                                     xgT[:, (n // CT) % C, (n % CT) * P:(n % CT + 1) * P], start=True, stop=True)
                last.then_inc(c_h, 1)

            def c_down(n):
                g, i = divmod(n, CT)
                e = pe.value_load(expert_of[0:1, n:n + 1], min_val=0, max_val=E - 1)
                pe.wait_ge(c_act, n + 1)
                if i == 0 and g >= 2:
                    pe.wait_ge(c_yc, g - 1)
                for k in range(FK):
                    last = pe.matmul(ps[6 + g % 2][:, i * P:(i + 1) * P], hS[:, n % 2, k, :], w2[:, bass.ds(e, 1), k, :],
                                     start=(k == 0), stop=(k == FK - 1))
                last.then_inc(c_y, 1)

            pe.wait_ge(c_badd, C)
            pe.wait_ge(c_expert, 1)
            c_turn_group(0)
            for n in range(C_SLOTS + 1):
                if n < C_SLOTS:
                    c_hidden(n)
                    if n % CT == 0 and n // CT + 1 < C_GROUPS:
                        c_turn_group(n // CT + 1)
                if n >= 1:
                    c_down(n - 1)

            xt = XNT[1]
            pe.wait_ge(s_lw, 16)

            def d_project(c):
                pe.wait_ge(xnt_ready, 3 * C + c + 1)
                if c >= 1:
                    pe.wait_ge(d_act, c)
                mov = xt[:, c * CW:(c + 1) * CW]
                for k in range(3):
                    last = pe.matmul(ps[2 + k][:], lw[:, k * D:(k + 1) * D], mov, start=True, stop=True)
                last.then_inc(d_proj, 1)

            def d_output(c):
                pe.wait_ge(d_scan, c + 1)
                if c >= 1:
                    pe.wait_ge(d_add, c)
                for i in range(CT):
                    last = pe.transpose(ps[5][:, i * P:(i + 1) * P], drive[:, c % 2, i * P:(i + 1) * P], ident)
                last.then_inc(d_turn, 1)

            for c in range(C + 1):
                if c < C:
                    turn_xn(c)
                    d_project(c)
                if c >= 1:
                    d_output(c - 1)

            xt = XNT[0]
            pe.wait_ge(s_aw, 16)
            pe.wait_ge(c_yc, C_GROUPS)
            for b in range(B):
                if b >= 2:
                    pe.wait_ge(e_kvc, b - 1)
                for i in range(2):
                    t = 2 * b + i
                    last = pe.matmul(ps[6 + b % 2][:, i * 2 * D:(i + 1) * 2 * D], ctxT[:, t * P:(t + 1) * P], aw[:, D:3 * D], start=True, stop=True)
                last.then_inc(e_kv, 1)
            for c in range(C):
                turn_xn(c)
                pe.wait_ge(xnt_ready, 4 * C + c + 1)
                if c >= 2:
                    pe.wait_ge(e_qc, c - 1)
                for i in range(CT):
                    t = c * CT + i
                    last = pe.matmul(ps[2 + c % 2][:, i * P:(i + 1) * P], xt[:, t * P:(t + 1) * P], aw[:, 0:D], start=True, stop=True)
                last.then_inc(e_q, 1)
            pe.wait_ge(xnt_ready, 5 * C)
            for b in range(B):
                pe.wait_ge(e_kk, b + 1)
                for k in range(2):
                    n = 2 * b + k
                    if n >= 2:
                        pe.wait_ge(e_ktc, n - 1)
                    for q in range(4):
                        for i in range(2):
                            last = pe.transpose(ps_b[n % 2][:, (2 * q + i) * P:(2 * q + i + 1) * P],
                                                KK[:, b % 2, i, 8 * k + 2 * q:8 * k + 2 * q + 2, :].rearrange("p a s -> p (a s)"), ident_b[:])
                    last.then_inc(e_kt, 1)
            pe.wait_ge(e_ktc, 2 * B)
            pe.wait_ge(e_qc, C)
            pe.wait_ge(e_kvc, B)
            pe.wait_ge(e_va, 16 * B)

            def next_fill(kind, which, k):
                f = fill_of[kind, which, k]
                if f >= 2:
                    wait_read(pe, f - 2)
                return f

            def turn_queries(kind, b):
                for k in range(2):
                    f = next_fill(kind, b, k)
                    for q in range(4):
                        for i in range(2):
                            last = pe.transpose(ps_b[f % 2][:, (2 * q + i) * P:(2 * q + i + 1) * P],
                                                QQ[:, b % 2, i, 8 * k + 2 * q:8 * k + 2 * q + 2, :].rearrange("p a s -> p (a s)"), ident_b[:])
                    last.then_inc(e_turn, 1)

            for step in range(FIRST, LAST):
                b = batch_at(step, AT_TURN)
                if b is not None:
                    pe.wait_ge(e_qq, b + 1)
                    turn_queries("q", b)
                b = batch_at(step, AT_TURN2)
                if b is not None:
                    pe.wait_ge(e_mq, b + 1)
                    turn_queries("q2", b)
                n = step
                if 0 <= n < NP:
                    b, a = divmod(n, NA)
                    rows = slice(SL * (a % 2), SL * (a % 2) + 6 * AD)
                    qt, kt = QT[rows, 0, b % 2, a // 2, :], KT[rows, n // 2, :]
                    if a % 8 == 0:
                        wait_read(pe, fill_of["q", b, a // 8])
                    if n >= 2:
                        pe.wait_ge(e_max, n - 1)
                    o = ps[2 + n % 2]
                    pe.matmul(o[:, 0:P], qt[:, 0:P], kt[:, 0:P], start=True, stop=False)
                    pe.matmul(o[:, 0:P], ident_b[:], neg_ij_b[:], start=False, stop=True)
                    pe.matmul(o[:, P:CUT], qt[:, P:S], kt[:, 0:S], start=True, stop=False)
                    pe.matmul(o[:, S:CUT], ident_b[:], neg_ij_b[:], start=False, stop=True).then_inc(e_i, 1)
                n = step - LAG_J
                if 0 <= n < NP:
                    b, a = divmod(n, NA)
                    rows = slice(SL * (a % 2), SL * (a % 2) + 6 * AD + 3)
                    qt, kt = QT[rows, 1, b % 2, a // 2, :], KT[rows, n // 2, :]
                    if a % 8 == 0:
                        wait_read(pe, fill_of["q2", b, a // 8])
                    if n >= 2:
                        pe.wait_ge(e_p, n - 1)
                    o = ps[4 + n % 2]
                    pe.matmul(o[:, 0:S], kt[:, 0:P], qt[:, 0:S], start=True, stop=False)
                    pe.matmul(o[:, 0:P], ident_b[:], neg_ji_b[:], start=False, stop=True)
                    pe.matmul(o[:, S:CUT], kt[:, P:S], qt[:, P:S], start=True, stop=False)
                    pe.matmul(o[:, S:CUT], ident_b[:], neg_ji_b[:], start=False, stop=True).then_inc(e_j, 1)
                g = group_at(step, AT_PV)
                if g is not None:
                    pe.wait_ge(e_p, OG * (g + 1))
                    if g >= 2:
                        pe.wait_ge(e_ov, g - 1)
                    for i in range(2):
                        for j in range(OG):
                            n = g * OG + j
                            o = ps[6 + g % 2][OW * j:OW * (j + 1), i * P:S]
                            v = v_room[:, (2 * n + i) * (AD + 1):(2 * n + i) * (AD + 1) + OW]
                            last = pe.matmul(o, v, pT[:, n % (2 * OG), i * S:CUT if i else S], start=(i == 0), stop=(i == 1))
                    last.then_inc(e_pv, 1)
                g = group_at(step, AT_GROUP)
                if g is not None:
                    f = next_fill("group", g, 0)
                    pe.wait_ge(e_ov, g + 1)
                    for i in range(2):
                        last = pe.transpose(ps[f % 2][:, i * P:(i + 1) * P], OV[:, g % 2, i * P:(i + 1) * P], ident)
                    last.then_inc(e_turn, 1)
                b = batch_at(step, AT_OUT)
                if b is not None:
                    f = next_fill("out", b, 0)
                    pe.wait_ge(e_ot[b % 2], 16 * (b // 2 + 1))
                    for i in range(2):
                        last = pe.transpose(ps[f % 2][:, i * P:(i + 1) * P], Otm[:, b % 2, i, :], ident)
                    last.then_inc(e_turn, 1)
                b = batch_at(step, AT_Y)
                if b is not None:
                    f = next_fill("y", b, 0)
                    wait_read(pe, fill_of["out", b, 0])
                    for i in range(2):
                        last = pe.matmul(ps[f % 2][:, i * P:(i + 1) * P], OT[:, b % 2, i * P:(i + 1) * P], aw[:, 3 * D:4 * D], start=True, stop=True)
                    last.then_inc(e_turn, 1)

            xt = XNT[1]
            wait_read(pe, len(fills) - 1)
            wait_read(pe, fill_of["out", B - 1, 0])
            for c in range(C):
                turn_xn(c)
                pe.wait_ge(xnt_ready, 5 * C + c + 1)
                if c == 0:
                    pe.wait_ge(e_max, NP)
                    pe.wait_ge(e_p, NP)
                for t in range(c * CT, (c + 1) * CT):
                    last = pe.matmul(ps[2][:, t * E:(t + 1) * E], xt[:, t * P:(t + 1) * P], col("gateT"), start=True, stop=True)
            last.then_inc(f_sc, 1)
            pe.wait_ge(s_w12, 16)
            pe.wait_ge(s_w3, 16)
            pe.wait_ge(f_d, 1)
            pe.wait_ge(e_add, B)

            def f_hidden(n):
                e, c = divmod(n, C)
                for k in range(2 * GH):
                    if n >= 1:
                        if k < GH:
                            pe.wait_ge(f_silu, GH * (n - 1) + k + 1)
                        else:
                            pe.wait_ge(f_mul, GH * (n - 1) + k - GH + 1)
                    pe.matmul(ps[2 + k][:], w12[:, e, k * P:(k + 1) * P], xt[:, c * CW:(c + 1) * CW], start=True, stop=True).then_inc(f_h, 1)

            def f_down(n):
                e, c = divmod(n, C)
                pe.wait_ge(f_mul, GH * (n + 1))
                if n >= 2:
                    pe.wait_ge(f_acc, n - 1)
                for i in range(CT):
                    for k in range(GH):
                        last = pe.matmul(ps[6 + n % 2][:, i * P:(i + 1) * P], hT[:, n % 2, 2 + k, i * P:(i + 1) * P], w3[:, e, k, :],
                                         start=(k == 0), stop=(k == GH - 1))
                last.then_inc(f_y, 1)

            for n in range(E * C + 1):
                if n < E * C:
                    f_hidden(n)
                if n >= 1:
                    f_down(n - 1)

        @block.vector
        def _(dve):
            chain = [0]
            ln_count = [0]

            def link(ins):
                chain[0] += 1
                ins.then_inc(dve_seq, 1)
                dve.wait_ge(dve_seq, chain[0])

            def layer_norm(c):
                t0, t1 = c * CT, (c + 1) * CT
                for t in range(t0, t1):
                    last = dve.bn_stats(stats[:, t, :], X[:, t, :])
                link(last)
                for t in range(t0, t1):
                    last = dve.bn_aggr(mv[:, t, :], stats[:, t, :])
                link(last)
                dve.tensor_scalar(vareps[:, t0:t1], mv[:, t0:t1, 1], LN_EPS, None, ALU.add).then_inc(var_ready, 1)
                ln_count[0] += 1
                dve.wait_ge(rstd_ready, ln_count[0])
                for t in range(t0, t1):
                    last = dve.tensor_scalar(XN[:, t, :], X[:, t, :], mv[:, t, 0:1], rstd[:, t:t + 1], ALU.subtract, ALU.mult)
                last.then_inc(xn_ready, 1)

            dve.wait_ge(s_x, 16)

            def a_scan_chunk(c):
                k = c % 2
                dve.wait_ge(s_small, 16)
                dve.wait_ge(a_gate, c + 1)
                if c >= 2:
                    dve.wait_ge(a_out, c - 1)
                dve.scalar_tensor_tensor(out=drive[:, k, :], in0=ps[4][:], scalar=col("bu"), in1=gate[:, k, :], op0=ALU.add, op1=ALU.mult)
                link(dve.scalar_tensor_tensor(out=decay[:, k, :], in0=tnh[:, k, :], scalar=-1.0, in1=gate[:, k, :], op0=ALU.add, op1=ALU.mult))
                link(dve.tensor_scalar(decay[:, k, :], decay[:, k, :], 1.0, None, ALU.add))
                for b in range(BC):
                    sl = slice(b * S, (b + 1) * S)
                    last = dve.tensor_tensor_scan(state[:, k, sl], decay[:, k, sl], drive[:, k, sl], 0.0, ALU.mult, ALU.add)
                    if b == 0:
                        last.then_inc(a_drive, 1)
                last.then_inc(a_scan, 1)

            def a_residual(c):
                dve.wait_ge(a_out, c + 1)
                dve.wait_ge(a_bias, c + 1)
                ch = X[:, c * CT:(c + 1) * CT, :]
                ins = dve.tensor_tensor(ch, ps[5][:].rearrange("p (t d) -> p t d", d=D), ch, ALU.add)
                ins.then_inc(a_add, 1)

            layer_norm(0)
            for c in range(C):
                if c + 1 < C:
                    layer_norm(c + 1)
                if c == 0:
                    dve.wait_ge(s_const, 16)
                    dve.tensor_copy(ident_b[:], ident)
                    dve.tensor_copy(neg_ji_b[:], cst("neg_ji"))
                    dve.tensor_copy(neg_ij_b[:], cst("neg_ij"))
                a_scan_chunk(c)
                if c >= 1:
                    a_residual(c - 1)
            a_residual(C - 1)

            for c in range(C):
                dve.wait_ge(a_add, c + 1)
                layer_norm(c)
            dve.tensor_scalar(rms1[:], col("rms"), 1.0, None, ALU.add)
            dve.wait_ge(b_gates, 1)
            gb = col("gbias")
            dve.tensor_scalar(g_i[:], ps[6][0:R, 0:S], gb[0:R, :], None, ALU.add)
            link(dve.tensor_scalar(g_f[:], ps[6][R:2 * R, 0:S], gb[R:2 * R, :], None, ALU.add))
            dve.tensor_scalar(g_l[:], g_f[:], 0.0, None, ALU.min)
            dve.scalar_tensor_tensor(out=g_n[:], in0=g_f[:], scalar=-1.0, in1=g_f[:], op0=ALU.mult, op1=ALU.min).then_inc(b_dve, 1)
            dve.wait_ge(b_dve, 1)
            dve.wait_ge(b_exp, 1)
            link(dve.tensor_tensor(g_l[:], g_l[:], g_n[:], ALU.subtract))
            dve.wait_ge(pool_const, 1)
            link(dve.tensor_tensor_scan(g_cs[:], ones[0:R, 0:1].to_broadcast([R, S]), g_l[:], 0.0, ALU.mult, ALU.add))
            link(dve.tensor_tensor(g_b[:], g_i[:], g_cs[:], ALU.subtract))
            link(dve.tensor_tensor_scan(g_g[:], g_b[:], g_b[:], -3.0e38, ALU.max, ALU.max))
            dve.tensor_tensor(g_m[:], g_cs[:], g_g[:], ALU.add).then_inc(b_dve, 1)
            link(dve.tensor_copy(gp[0:R, :], g_g[:]))
            link(dve.tensor_tensor(g_l[:], g_g[:], gp[0:R, :], ALU.subtract))
            link(dve.tensor_copy(g_part[:], g_l[:]))
            dve.tensor_copy(gp[R:2 * R, :], g_part[:])
            link(dve.tensor_tensor(g_f[:], g_l[:], g_part[:], ALU.subtract))
            dve.tensor_copy(gp[2 * R:3 * R, :], g_f[:]).then_inc(b_dve, 1)

            def b_norm(b):
                o = ps[7][:].rearrange("p (n d) -> p n d", d=HW)
                dve.wait_ge(b_ot, b + 1)
                em = bT[:, 1, :, NH * b:NH * b + NH].rearrange("p i (q f) -> p q i f", q=2)
                link(dve.tensor_tensor(hn[:].rearrange("p (q i f) -> p q i f", q=2, i=2),
                                       o[:, :, HD].rearrange("p (q i f) -> p q i f", q=2, i=2), em, ALU.max))
                link(dve.tensor_scalar(hn[:], hn[:], 1e-6, None, ALU.add))
                link(dve.reciprocal(hr[:], hn[:]))
                dve.tensor_tensor(hh[:], o[:, :, 0:HD], hr[:].unsqueeze(2).to_broadcast([P, 2 * NH, HD]), ALU.mult).then_inc(b_num, 1)
                dve.wait_ge(b_num, 2 * b + 1)
                link(dve.tensor_tensor(hq[:], hh[:], hh[:], ALU.mult))
                link(dve.tensor_reduce(hv[:], hq[:], AX.X, ALU.add))
                dve.tensor_scalar(hv2[:], hv[:], 1.0 / HD, 1e-6, ALU.mult, ALU.add).then_inc(pow_asked, 1)
                dve.wait_ge(pow_done, b + 1)
                link(dve.tensor_tensor(hq[:], hh[:], hv[:].unsqueeze(2).to_broadcast([P, 2 * NH, HD]), ALU.mult))
                link(dve.tensor_tensor(hh[:], hq[:], rms1[:].unsqueeze(1).to_broadcast([P, 2 * NH, HD]), ALU.mult))
                xx = X[:, 2 * b:2 * b + 2, :].rearrange("p i (q w) -> p q i w", q=2)
                dve.tensor_tensor(xx, xx, hh[:].rearrange("p (q i f) d -> p q i (f d)", q=2, i=2), ALU.add).then_inc(b_num, 1)

            for r in range(R):
                b, h = divmod(r, NH)
                dve.wait_ge(b_dec, r + 1)
                if r >= 2 * NH:
                    dve.wait_ge(b_pv, b - 1)
                dve.scalar_tensor_tensor(out=cT[:, r % (2 * NH), :], in0=ps[4 + r % 2][:, 0:CUT], scalar=float(HD) ** -0.5,
                                         in1=dec[:, r % 3, :], op0=ALU.mult, op1=ALU.mult).then_inc(b_ct, 1)
                if h == 2 and b >= 1:
                    b_norm(b - 1)
            b_norm(B - 1)

            dve.tensor_tensor(wsq[:], col("waffT"), col("waffT"), ALU.mult).then_inc(c_wsq, 1)
            for c in range(C):
                dve.wait_ge(b_num, 2 * BC * (c + 1))
                layer_norm(c)
            dve.wait_ge(c_wn, 1)
            dve.tensor_copy(wsum[:], ps[3][:, 0:E]).then_inc(pow_asked, 1)
            dve.wait_ge(pow_done, B + 1)
            link(dve.tensor_tensor(den[:], xnm[:].unsqueeze(2).to_broadcast([P, T, E]),
                                   wn[:].unsqueeze(1).to_broadcast([P, T, E]), ALU.mult))
            link(dve.tensor_scalar(den[:], den[:], 1e-9, None, ALU.add))
            link(dve.reciprocal(rden[:], den[:]))
            dve.wait_ge(c_num, 1)
            link(dve.tensor_tensor(aff[:], ps[2][:, 0:T * E].rearrange("p (t e) -> p t e", e=E), rden[:], ALU.mult))
            dve.tensor_reduce(asum[:], aff[:], AX.XY, ALU.add).then_inc(c_sum, 1)
            link(dve.tensor_reduce(amax[:], aff[:], AX.X, ALU.max))

            def first_max(dst, scores, best):
                link(dve.tensor_tensor(eq[:], scores, best[:].unsqueeze(2).to_broadcast([P, T, E]), ALU.is_equal))
                link(dve.tensor_tensor(pri[:], eq[:], col("prio").unsqueeze(1).to_broadcast([P, T, E]), ALU.mult))
                link(dve.tensor_reduce(pm[:], pri[:], AX.X, ALU.max))
                return dve.tensor_tensor(dst[:], pri[:], pm[:].unsqueeze(2).to_broadcast([P, T, E]), ALU.is_equal)

            first_max(oh, aff[:], amax).then_inc(c_oh, 1)
            dve.wait_ge(c_mean, 1)
            dve.scalar_tensor_tensor(out=zc[:], in0=ps[7][:, 0:1], scalar=1.0 / (T * P * E), in1=col("thr"),
                                     op0=ALU.mult, op1=ALU.subtract).then_inc(c_z, 1)
            dve.wait_ge(c_g0, 1)
            dve.tensor_copy(G0[:], ps[6][0:E, 0:D]).then_inc(c_g0c, 1)
            dve.wait_ge(c_sig, 1)
            link(dve.tensor_scalar(cap[:], sg[:], float(S), 4.0, ALU.mult, ALU.max))
            link(dve.tensor_scalar(cap[:], cap[:], float(S), None, ALU.min))
            for t in range(T):
                dve.wait_ge(c_row, t + 1)
                m = (t % 2) * S
                row = ps[4 + t % 2][:, 0:S]
                if t >= 1:
                    dve.wait_ge(c_cnt, t)
                own = amax[:, t:t + 1]
                dve.scalar_tensor_tensor(out=cj[:, 0, :], in0=row, scalar=own, in1=cst("before")[:, m:m + S],
                                         op0=ALU.is_ge, op1=ALU.mult, accum_out=cnt[:, 0, t:t + 1])
                dve.scalar_tensor_tensor(out=cj[:, 1, :], in0=row, scalar=own, in1=cst("after")[:, m:m + S],
                                         op0=ALU.is_gt, op1=ALU.mult, accum_out=cnt[:, 1, t:t + 1]).then_inc(c_cnt, 1)
            dve.wait_ge(c_cnt, T)
            link(dve.scalar_tensor_tensor(out=rank1[:], in0=cnt[:, 0, :], scalar=1.0, in1=cnt[:, 1, :], op0=ALU.add, op1=ALU.add))
            link(dve.tensor_scalar(keep[:], rank1[:], cap[:], None, ALU.is_le))
            link(dve.tensor_tensor(disp[:], oh[:], keep[:].unsqueeze(2).to_broadcast([P, T, E]), ALU.mult))
            dve.tensor_scalar(ndisp[:], disp[:], -1.0, 1.0, ALU.mult, ALU.add).then_inc(c_nd, 1)
            dve.wait_ge(c_totals, 1)
            link(dve.tensor_copy(total, ps[5][:, 0:T * E].rearrange("p (t e) -> p e t", e=E)))
            link(dve.tensor_tensor_scan(running.rearrange("p e t -> p (e t)"), ones[:, 0:E * T], total.rearrange("p e t -> p (e t)"),
                                        0.0, ALU.mult, ALU.add))
            link(dve.tensor_tensor(running, running, total, ALU.subtract))
            link(dve.tensor_reduce(size[:], total, AX.X, ALU.add))
            link(dve.tensor_tensor(over, size[:].unsqueeze(2).to_broadcast([P, E, T]),
                                   cst("tile_sizes").unsqueeze(1).to_broadcast([P, E, T]), ALU.is_gt))
            link(dve.tensor_reduce(tiles_of[:], over, AX.X, ALU.add))
            link(dve.tensor_tensor_scan(tile_end[:], ones[:, 0:E], tiles_of[:], 0.0, ALU.mult, ALU.add))
            link(dve.tensor_tensor(shift[:], tile_end[:], tiles_of[:], ALU.subtract))
            link(dve.scalar_tensor_tensor(out=shift[:], in0=shift[:], scalar=float(P), in1=running[:, :, 0], op0=ALU.mult, op1=ALU.subtract))
            link(dve.tensor_tensor(place, ps[4][:, 0:T * E].rearrange("p (t e) -> p t e", e=E),
                                   running.rearrange("p e t -> p t e"), ALU.add))
            link(dve.tensor_tensor(place, place, shift[:].unsqueeze(1).to_broadcast([P, T, E]), ALU.add))
            link(dve.tensor_tensor(place, place, disp[:], ALU.mult))
            dve.tensor_scalar(unsent[:], keep[:], -1.0, 1.0, ALU.mult, ALU.add)
            link(dve.tensor_reduce(row_of[:], place, AX.X, ALU.add))
            link(dve.tensor_tensor(unsent[:], unsent[:], cst("spare"), ALU.mult))
            link(dve.tensor_tensor(row_of[:], row_of[:], unsent[:], ALU.add))
            dve.tensor_scalar(unsent[:], row_of[:], float(C_ZERO), None, ALU.min)
            dve.tensor_copy(to_row[:], row_of[:]).then_inc(c_rows, 1)
            link(dve.tensor_tensor(passed, tile_end[:].unsqueeze(1).to_broadcast([P, C_SLOTS, E]),
                                   cst("slot").unsqueeze(2).to_broadcast([P, C_SLOTS, E]), ALU.is_le))
            dve.tensor_copy(from_row[:], unsent[:])
            link(dve.tensor_reduce(expert_f[:], passed, AX.X, ALU.add))
            link(dve.tensor_scalar(expert_f[:], expert_f[:], float(E - 1), None, ALU.min))
            dve.tensor_copy(expert_of[:], expert_f[:]).then_inc(c_expert, 1)
            dve.wait_ge(c_expert, 1)

            def c_weights(n):
                e = dve.value_load(expert_of[0:1, n:n + 1], min_val=0, max_val=E - 1)
                if n == 0:
                    dve.wait_ge(s_w1, 16)
                if n >= 2:
                    dve.wait_ge(c_act, n - 1)
                dve.tensor_copy(w1_now[:, n % 2, :], w1[:, bass.ds(e, 1), :].rearrange("p a f -> p (a f)"))
                b1 = col("b1").rearrange("p (e k) -> p e k", e=E)
                dve.tensor_copy(b1_now[:, n % 2, :], b1[:, bass.ds(e, 1), :].rearrange("p a k -> p (a k)")).then_inc(c_w, 1)

            for n in range(2):
                c_weights(n)
            for c in range(C):
                dve.wait_ge(c_base, c + 1)
                ch = X[:, c * CT:(c + 1) * CT, :]
                dve.tensor_tensor(ch, ps[6 + c % 2][:].rearrange("p (t d) -> p t d", d=D), ch, ALU.add).then_inc(c_badd, 1)
            for n in range(2, C_SLOTS + 2):
                if n < C_SLOTS:
                    c_weights(n)
                done = n - 1
                if done % CT == 0 or done == C_SLOTS:
                    g = (done - 1) // CT
                    w = (done - g * CT) * P
                    dve.wait_ge(c_y, done)
                    if g >= C:
                        dve.wait_ge(c_stored[g - C], 16)
                    dve.tensor_copy(yg[:, g % C, 0:w], ps[6 + g % 2][:, 0:w]).then_inc(c_yc, 1)

            def c_residual(c):
                dve.wait_ge(c_back[c], 16 * CT)
                if c == 0:
                    dve.wait_ge(c_badd, C)
                ch = X[:, c * CT:(c + 1) * CT, :]
                dve.tensor_tensor(ch, XN[:, c * CT:(c + 1) * CT, :], ch, ALU.add).then_inc(c_acc, 1)

            def d_scan_chunk(c):
                k = c % 2
                dve.wait_ge(d_act, c + 1)
                if c >= 2:
                    dve.wait_ge(d_turn, c - 1)
                dve.tensor_scalar(decay[:, k, :], state[:, k, :], 0.998, 0.001, ALU.mult, ALU.add)
                link(dve.tensor_tensor(gate[:, k, :], gate[:, k, :], tnh[:, k, :], ALU.mult))
                for b in range(BC):
                    sl = slice(b * S, (b + 1) * S)
                    last = dve.tensor_tensor_scan(drive[:, k, sl], decay[:, k, sl], gate[:, k, sl], 0.0, ALU.mult, ALU.add)
                last.then_inc(d_scan, 1)

            def d_residual(c):
                dve.wait_ge(d_turn, c + 1)
                ch = X[:, c * CT:(c + 1) * CT, :]
                dve.tensor_tensor(ch, ps[5][:].rearrange("p (t d) -> p t d", d=D), ch, ALU.add).then_inc(d_add, 1)

            for c in range(C):
                c_residual(c)
                dve.wait_ge(c_acc, c + 1)
                layer_norm(c)
                if c >= 1:
                    d_scan_chunk(c - 1)
                if c >= 2:
                    d_residual(c - 2)
            d_scan_chunk(C - 1)
            d_residual(C - 2)
            d_residual(C - 1)

            for c in range(C):
                dve.wait_ge(d_add, c + 1)
                layer_norm(c)
            parts = 0
            for step in range(FIRST, LAST):
                b = batch_at(step, AT_SPLIT)
                if b is not None:
                    k = b % 2
                    dve.wait_ge(e_fill, 2)
                    dve.wait_ge(e_qs[k], 16 * (b // 2 + 1))
                    if b >= 2:
                        dve.wait_ge(e_turn, fill_of["q2", b - 2, 1] + 1)
                    src = Qs[:, k].rearrange("p (a i) d -> p i a d", i=2)
                    va, vb = (v[:].rearrange("p (a i) d -> p i a d", i=2) for v in (q1, q2))
                    slot = [QQ[:, k, :, :, AD * j:AD * (j + 1)] for j in range(6)]
                    parts = split_parts(dve, e_qpart, parts, src, va, vb, slot[0], slot[1], slot[3])
                    dve.tensor_copy(slot[2], slot[0])
                    dve.tensor_copy(slot[4], slot[0])
                    dve.tensor_copy(slot[5], slot[1]).then_inc(e_qq, 1)
                b = batch_at(step, AT_MAX)
                if b is not None:
                    k = b % 2
                    dve.wait_ge(e_max, NA * (b + 1))
                    dve.tensor_scalar(mx[:, 0, :], mx3[:, k, :, 0], -1.0, None, ALU.mult)
                    link(dve.tensor_tensor(mr[:, 0, :], mx3[:, k, :, 1], mx3[:, k, :, 2], ALU.max))
                    link(dve.tensor_scalar(mx[:, 1, :], mr[:, 0, :], -1.0, None, ALU.mult))
                    top = [QQ[:, k, :, :, 6 * AD + j] for j in range(3)]
                    parts = split_parts(dve, e_qpart, parts, mx[:], mr[:], mr2[:], *top)
                    dve.sem_inc(e_mq, 1)
                g = group_at(step, AT_GROUP)
                if g is not None:
                    b, a = divmod(g * OG, NA)
                    f = fill_of["group", g, 0]
                    dve.wait_ge(e_turn, f + 1)
                    if a == 0 and b >= 2:
                        dve.wait_ge(e_od[b % 2], 16 * (b // 2))
                    o = ps[f % 2][:, 0:2 * P].rearrange("p (i a d) -> p i a d", i=2, d=OW)
                    dve.reciprocal(orec[:], o[:, :, :, AD]).then_inc(e_rec, 1)
                    dve.wait_ge(e_rec, g + 1)
                    dst = Os[:, b % 2, 2 * a:2 * (a + OG), :].rearrange("p (a i) d -> p i a d", i=2)
                    dve.tensor_tensor(dst, o[:, :, :, 0:AD], orec[:].unsqueeze(3).to_broadcast([P, 2, OG, AD]), ALU.mult).then_inc(e_read, 1)
                    dve.wait_ge(e_read, read_count(f))
                    dve.sem_inc(e_o, 1)
                n = step
                if 0 <= n < NP:
                    b, a = divmod(n, NA)
                    dve.wait_ge(e_i, n + 1)
                    dve.tensor_reduce(mx3[:, b % 2, a, :], ps[2 + n % 2][:, 0:CUT].rearrange("p (g j) -> p g j", g=3), AX.X, ALU.max).then_inc(e_max, 1)
                b = batch_at(step, AT_Y)
                if b is not None:
                    f = fill_of["y", b, 0]
                    dve.wait_ge(e_turn, f + 1)
                    xx = X[:, 2 * b:2 * b + 2, :]
                    dve.tensor_tensor(xx, ps[f % 2][:, 0:2 * P].rearrange("p (t d) -> p t d", d=D), xx, ALU.add).then_inc(e_read, 1)
                    dve.wait_ge(e_read, read_count(f))
                    dve.sem_inc(e_add, 1)

            for c in range(C):
                dve.wait_ge(e_add, BC * (c + 1))
                layer_norm(c)
            dve.wait_ge(f_sc, 1)
            link(dve.tensor_copy(aff[:], ps[2][:, 0:T * E].rearrange("p (t e) -> p t e", e=E)))
            link(dve.tensor_reduce(amax[:], aff[:], AX.X, ALU.max))
            link(first_max(oh, aff[:], amax))
            link(dve.scalar_tensor_tensor(out=rden[:], in0=oh[:], scalar=-3.0e38, in1=aff[:], op0=ALU.mult, op1=ALU.add))
            link(dve.tensor_reduce(f_m2[:], rden[:], AX.X, ALU.max))
            dve.tensor_tensor(f_z[:], f_m2[:], amax[:], ALU.subtract).then_inc(f_d, 1)
            link(first_max(ndisp, rden[:], f_m2))
            dve.wait_ge(f_ex, 1)
            link(dve.tensor_scalar(f_p[:], f_e[:], 1.0, None, ALU.add))
            link(dve.reciprocal(f_m2[:], f_p[:]))
            link(dve.tensor_tensor(f_p[:], f_e[:], f_m2[:], ALU.mult))
            link(dve.tensor_tensor(disp[:], oh[:], f_m2[:].unsqueeze(2).to_broadcast([P, T, E]), ALU.mult))
            link(dve.tensor_tensor(ndisp[:], ndisp[:], f_p[:].unsqueeze(2).to_broadcast([P, T, E]), ALU.mult))
            link(dve.tensor_tensor(disp[:], disp[:], ndisp[:], ALU.add))

            def f_hidden_mul(n):
                for k in range(GH):
                    dve.wait_ge(f_h, 2 * GH * n + GH + k + 1)
                    dve.wait_ge(f_silu, GH * n + k + 1)
                    if n >= 2:
                        dve.wait_ge(f_y, n - 1)
                    dve.tensor_tensor(hT[:, n % 2, 2 + k, :], ps[2 + GH + k][:], hT[:, n % 2, k, :], ALU.mult).then_inc(f_mul, 1)

            def f_accumulate(n):
                e, c = divmod(n, C)
                dve.wait_ge(f_y, n + 1)
                if e >= 1:
                    dve.wait_ge(f_acc, n - C + 1)
                for i in range(CT):
                    t = c * CT + i
                    last = dve.scalar_tensor_tensor(out=X[:, t, :], in0=ps[6 + n % 2][:, i * P:(i + 1) * P],
                                                    scalar=disp[:, t, e:e + 1], in1=X[:, t, :], op0=ALU.mult, op1=ALU.add)
                last.then_inc(f_acc, 1)

            for n in range(E * C + 1):
                if n < E * C:
                    f_hidden_mul(n)
                if n >= 1:
                    f_accumulate(n - 1)


def _constants():
    c = np.zeros((P, NCONST), np.float32)
    i = np.arange(P)
    c[:, 0:P] = np.eye(P, dtype=np.float32)
    c[:, P:2 * P] = np.where(i[:, None] > i[None, :], NEG, 0.0)
    c[:, 2 * P:3 * P] = np.where(i[None, :] > i[:, None], NEG, 0.0)
    at = CONST["minus3"][0]
    c[0:3 * R, at:at + R] = -np.tile(np.eye(R, dtype=np.float32), (3, 1))
    for name, values in (("earlier", i[:, None] < i[None, :]), ("tile_sizes", P * np.arange(T)[None, :]),
                         ("slot", np.arange(C_SLOTS)[None, :]), ("spare", C_ZERO + P * np.arange(T)[None, :] + i[:, None])):
        at, width = CONST[name]
        c[:, at:at + width] = values
    s = np.arange(S)
    for h in range(2):
        before = (s[None, :] < (h * P + i)[:, None]).astype(np.float32)
        c[:, 3 * P + h * S:3 * P + (h + 1) * S] = before
        c[:, 3 * P + 2 * S + h * S:3 * P + 2 * S + (h + 1) * S] = 1.0 - before
    return c


def kernel(**inputs):
    import concourse.bacc as _bacc
    from concourse import mybir as _mybir
    from concourse.bass_utils import run_bass_kernel_spmd as _run

    g = {k: np.asarray(v) for k, v in inputs.items()}
    small = np.zeros((P, NCOLS), np.float32)

    def put(name, a):
        at, w = COLS[name]
        small[0:a.shape[0], at:at + w] = a

    bp = g["L0_attn_bp"].reshape(3, D)
    put("bw", bp[0][:, None])
    put("bk", bp[1][:, None])
    put("bu", g["L0_attn_bu"][:, None])
    put("bg", g["L1_attn_bg"][:, None])
    put("bv", g["L1_attn_bv"][:, None])
    put("bd", g["L1_attn_bd"][:, None])
    put("b1", g["L0_ffn_b1"].reshape(E * FK, P).T)
    gi, gf = g["L0_xattn_igate_kernel"].reshape(3, D, NH), g["L0_xattn_fgate_kernel"].reshape(3, D, NH)
    for n, name in enumerate(("gq", "gk", "gv")):
        put(name, np.concatenate([gi[n], gf[n]], axis=1))
    put("gbias", np.concatenate([np.tile(g["L0_xattn_igate_bias"], B), np.tile(g["L0_xattn_fgate_bias"], B)])[:, None])
    put("thr", np.broadcast_to(g["L0_ffn_affinity_threshold"].reshape(1, 1), (P, 1)))
    put("rms", np.broadcast_to(g["L0_xattn_rms_scale"][None, :], (P, HD)))
    put("bo", np.broadcast_to(g["L0_attn_bo"][None, :], (P, D)))
    put("waffT", g["L0_ffn_waff"].T)
    put("gateT", g["L1_ffn_gate_w"].T)
    put("b2", g["L0_ffn_b2"])
    put("prio", np.broadcast_to(np.arange(E, 0, -1, dtype=np.float32)[None, :], (P, E)))

    arrays = {
        "x": g["x"].reshape(B * S, D),
        "ctx": g["ctx_1024"].reshape(B * S, D),
        "ctxT": g["ctx_1024"].reshape(B * S, D).T,
        "small": small,
        "const": _constants(),
        "wp": g["L0_attn_Wp"],
        "wu": g["L0_attn_Wu"],
        "wo": g["L0_attn_Wo"],
        "w1": g["L0_ffn_W1"].transpose(1, 0, 2),
        "w2": g["L0_ffn_W2"].reshape(E, FK, P, D).transpose(2, 0, 1, 3),
        "lw": np.concatenate([g["L1_attn_Wg"].T, g["L1_attn_Wv"].T, g["L1_attn_Wd"].T], axis=1),
        "aw": np.concatenate([g["L1_xattn_wq"].T, g["L1_xattn_wk"].T, g["L1_xattn_wv"].T, g["L1_xattn_wo"].T], axis=1),
        "w12": g["L1_ffn_w12"].transpose(2, 0, 1),
        "w3": g["L1_ffn_w3"].reshape(E, D, GH, P).transpose(3, 0, 2, 1),
    }
    nc = _bacc.Bacc("TRN2", target_bir_lowering=False, num_devices=1)
    feed, args = {}, []
    for name, a in arrays.items():
        a = np.ascontiguousarray(a)
        feed[f"in_{name}"] = a
        args.append(nc.dram_tensor(f"in_{name}", a.shape, _mybir.dt.from_np(a.dtype), kind="ExternalInput").ap())
    args.append(nc.dram_tensor("out_x", (B * S, D), F32, kind="ExternalOutput").ap())
    build(nc, *args)
    r = _run(nc, [feed], core_ids=[0])
    return r.results[0]["out_x"].reshape(B, S, D)
```

```python
from contextlib import ExitStack

import numpy as np
import concourse.bass as bass
from concourse import mybir


F32 = mybir.dt.float32
BF16 = mybir.dt.bfloat16
I32 = mybir.dt.int32
ALU = mybir.AluOpType
ACT = mybir.ActivationFunctionType
AX = mybir.AxisListType

B, S, D = 8, 256, 128
P = 128
T = B * S // P
C = 4
CT = T // C
CW = CT * P
BC = CW // S
NH = 4
HD = D // NH
R = B * NH
E = 8
FK = 4
GH = 2
NA = 16
AD = 8
NP = B * NA
CUT = 2 * P + P
SL = 64
OW = 32
HW = 64
OG = P // OW
NEG = -1.0e30
LN_EPS = 1e-5

COLS = {}
C_SLOTS = T + E - 1
C_GROUPS = -(-C_SLOTS // CT)
C_ZERO = C_SLOTS * P
TOP = 2
PARTS = (range(0, T - 2 * CT), range(T - 2 * CT, T - CT), range(T - CT, T))
SLOT_DELAY = 0
F_SLOTS = [TOP * len(part) + E - 1 for part in PARTS]
F_GROUPS = [-(-n // CT) for n in F_SLOTS]
FIRST_SLOT = [sum(F_SLOTS[:p]) for p in range(len(PARTS) + 1)]
FIRST_GROUP = [sum(F_GROUPS[:p]) for p in range(len(PARTS) + 1)]
MAX_SLOTS = max([C_SLOTS] + F_SLOTS)


def _pack_columns():
    at = 0
    for name, width in (("bw", 1), ("bk", 1), ("bu", 1), ("bg", 1), ("bv", 1), ("bd", 1), ("b1", E * FK),
                        ("gq", 8), ("gk", 8), ("gv", 8), ("gbias", 1), ("thr", 1), ("rms", HD), ("bo", D),
                        ("waffT", E), ("gateT", E), ("b2", D), ("prio", E)):
        COLS[name] = (at, width)
        at += width
    return at


NCOLS = _pack_columns()

CONST = {"ident": (0, P), "neg_ji": (P, P), "neg_ij": (2 * P, P), "before": (3 * P, 2 * S), "after": (3 * P + 2 * S, 2 * S),
         "minus3": (3 * P + 4 * S, R), "earlier": (3 * P + 4 * S + R, P), "tile_sizes": (4 * P + 4 * S + R, T),
         "slot": (4 * P + 4 * S + R + T, MAX_SLOTS), "spare": (4 * P + 4 * S + R + T + MAX_SLOTS, T)}
NCONST = CONST["spare"][0] + T


def build(nc, x, ctx_in, ctxT_in, small_in, const_in, wp_in, wu_in, wo_in, w1_in, w2_in, lw_in, aw_in, w12_in, w3_in, out):
    es = ExitStack()
    with es:
        def sb(name, shape, dt=F32):
            return es.enter_context(nc.sbuf_tensor(name, shape, dt))

        def sem(name):
            return es.enter_context(nc.semaphore(name))

        X = sb("X", [P, T, D])
        XN = sb("XN", [P, T, D])
        XNT = [sb(f"XNT{i}", [P, T * P]) for i in range(2)]
        small = sb("small", [P, NCOLS])
        const = sb("const", [P, NCONST])
        ctxT = sb("ctxT", [P, T * P])
        ones = sb("ones", [P, P])
        ident_b = sb("ident_b", [P, P], BF16)
        neg_ji_b = sb("neg_ji_b", [P, P], BF16)
        neg_ij_b = sb("neg_ij_b", [P, P], BF16)
        wp = sb("wp", [P, 3 * D])
        wu = sb("wu", [P, D])
        wo = sb("wo", [P, D])
        lw = sb("lw", [P, 3 * D])
        aw = sb("aw", [P, 4 * D])
        stats = sb("stats", [P, T, 6])
        mv = sb("mv", [P, T, 2])
        vareps = sb("vareps", [P, T])
        rstd = sb("rstd", [P, T])
        power = sb("power", [P, 2])

        scan_room = sb("scan_room", [P, 5, 2 * CW])
        gate, tnh, decay, drive, state = (scan_room[:, i, :].rearrange("p (n c) -> p n c", n=2) for i in range(5))

        zpad = sb("zpad", [P, 2, 68 * B])
        gkv = sb("gkv", [P, 8])
        sel_room = sb("sel_room", [P, R * P])
        sel = sel_room[0:3 * R, 0:R * P // 2].bitcast(BF16).rearrange("p (r m) -> p r m", m=P)
        gp = sb("gp", [3 * R, S], BF16)
        g_part = sb("g_part", [R, S], BF16)
        g_i = sb("g_i", [R, S])
        g_f = sb("g_f", [R, S])
        g_n = sb("g_n", [R, S])
        g_l = sb("g_l", [R, S])
        g_e = sb("g_e", [R, S])
        g_cs = sb("g_cs", [R, S])
        g_b = sb("g_b", [R, S])
        g_g = sb("g_g", [R, S])
        g_m = sb("g_m", [R, S])
        bT = sb("bT", [P, 2, 2, R])
        v_room = sb("v_room", [P, 2 * NP * (AD + 1) + OW])
        vaug = v_room[:, 0:T * NH * (HD + 1)].rearrange("p (t h d) -> p t h d", t=T, h=NH)
        score_room = sb("score_room", [P, 2 * OG * CUT])
        cT = score_room[:].rearrange("p (n c) -> p n c", n=2 * NH)
        hn = sb("hn", [P, 2 * NH])
        hr = sb("hr", [P, 2 * NH])
        hh = sb("hh", [P, 2 * NH, HD])
        hq = sb("hq", [P, 2 * NH, HD])
        hv = sb("hv", [P, 2 * NH])
        hv2 = sb("hv2", [P, 2 * NH])
        rms1 = sb("rms1", [P, HD])

        w_room = sb("w_room", [P, 2 * E * FK * P])
        w1 = w_room[:, 0:E * FK * P].rearrange("p (e f) -> p e f", e=E)
        w2 = w_room[:, E * FK * P:].rearrange("p (e k d) -> p e k d", e=E, k=FK)
        h_room = sb("h_room", [P, 2 * FK * CW])
        hS = h_room[:, 6 * FK * P:].rearrange("p (n k c) -> p n k c", n=2, k=FK)
        dec = h_room[:, 0:3 * CUT].rearrange("p (n c) -> p n c", n=3)
        OB = h_room[:, 3 * CUT:3 * CUT + 2 * S]
        gz = sb("gz", [P, E, FK, E])
        G0 = sb("G0", [E, D])
        wsq = sb("wsq", [P, E])
        wsum = sb("wsum", [P, E])
        wn = sb("wn", [P, E])
        xsq = sb("xsq", [P, T])
        xnm = sb("xnm", [P, T])
        sqj = sb("sqj", [P, D])
        den = sb("den", [P, T, E])
        rden = sb("rden", [P, T, E])
        aff = sb("aff", [P, T, E])
        amax = sb("amax", [P, T])
        eq = sb("eq", [P, T, E])
        pri = sb("pri", [P, T, E])
        pm = sb("pm", [P, T])
        oh = sb("oh", [P, T, E])
        ohT = h_room[0:E, 0:T * P]
        affT = h_room[0:E, T * P:2 * T * P]
        ndT = sel_room[0:E, 0:T * P]
        asum = sb("asum", [P, 1])
        zc = sb("zc", [P, 1])
        sg = sb("sg", [P, 1])
        cap = sb("cap", [P, 1])
        cnt = sb("cnt", [P, 2, T])
        cj = scan_room[:, 3, 0:2 * S].rearrange("p (n s) -> p n s", n=2)
        rank1 = sb("rank1", [P, T])
        keep = sb("keep", [P, T])
        disp = sb("disp", [P, T, E])
        ndisp = sb("ndisp", [P, T, E])

        sums = scan_room[:, 4, :]
        size = sb("size", [P, E])
        tiles_of = sb("tiles_of", [P, E])
        tile_end = sb("tile_end", [P, E])
        shift = sb("shift", [P, E])
        row_of = sb("row_of", [P, T])
        unsent = sb("unsent", [P, T])
        to_row = sb("to_row", [P, T], I32)
        from_row = sb("from_row", [P, T], I32)
        passed = sums[:, 4 * E * T:4 * E * T + MAX_SLOTS * E].rearrange("p (n e) -> p n e", e=E)
        expert_f = sb("expert_f", [P, MAX_SLOTS])
        expert_of = sb("expert_of", [P, C_SLOTS], I32)
        f_expert_of = sb("f_expert_of", [P, FIRST_SLOT[-1]], I32)
        f_row = sb("f_row", [P, T])
        f_rows = sb("f_rows", [P, TOP, T], I32)
        w1_now = scan_room[:, 0, :].rearrange("p (n f) -> p n f", n=2)
        b1_now = scan_room[:, 1, 0:2 * FK].rearrange("p (n k) -> p n k", n=2)
        xg = score_room[:].rearrange("p (t d) -> p t d", d=P)
        xgT = XNT[0][:].rearrange("p (n c) -> p n c", n=C)
        yg = XNT[1][:].rearrange("p (n c) -> p n c", n=C)

        kv_tm = [room.rearrange("p (b i d) -> p b i d", i=2, d=2 * D) for room in
                 (XN[:].rearrange("p t d -> p (t d)"), h_room[:, 4 * CW:8 * CW])]
        Qs = sb("Qs", [P, 2, 2 * NA, AD])
        q1 = sb("q1", [P, 2 * NA, AD])
        q2 = sb("q2", [P, 2 * NA, AD])
        mx3 = sb("mx3", [P, 2, NA, 3])
        mx = sb("mx", [P, 2, NA])
        mr = sb("mr", [P, 2, NA])
        mr2 = sb("mr2", [P, 2, NA])
        pT = score_room[:].rearrange("p (n c) -> p n c", n=2 * OG)
        orec = sb("orec", [P, 2, OG])
        Os = sb("Os", [P, 2, 2 * NA, AD])
        Otm = sb("Otm", [P, 2, 2, D])
        OT = sb("OT", [P, 2, 2 * P])
        w12 = scan_room[:, 0:4, :].rearrange("p a (n c) -> p (a n) c", n=2)
        w3 = ctxT[:].rearrange("p (e k d) -> p e k d", e=E, k=GH)
        f_p2 = sb("f_p2", [P, T])
        f_xg = [XNT[1][:].rearrange("p (t d) -> p t d", d=P), h_room[:, T * P:].rearrange("p (t d) -> p t d", d=P),
                w_room[:, 0:2 * T * P].rearrange("p (t d) -> p t d", d=P)]
        f_hS = h_room[:, 8 * P:8 * P + 4 * GH * P].rearrange("p (n k c) -> p n k c", n=2, k=2 * GH)
        f_xgT = sel_room[:, 0:2 * CW].rearrange("p (n c) -> p n c", n=2)
        w12_now = sel_room[:, 2 * CW:4 * CW].rearrange("p (n f) -> p n f", n=2)
        f_yg = sel_room[:, 4 * CW:8 * CW].rearrange("p (n c) -> p n c", n=4)
        f_back_rows = w_room[:, E * FK * P:].rearrange("p (j t d) -> p j t d", j=TOP, d=P)
        f_m2 = sb("f_m2", [P, T])
        f_z = sb("f_z", [P, T])
        f_e = sb("f_e", [P, T])
        f_p = sb("f_p", [P, T])
        Ks = sb("Ks", [P, 2, 2 * NA, AD])
        r1 = sb("r1", [P, 2 * NA, AD])
        r2 = sb("r2", [P, 2 * NA, AD])
        KK = h_room[:, 0:2048].bitcast(BF16).rearrange("p (n i a s) -> p n i a s", n=2, i=2, s=SL)
        QQ = h_room[:, 2048:4096].bitcast(BF16).rearrange("p (n i a s) -> p n i a s", n=2, i=2, s=SL)
        KT = w_room[:].bitcast(BF16).rearrange("p (q s) -> p q s", s=S)
        QT = sel_room[:].bitcast(BF16).rearrange("p (v n q s) -> p v n q s", v=2, n=2, s=S)
        Va = v_room[:, 0:2 * NP * (AD + 1)].rearrange("p (n d) -> p n d", d=AD + 1)
        OV = sb("OV", [P, 2, S])
        zero_row = OV[:, 0, 0:P]

        ps = [es.enter_context(nc.psum_tensor(f"bank{i}", [P, 512], F32)) for i in range(8)]
        ps_b = [bank[:].bitcast(BF16) for bank in ps]

        kv_d = nc.dram_tensor("kv_rows", (2, B, 2, P, D), F32, kind="Internal").ap()
        q_d = nc.dram_tensor("q_rows", (T, P, D), F32, kind="Internal").ap()
        o_d = nc.dram_tensor("o_rows", (T, P, D), F32, kind="Internal").ap()

        xg_d = nc.dram_tensor("slot_rows", ((C_SLOTS + T) * P, D), F32, kind="Internal").ap()
        y_d = nc.dram_tensor("slot_outputs", ((C_SLOTS + 1) * P, D), F32, kind="Internal").ap()

        f_xg_d = [nc.dram_tensor(f"part_rows{h}", (F_SLOTS[h] * P, D), F32, kind="Internal").ap() for h in range(len(PARTS))]
        f_y_d = [nc.dram_tensor(f"part_outputs{h}", (F_SLOTS[h] * P, D), F32, kind="Internal").ap() for h in range(len(PARTS))]

        def problems(rows):
            return rows.rearrange("i p (g d) -> (i p g) d", d=AD).rearrange("(n p) d -> p n d", p=P)

        def col(name):
            a, w = COLS[name]
            return small[:, a:a + w]

        def cst(name):
            a, w = CONST[name]
            return const[:, a:a + w]

        ident = cst("ident")

        s_x = [sem(f"s_x{k}") for k in range(2)]
        s_small = sem("s_small")
        s_ident = sem("s_ident")
        s_const = sem("s_const")
        s_wa = sem("s_wa")
        s_ctxT = sem("s_ctxT")
        s_ctx = sem("s_ctx")
        s_lw = sem("s_lw")
        s_aw = sem("s_aw")
        s_w1 = sem("s_w1")
        s_w2 = sem("s_w2")
        s_out = sem("s_out")
        dve_seq = sem("dve_seq")
        pool_seq = sem("pool_seq")
        act_seq = sem("act_seq")
        var_ready = sem("var_ready")
        rstd_ready = sem("rstd_ready")
        pow_asked = sem("pow_asked")
        pow_done = sem("pow_done")
        xn_ready = sem("xn_ready")
        xnt_turned = sem("xnt_turned")
        xnt_ready = sem("xnt_ready")
        a_proj = sem("a_proj")
        a_gate = sem("a_gate")
        a_drive = sem("a_drive")
        a_scan = sem("a_scan")
        a_out = sem("a_out")
        a_add = sem("a_add")
        a_bias = sem("a_bias")
        pool_const = sem("pool_const")
        b_gates = sem("b_gates")
        b_pad = sem("b_pad")
        b_exp = sem("b_exp")
        b_dve = sem("b_dve")
        b_turn = sem("b_turn")
        b_turned = sem("b_turned")
        b_sc = sem("b_sc")
        b_dec = sem("b_dec")
        b_ct = sem("b_ct")
        b_pv = sem("b_pv")
        b_ov = sem("b_ov")
        b_ot = sem("b_ot")
        b_num = sem("b_num")
        c_sq = sem("c_sq")
        c_gb = sem("c_gb")
        c_num = sem("c_num")
        c_wn = sem("c_wn")
        c_wsum = sem("c_wsum")
        c_wsq = sem("c_wsq")
        c_sum = sem("c_sum")
        c_mean = sem("c_mean")
        c_z = sem("c_z")
        c_sig = sem("c_sig")
        c_oh = sem("c_oh")
        c_turn = sem("c_turn")
        c_turned = sem("c_turned")
        c_row = sem("c_row")
        c_cnt = sem("c_cnt")
        c_nd = sem("c_nd")
        c_g0 = sem("c_g0")
        c_g0c = sem("c_g0c")
        c_base = sem("c_base")
        c_badd = sem("c_badd")
        c_zero = sem("c_zero")
        c_totals = sem("c_totals")
        c_rows = sem("c_rows")
        c_expert = sem("c_expert")
        c_sent = sem("c_sent")
        slot_load = [sem(f"slot_load{g}") for g in range(max([C_GROUPS] + F_GROUPS))]
        c_xt = sem("c_xt")
        c_xtc = sem("c_xtc")
        c_w = sem("c_w")
        c_h = sem("c_h")
        c_act = sem("c_act")
        c_y = sem("c_y")
        c_yc = sem("c_yc")
        slot_stored = [sem(f"slot_stored{g}") for g in range(max([C_GROUPS] + F_GROUPS))]
        token_back = [sem(f"token_back{c}") for c in range(C)]
        c_acc = sem("c_acc")
        d_proj = sem("d_proj")
        d_act = sem("d_act")
        d_scan = sem("d_scan")
        d_turn = sem("d_turn")
        d_add = sem("d_add")

        e_fill = sem("e_fill")
        e_kv = sem("e_kv")
        e_kvc = sem("e_kvc")
        e_kvd = sem("e_kvd")
        e_ks = [sem(f"e_ks{i}") for i in range(2)]
        e_va = sem("e_va")
        e_kpart = sem("e_kpart")
        e_qpart = sem("e_qpart")
        e_kk = sem("e_kk")
        e_kt = sem("e_kt")
        e_ktc = sem("e_ktc")
        e_q = sem("e_q")
        e_qc = sem("e_qc")
        e_qd = [sem(f"e_qd{i}") for i in range(C)]
        e_qs = [sem(f"e_qs{i}") for i in range(2)]
        e_qq = sem("e_qq")
        e_mq = sem("e_mq")
        e_turn = sem("e_turn")
        e_turned = sem("e_turned")
        e_i = sem("e_i")
        e_max = sem("e_max")
        e_j = sem("e_j")
        e_p = sem("e_p")
        e_pv = sem("e_pv")
        e_ov = sem("e_ov")
        e_rec = sem("e_rec")
        e_read = sem("e_read")
        e_o = sem("e_o")
        e_od = [sem(f"e_od{i}") for i in range(2)]
        e_ot = [sem(f"e_ot{i}") for i in range(2)]
        e_add = sem("e_add")
        s_w12 = sem("s_w12")
        s_w3 = sem("s_w3")
        f_zero = sem("f_zero")
        f_top = sem("f_top")
        f_d = sem("f_d")
        f_ex = sem("f_ex")
        f_sorted = sem("f_sorted")
        f_expert = sem("f_expert")
        f_sent = [sem(f"f_sent{h}") for h in range(len(PARTS))]
        f_w = sem("f_w")
        f_h = sem("f_h")
        f_silu = sem("f_silu")
        f_mul = sem("f_mul")
        f_y = sem("f_y")
        f_yc = sem("f_yc")
        f_first = sem("f_first")
        f_acc = sem("f_acc")

        KV_BANK = (4, 5, 0, 1)
        DECAY_BANK, SCORE_BANK = (2, 3, 0), (4, 5, 1)
        EARLY = 1

        def chunk_behind(b):
            c = (b - 3) // 2
            return c if b % 2 == 1 and 0 <= c < EARLY else None

        LAG_J = NA + 5
        FIRST = -NA - 4

        def batch_at(step, offset):
            b, left = divmod(step - offset, NA)
            return b if left == 0 and 0 <= b < B else None

        def group_at(step, offset):
            g, left = divmod(step - offset, OG)
            return g if left == 0 and 0 <= g < NP // OG else None

        AT_LOAD, AT_SPLIT, AT_TURN, AT_MAX, AT_TURN2 = -NA - 4, -12, -3, NA, NA + 3
        AT_PV = LAG_J + OG
        AT_GROUP = AT_PV + 2
        AT_STORE, AT_OUT, AT_Y = LAG_J + NA + 3, LAG_J + NA + 11, LAG_J + NA + 13
        AT_STATS, AT_NORM, AT_XT, AT_GATE = AT_Y + 1, AT_Y + 3, AT_Y + 5, AT_Y + 7
        AT_TOP, AT_PLACE, AT_SEND = AT_Y + 8, AT_Y + 9, AT_Y + 10
        SLOT_START = [NP + LAG_J + SLOT_DELAY + FIRST_SLOT[h] + h for h in range(len(PARTS))]
        LAST = SLOT_START[-1] + F_SLOTS[-1] + 1

        def chunk_at(step, offset):
            c, left = divmod(step - offset - (BC - 1) * NA, BC * NA)
            return c if left == 0 and 0 <= c < C else None

        def part_at(step, offset):
            for h, part in enumerate(PARTS):
                if step == offset + (part.stop * P // S - 1) * NA:
                    return h
            return None

        def slots_at(step, behind=0):
            for h, start in enumerate(SLOT_START):
                if 0 <= step - behind - start < F_SLOTS[h]:
                    return h, step - behind - start
            return None

        def turn_at(step):
            for h, start in enumerate(SLOT_START):
                g, left = divmod(step - start + 3, CT)
                if step == start - 1:
                    return h, 0
                if left == 0 and 0 < g < F_GROUPS[h]:
                    return h, g
            return None

        def group_tiles(h, g):
            return g * CT, min((g + 1) * CT, F_SLOTS[h])

        def loads_of(h, g):
            return 1 + sum(g < n for n in F_GROUPS[:h]) + (g < C_GROUPS)

        def part_and_group(n):
            h = max(h for h in range(len(PARTS)) if FIRST_GROUP[h] <= n)
            return h, n - FIRST_GROUP[h]

        def slot_rows_of(h, g):
            t0, t1 = group_tiles(h, g)
            if h > 0:
                t0, t1 = t0 + FIRST_SLOT[h] - F_SLOTS[0], t1 + FIRST_SLOT[h] - F_SLOTS[0]
                return f_xg[2][:, t0:t1, :]
            return f_xg[0][:, t0:t1, :] if t0 < T else f_xg[1][:, t0 - T:t1 - T, :]

        def split_parts(eng, part_done, count, src, left1, left2, hi, mid, lo):
            for ins in (lambda: eng.tensor_copy(hi, src),
                        lambda: eng.tensor_tensor(left1, src, hi, ALU.subtract),
                        lambda: eng.tensor_copy(mid, left1),
                        lambda: eng.tensor_tensor(left2, left1, mid, ALU.subtract),
                        lambda: eng.tensor_copy(lo, left2)):
                ins().then_inc(part_done, 1)
                count += 1
                eng.wait_ge(part_done, count)
            return count

        fills = []
        for step in range(FIRST, LAST):
            for kind, which, n in (("q", batch_at(step, AT_TURN), 2), ("q2", batch_at(step, AT_TURN2), 2),
                                   ("group", group_at(step, AT_GROUP), 1), ("out", batch_at(step, AT_OUT), 1),
                                   ("y", batch_at(step, AT_Y), 1), ("norm", chunk_at(step, AT_XT), 1),
                                   ("gate", chunk_at(step, AT_GATE), 1), ("route", part_at(step, AT_PLACE), 1),
                                   ("slots", turn_at(step), 1)):
                if which is not None:
                    fills += [(kind, which, k) for k in range(n)]
        fill_of = {f: n for n, f in enumerate(fills)}
        by_dve = ("group", "y", "gate", "route")

        def read_count(f):
            mine = fills[f][0] in by_dve
            return sum((kind in by_dve) == mine for kind, _, _ in fills[:f + 1])

        def wait_read(eng, f):
            eng.wait_ge(e_read if fills[f][0] in by_dve else e_turned, read_count(f))

        block = es.enter_context(nc.Block())

        @block.sync
        def _(sp):
            def load_x(k, tiles):
                sp.dma_start(X[:, tiles, :], x.rearrange("(t p) d -> p t d", p=P)[:, tiles, :]).then_inc(s_x[k], 16)

            load_x(0, slice(0, CT))
            sp.dma_start(const[:, 0:P], const_in[:, 0:P]).then_inc(s_ident, 16)
            sp.dma_start(wp[:], wp_in).then_inc(s_wa, 16)
            sp.dma_start(wu[:], wu_in).then_inc(s_wa, 16)
            load_x(1, slice(CT, T))
            sp.dma_start(wo[:], wo_in).then_inc(s_wa, 16)
            sp.dma_start(const[:, P:], const_in[:, P:]).then_inc(s_const, 16)
            sp.dma_start(ctxT[:], ctxT_in).then_inc(s_ctxT, 16)
            for h in range(NH):
                sp.dma_start(vaug[:, :, h, 0:HD],
                             ctx_in.rearrange("(t p) (h d) -> p t h d", p=P, h=NH)[:, :, h, :]).then_inc(s_ctx, 16)
            sp.dma_start(w1, w1_in).then_inc(s_w1, 16)
            sp.dma_start(w2, w2_in).then_inc(s_w2, 16)
            sp.wait_ge(pool_const, 1)
            sp.dma_start(xg_d[0:C_SLOTS * P].rearrange("(t p) d -> p t d", p=P), zero_row.unsqueeze(1).to_broadcast([P, C_SLOTS, P])).then_inc(c_zero, 16)
            sp.dma_start(y_d[C_ZERO:C_ZERO + P], zero_row).then_inc(c_zero, 16)
            for h in range(len(PARTS)):
                sp.dma_start(f_xg_d[h].rearrange("(t p) d -> p t d", p=P), zero_row.unsqueeze(1).to_broadcast([P, F_SLOTS[h], P])).then_inc(f_zero, 16)
            sp.dma_start(lw[:], lw_in).then_inc(s_lw, 16)
            sp.dma_start(aw[:], aw_in).then_inc(s_aw, 16)
            def group_rows(g):
                return g * CT, min((g + 1) * CT, C_SLOTS)

            for b in range(B):
                sp.wait_ge(e_kvc, b + 1)
                for n in range(2):
                    sp.dma_start(kv_d[n, b].rearrange("i p d -> p i d"),
                                 kv_tm[b // C][:, b % C, :, n * D:(n + 1) * D]).then_inc(e_kvd, 16)
            sp.wait_ge(c_sent, 16 * T)
            for g in range(C_GROUPS):
                t0, t1 = group_rows(g)
                sp.dma_start(xg[:, t0:t1, :], xg_d[t0 * P:t1 * P].rearrange("(t p) d -> p t d", p=P)).then_inc(slot_load[g], 16)
            def load_keys(b):
                if b >= 2:
                    sp.wait_ge(e_kk, b - 1)
                sp.dma_start(Ks[:, b % 2], problems(kv_d[0, b])).then_inc(e_ks[b % 2], 16)

            sp.wait_ge(e_kvd, 32 * B)
            for b in range(2):
                load_keys(b)
            for b in range(B):
                sp.dma_start(Va[:, b * 2 * NA:(b + 1) * 2 * NA, 0:AD], problems(kv_d[1, b])).then_inc(e_va, 16)
            for g in range(C_GROUPS):
                t0, t1 = group_rows(g)
                sp.wait_ge(c_yc, g + 1)
                sp.dma_start(y_d[t0 * P:t1 * P].rearrange("(t p) d -> p t d", p=P),
                             yg[:, g % C, 0:(t1 - t0) * P].rearrange("p (t d) -> p t d", d=D)).then_inc(slot_stored[g], 16)
            for b in range(2, B):
                load_keys(b)
            for c in range(C):
                sp.wait_ge(e_qc, c + 1)
                sp.dma_start(q_d[c * CT:(c + 1) * CT].rearrange("t p d -> p t d"), XN[:, c * CT:(c + 1) * CT, :]).then_inc(e_qd[c], 16)
            for step in range(FIRST, LAST):
                b = batch_at(step, AT_LOAD)
                if b is not None:
                    sp.wait_ge(e_qd[b // BC], 16)
                    if b >= 2:
                        sp.wait_ge(e_qq, b - 1)
                    sp.dma_start(Qs[:, b % 2], problems(q_d[2 * b:2 * b + 2])).then_inc(e_qs[b % 2], 16)
                    if b == 1:
                        sp.wait_ge(d_add, C)
                        sp.dma_start(w12, w12_in).then_inc(s_w12, 16)
                        sp.dma_start(w3, w3_in).then_inc(s_w3, 16)
            def load_slots(h):
                sp.wait_ge(f_sent[h], 16 * TOP * len(PARTS[h]))
                if h == 0:
                    sp.wait_ge(e_turn, fill_of["q2", B - 1, 1] + 1)
                else:
                    sp.wait_ge(e_j, NP)
                    sp.wait_ge(e_turn, fill_of["slots", (h - 1, F_GROUPS[h - 1] - 1), 0] + 1)
                for g in range(F_GROUPS[h]):
                    t0, t1 = group_tiles(h, g)
                    sp.dma_start(slot_rows_of(h, g), f_xg_d[h][t0 * P:t1 * P].rearrange("(t p) d -> p t d", p=P)).then_inc(slot_load[g], 16)

            load_slots(0)
            for n in range(FIRST_GROUP[-1]):
                if n + 2 in FIRST_GROUP[1:-1]:
                    load_slots(FIRST_GROUP.index(n + 2))
                h, g = part_and_group(n)
                t0, t1 = group_tiles(h, g)
                sp.wait_ge(f_yc, n + 1)
                sp.dma_start(f_y_d[h][t0 * P:t1 * P].rearrange("(t p) d -> p t d", p=P),
                             f_yg[:, n % 4, 0:(t1 - t0) * P].rearrange("p (t d) -> p t d", d=D)).then_inc(slot_stored[g], 16)
            rows = out.rearrange("(t p) d -> p t d", p=P)
            for c in range(C):
                sp.wait_ge(f_acc, c + 1)
                sp.dma_start(rows[:, c * CT:(c + 1) * CT, :], X[:, c * CT:(c + 1) * CT, :]).then_inc(s_out, 16)
            sp.wait_ge(s_out, 16 * C)

        @block.gpsimd
        def _(pool):
            pool.memset(ones[:], 1.0)
            pool.memset(power[:, 0:1], -0.5)
            pool.memset(power[:, 1:2], 0.5).then_inc(pool_seq, 1)
            pool.memset(zpad[:], 0.0)
            pool.memset(gz[:], 0.0)
            pool.memset(zero_row, 0.0)
            pool.memset(v_room[:, T * NH * (HD + 1):T * NH * (HD + 1) + HW], 0.0)
            pool.memset(vaug[:, :, :, HD:HD + 1], 1.0).then_inc(pool_const, 1)
            ln_count = [0]

            def rstd_of(c):
                ln_count[0] += 1
                pool.wait_ge(var_ready, ln_count[0])
                t0, t1 = c * CT, (c + 1) * CT
                pool.tensor_tensor(rstd[:, t0:t1], vareps[:, t0:t1], power[:, 0:1].to_broadcast([P, CT]), ALU.pow).then_inc(rstd_ready, 1)

            pool.wait_ge(pool_seq, 1)
            pool.wait_ge(s_small, 16)
            rstd_of(0)
            for c in range(C):
                if c + 1 < C:
                    rstd_of(c + 1)
                pool.wait_ge(xn_ready, c + 1)
                if c < 2:
                    pool.wait_ge(s_x[c], 16)
                ch = X[:, c * CT:(c + 1) * CT, :]
                pool.tensor_tensor(ch, ch, col("bo").unsqueeze(1).to_broadcast([P, CT, D]), ALU.add).then_inc(a_bias, 1)
            pool.wait_ge(s_const, 16)
            pool.wait_ge(s_small, 16)
            pool.wait_ge(a_bias, C)
            pool.tensor_copy(sel, cst("minus3")[0:3 * R, :].unsqueeze(2).to_broadcast([3 * R, R, P])).then_inc(pool_seq, 1)
            pool.wait_ge(pool_seq, 2)
            pool.tensor_tensor(gkv[:], col("gk"), col("gv"), ALU.add).then_inc(pool_seq, 1)
            pool.wait_ge(pool_seq, 3)
            for n, g in enumerate((col("gq"), gkv[:])):
                z = zpad[:, n, :].rearrange("p (b s) -> p b s", s=68)
                for k in range(2):
                    last = pool.tensor_copy(z[:, :, 32 * k:32 * k + 4],
                                            g[:, 4 * k:4 * k + 4].unsqueeze(1).to_broadcast([P, B, 4]))
            last.then_inc(b_pad, 1)
            for c in range(C):
                rstd_of(c)
            pool.wait_ge(c_wsum, 1)
            pool.tensor_tensor(wn[:], wsum[:], power[:, 1:2].to_broadcast([P, E]), ALU.pow)
            for b in range(B):
                if chunk_behind(b + 1) is not None:
                    rstd_of(chunk_behind(b + 1))
                pool.wait_ge(pow_asked, b + 1)
                pool.tensor_tensor(hv[:], hv2[:], power[:, 0:1].to_broadcast([P, 2 * NH]), ALU.pow).then_inc(pow_done, 1)
            for c in range(EARLY, C):
                rstd_of(c)
            pool.wait_ge(c_sq, T)
            pool.tensor_tensor(xnm[:], xsq[:], power[:, 1:2].to_broadcast([P, T]), ALU.pow).then_inc(pow_done, 1)
            pool.wait_ge(c_zero, 32)
            pool.wait_ge(c_rows, 1)
            for t in range(T):
                pool.indirect_dma_start(out=xg_d, out_offset=bass.IndirectOffsetOnAxis(ap=to_row[:, t:t + 1], axis=0),
                                        in_=XN[:, t, :], in_offset=None).then_inc(c_sent, 16)
            for n in range(2):
                pool.memset(KK[:, n, :, :, 6 * AD:SL], 0.0)
            pool.memset(v_room[:, 2 * NP * (AD + 1):], 0.0)
            pool.memset(Va[:, :, AD:AD + 1], 1.0).then_inc(e_fill, 1)
            pool.wait_ge(e_fill, 1)
            for n in range(2):
                last = pool.memset(KK[:, n, :, :, 6 * AD:6 * AD + 3], 1.0)
            last.then_inc(e_fill, 1)
            for g in range(C_GROUPS):
                pool.wait_ge(slot_stored[g], 16)
            for t in range(T):
                pool.indirect_dma_start(out=XN[:, t, :], out_offset=None, in_=y_d,
                                        in_offset=bass.IndirectOffsetOnAxis(ap=from_row[:, t:t + 1], axis=0)).then_inc(token_back[t // CT], 16)
            for c in range(C):
                rstd_of(c)
            pool.wait_ge(c_y, C_SLOTS)
            for n in range(2):
                last = pool.memset(QQ[:, n, :, :, 6 * AD:SL], 0.0)
            last.then_inc(e_fill, 1)
            for c in range(C):
                rstd_of(c)
            for step in range(FIRST, LAST):
                b = batch_at(step, AT_STORE)
                if b is not None:
                    pool.wait_ge(e_o, NA // OG * (b + 1))
                    pool.dma_start(problems(o_d[2 * b:2 * b + 2]), Os[:, b % 2]).then_inc(e_od[b % 2], 16)
                    pool.wait_ge(e_od[b % 2], 16 * (b // 2 + 1))
                    if b >= 2:
                        pool.wait_ge(e_turn, fill_of["out", b - 2, 0] + 1)
                    pool.dma_start(Otm[:, b % 2], o_d[2 * b:2 * b + 2].rearrange("i p d -> p i d")).then_inc(e_ot[b % 2], 16)
                c = chunk_at(step, AT_STATS)
                if c is not None:
                    rstd_of(c)
                for i in range(T):
                    h = part_at(step, AT_SEND + i)
                    if h is not None and i < len(PARTS[h]):
                        if i == 0:
                            pool.wait_ge(f_zero, 16 * len(PARTS))
                            pool.wait_ge(f_sorted, h + 1)
                        t = PARTS[h].start + i
                        for j in range(TOP):
                            pool.indirect_dma_start(out=f_xg_d[h], out_offset=bass.IndirectOffsetOnAxis(ap=f_rows[:, j, t:t + 1], axis=0),
                                                    in_=XN[:, t, :], in_offset=None).then_inc(f_sent[h], 16)
            for h, part in enumerate(PARTS):
                for g in range(F_GROUPS[h]):
                    pool.wait_ge(slot_stored[g], 16 * loads_of(h, g))
                for t in part:
                    for j in range(TOP):
                        pool.indirect_dma_start(out=f_back_rows[:, j, t, :], out_offset=None, in_=f_y_d[h],
                                                in_offset=bass.IndirectOffsetOnAxis(ap=f_rows[:, j, t:t + 1], axis=0)).then_inc(token_back[t // CT], 16)

        @block.scalar
        def _(act):
            act.dma_start(small[:], small_in).then_inc(s_small, 16)
            ln_count = [0]

            def copy_xnt(layer):
                def one(c):
                    n = ln_count[0]
                    act.wait_ge(xnt_turned, n + 1)
                    act.activation(XNT[layer % 2][:, c * CW:(c + 1) * CW], ps[n % 2][:], ACT.Copy).then_inc(xnt_ready, 1)
                    ln_count[0] += 1
                return one

            cp = copy_xnt(0)
            act.wait_ge(s_small, 16)
            for c in range(C):
                cp(c)
                act.wait_ge(a_proj, c + 1)
                if c >= 2:
                    act.wait_ge(a_drive, c - 1)
                act.activation(gate[:, c % 2, :], ps[2][:], ACT.Sigmoid, bias=col("bw"))
                act.activation(tnh[:, c % 2, :], ps[3][:], ACT.Tanh, bias=col("bk")).then_inc(a_gate, 1)

            cp = copy_xnt(1)
            for c in range(C):
                cp(c)
            def copy_keys_values(b):
                act.wait_ge(e_kv, b + 1)
                act.activation(kv_tm[b // C][:, b % C].rearrange("p i d -> p (i d)"), ps[KV_BANK[b % 4]][:], ACT.Copy).then_inc(e_kvc, 1)

            act.wait_ge(b_dve, 1)
            act.activation(g_e[:], g_n[:], ACT.Exp).then_inc(act_seq, 1)
            act.wait_ge(act_seq, 1)
            act.activation(g_n[:], g_e[:], ACT.Ln, bias=1.0).then_inc(b_exp, 1)
            for b in range(B // 2):
                copy_keys_values(b)
            act.wait_ge(b_dve, 2)
            act.activation(g_e[:], g_m[:], ACT.Exp, scale=-1.0).then_inc(b_exp, 1)
            for b in range(B // 2, B):
                copy_keys_values(b)
            act.wait_ge(b_turn, 1)
            act.activation(bT[:], ps[2][:, 0:4 * R], ACT.Copy).then_inc(b_turned, 1)
            act.wait_ge(b_turned, 1)

            def copy_values(b):
                act.wait_ge(b_pv, b + 1)
                if b >= 1:
                    act.wait_ge(b_ot, b)
                act.activation(OB, ps[6][:], ACT.Copy).then_inc(b_ov, 1)

            cp = copy_xnt(2)

            def next_layer(c):
                cp(c)
                for t in range(c * CT, (c + 1) * CT):
                    act.activation(sqj[:], XN[:, t, :], ACT.Square, accum_out=xsq[:, t:t + 1]).then_inc(c_sq, 1)
                    act.wait_ge(c_sq, t + 1)

            for r in range(R):
                b, h = divmod(r, NH)
                act.wait_ge(b_sc, r + 1)
                if r >= 3:
                    act.wait_ge(b_ct, r - 2)
                if r % NH == 2 and r > NH:
                    copy_values(r // NH - 1)
                act.activation(dec[:, r % 3, 0:S], ps[DECAY_BANK[r % 3]][:, 0:S], ACT.Exp, bias=bT[:, 0, 0, r:r + 1])
                act.activation(dec[:, r % 3, S:CUT], ps[DECAY_BANK[r % 3]][:, S:CUT], ACT.Exp,
                               bias=bT[:, 0, 1, r:r + 1]).then_inc(b_dec, 1)
            copy_values(B - 1)
            for c in range(C):
                next_layer(c)

            act.wait_ge(pool_const, 1)
            for e in range(E):
                last = act.activation(gz[:, e, :, e], small[:, COLS["b1"][0] + FK * e:COLS["b1"][0] + FK * e + FK], ACT.Gelu)
            last.then_inc(c_gb, 1)
            for c in range(C):
                act.wait_ge(c_turn, c + 1)
                act.activation(affT[:, c * CW:(c + 1) * CW], ps[2 + 2 * (c % 2)][0:E, :], ACT.Copy)
                act.activation(ohT[:, c * CW:(c + 1) * CW], ps[3 + 2 * (c % 2)][0:E, :], ACT.Copy).then_inc(c_turned, 1)
            act.wait_ge(c_z, 1)
            act.activation(sg[:], zc[:], ACT.Sigmoid).then_inc(c_sig, 1)
            for c in range(C):
                act.wait_ge(c_turn, C + c + 1)
                act.activation(ndT[:, c * CW:(c + 1) * CW], ps[2 + c % 2][0:E, :], ACT.Copy).then_inc(c_turned, 1)
            def copy_group(g):
                w = min(CT, C_SLOTS - g * CT) * P
                act.wait_ge(c_xt, g + 1)
                if g >= C:
                    act.wait_ge(c_h, CT * (g - C + 1))
                act.activation(xgT[:, g % C, 0:w], ps[g % 2][:, 0:w], ACT.Copy).then_inc(c_xtc, 1)

            copy_group(0)
            for n in range(C_SLOTS):
                if n % CT == 1 and n // CT + 1 < C_GROUPS:
                    copy_group(n // CT + 1)
                if n >= 2:
                    act.wait_ge(c_y, n - 1)
                act.wait_ge(c_w, n + 1)
                act.wait_ge(c_h, n + 1)
                for k in range(FK):
                    last = act.activation(hS[:, n % 2, k, :], ps[2 + n % 2][:, k * P:(k + 1) * P], ACT.Gelu, bias=b1_now[:, n % 2, k:k + 1])
                last.then_inc(c_act, 1)

            def copy_keys(b):
                for n in range(2 * b, 2 * b + 2):
                    act.wait_ge(e_kt, n + 1)
                    act.activation(KT[:, 4 * n:4 * n + 4, :].rearrange("p q s -> p (q s)"), ps_b[6 + n % 2], ACT.Copy).then_inc(e_ktc, 1)

            cp = copy_xnt(3)
            for b in range(2):
                copy_keys(b)
            for c in range(C):
                cp(c)
                act.wait_ge(d_proj, c + 1)
                if c >= 2:
                    act.wait_ge(d_scan, c - 1)
                act.activation(gate[:, c % 2, :], ps[2][:], ACT.Sigmoid, bias=col("bg"))
                act.activation(tnh[:, c % 2, :], ps[3][:], ACT.Tanh, bias=col("bv"))
                act.activation(state[:, c % 2, :], ps[4][:], ACT.Sigmoid, bias=col("bd")).then_inc(d_act, 1)
                copy_keys(c + 2)

            cp = copy_xnt(4)
            for c in range(C):
                cp(c)
                act.wait_ge(e_q, c + 1)
                act.activation(XN[:, c * CT:(c + 1) * CT, :].rearrange("p t d -> p (t d)"), ps[2 + c % 2][:], ACT.Copy).then_inc(e_qc, 1)
                if c % 2 == 1:
                    copy_keys(6 + c // 2)

            def copy_turned(kind, b, dst):
                for k, d in enumerate(dst):
                    f = fill_of[kind, b, k]
                    act.wait_ge(e_turn, f + 1)
                    src = ps[f % 2][:, 0:2 * P] if kind == "out" else ps_b[f % 2]
                    act.activation(d, src, ACT.Copy).then_inc(e_turned, 1)

            for step in range(FIRST, LAST):
                b = batch_at(step, AT_TURN)
                if b is not None:
                    if b >= 2:
                        act.wait_ge(e_i, NA * (b - 1))
                    copy_turned("q", b, [QT[:, 0, b % 2, 4 * k:4 * k + 4, :].rearrange("p q s -> p (q s)") for k in range(2)])
                b = batch_at(step, AT_TURN2)
                if b is not None:
                    if b >= 2:
                        act.wait_ge(e_j, NA * (b - 1))
                    copy_turned("q2", b, [QT[:, 1, b % 2, 4 * k:4 * k + 4, :].rearrange("p q s -> p (q s)") for k in range(2)])
                b = batch_at(step, AT_OUT)
                if b is not None:
                    if b >= 2:
                        act.wait_ge(e_turn, fill_of["y", b - 2, 0] + 1)
                    copy_turned("out", b, [OT[:, b % 2, :]])
                c = chunk_at(step, AT_XT)
                if c is not None:
                    f = fill_of["norm", c, 0]
                    act.wait_ge(e_turn, f + 1)
                    act.activation(XNT[0][:, c * CW:(c + 1) * CW], ps[f % 2][:], ACT.Copy).then_inc(e_turned, 1)
                turn = turn_at(step)
                if turn is not None:
                    f = fill_of["slots", turn, 0]
                    n = FIRST_GROUP[turn[0]] + turn[1]
                    t0, t1 = group_tiles(*turn)
                    w = (t1 - t0) * P
                    act.wait_ge(e_turn, f + 1)
                    if n == 0:
                        act.wait_ge(e_i, NP)
                    if n >= 2:
                        h, g = part_and_group(n - 2)
                        act.wait_ge(f_h, FIRST_SLOT[h] + group_tiles(h, g)[1])
                    act.activation(f_xgT[:, n % 2, 0:w], ps[f % 2][:, 0:w], ACT.Copy).then_inc(e_turned, 1)
                h = part_at(step, AT_TOP)
                if h is not None:
                    part = slice(PARTS[h].start, PARTS[h].stop)
                    act.wait_ge(f_d, h + 1)
                    act.activation(f_e[:, part], f_z[:, part], ACT.Exp).then_inc(f_ex, 1)
                g = group_at(step, AT_GROUP - 1)
                if g is not None:
                    act.wait_ge(e_pv, g + 1)
                    if g >= 2:
                        act.wait_ge(e_turn, fill_of["group", g - 2, 0] + 1)
                    act.activation(OV[:, g % 2, :], ps[6 + g % 2][:, 0:S], ACT.Copy).then_inc(e_ov, 1)
                n = step - LAG_J
                if 0 <= n < NP:
                    act.wait_ge(e_j, n + 1)
                    if n >= 2 * OG:
                        act.wait_ge(e_pv, n // OG - 1)
                    act.activation(pT[:, n % (2 * OG), :], ps[4 + n % 2][:, 0:CUT], ACT.Exp, scale=float(AD) ** -0.5).then_inc(e_p, 1)

                slot = slots_at(step)
                if slot is not None:
                    n = FIRST_SLOT[slot[0]] + slot[1]
                    act.wait_ge(f_h, n + 1)
                    if n >= 2:
                        act.wait_ge(f_mul, n - 1)
                    act.activation(f_hS[:, n % 2, 0:GH, :], ps[2 + n % 2][:, 0:GH * P].rearrange("p (k c) -> p k c", k=GH),
                                   ACT.Silu).then_inc(f_silu, 1)

        @block.tensor
        def _(pe):
            ln_count = [0]

            def turn_xn(c):
                n = ln_count[0]
                pe.wait_ge(xn_ready, n + 1)
                if n >= 2:
                    pe.wait_ge(xnt_ready, n - 1)
                for i in range(CT):
                    last = pe.transpose(ps[n % 2][:, i * P:(i + 1) * P], XN[:, c * CT + i, :], ident)
                last.then_inc(xnt_turned, 1)
                ln_count[0] += 1

            pe.wait_ge(s_ident, 16)
            xt = XNT[0]

            def a_project(c):
                pe.wait_ge(xnt_ready, c + 1)
                if c == 0:
                    pe.wait_ge(s_wa, 48)
                if c >= 1:
                    pe.wait_ge(a_gate, c)
                    pe.wait_ge(a_drive, c)
                mov = xt[:, c * CW:(c + 1) * CW]
                pe.matmul(ps[2][:], wp[:, 0:D], mov, start=True, stop=True)
                pe.matmul(ps[3][:], wp[:, D:2 * D], mov, start=True, stop=True)
                pe.matmul(ps[4][:], wu[:], mov, start=True, stop=True).then_inc(a_proj, 1)

            def a_output(c):
                pe.wait_ge(a_scan, c + 1)
                if c >= 1:
                    pe.wait_ge(a_add, c)
                for i in range(CT):
                    last = pe.matmul(ps[5][:, i * P:(i + 1) * P], state[:, c % 2, i * P:(i + 1) * P], wo[:], start=True, stop=True)
                last.then_inc(a_out, 1)

            for c in range(C + 1):
                if c < C:
                    turn_xn(c)
                    a_project(c)
                if c >= 1:
                    a_output(c - 1)

            xt = XNT[1]
            pe.wait_ge(b_pad, 1)
            pe.wait_ge(s_ctxT, 16)
            for b in range(B):
                pe.matmul(ps[6][0:2 * R, 0:S], zpad[:, 1, b * 64:b * 64 + 64], ctxT[:, b * S:(b + 1) * S], start=(b == 0), stop=False)
            for c in range(C):
                turn_xn(c)
            for b in range(B):
                pe.wait_ge(xnt_ready, C + b // BC + 1)
                last = pe.matmul(ps[6][0:2 * R, 0:S], zpad[:, 0, b * 64:b * 64 + 64], xt[:, b * S:(b + 1) * S], start=False, stop=(b == B - 1))
            last.then_inc(b_gates, 1)
            pe.wait_ge(c_wsq, 1)
            pe.matmul(ps[3][:, 0:E], ones[:], wsq[:], start=True, stop=True).then_inc(c_wn, 1)
            pe.wait_ge(s_aw, 16)
            for b in range(B):
                if b >= 4:
                    pe.wait_ge(e_kvc, b - 3)
                for i in range(2):
                    t = 2 * b + i
                    last = pe.matmul(ps[KV_BANK[b % 4]][:, i * 2 * D:(i + 1) * 2 * D], ctxT[:, t * P:(t + 1) * P], aw[:, D:3 * D], start=True, stop=True)
                last.then_inc(e_kv, 1)
            pe.wait_ge(b_dve, 2)
            pe.wait_ge(b_exp, 2)
            for n, src in enumerate((g_b, g_e)):
                for i in range(2):
                    at = (2 * n + i) * R
                    last = pe.transpose(ps[2][:, at:at + R], src[:, i * P:(i + 1) * P], ident[0:R, 0:R])
            last.then_inc(b_turn, 1)

            def b_scores(r):
                b, h = divmod(r, NH)
                row = slice(HD * h, HD * h + HD)
                i0 = b * S
                if r == 0:
                    pe.wait_ge(b_turned, 1)
                    pe.wait_ge(c_wsum, 1)
                    pe.wait_ge(e_kvc, B)
                    pe.wait_ge(pool_seq, 3)
                    pe.wait_ge(b_dve, 3)
                if r >= 3:
                    pe.wait_ge(b_dec, r - 2)
                    pe.wait_ge(b_ct, r - 2)
                dk, sk = ps[DECAY_BANK[r % 3]], ps[SCORE_BANK[r % 3]]
                pe.matmul(dk[:, 0:S], sel[:, r, :], gp[:], start=True, stop=False)
                pe.matmul(dk[:, 0:P], ident_b[:], neg_ji_b[:], start=False, stop=True)
                pe.matmul(dk[:, S:CUT], sel[:, r, :], gp[:, P:S], start=True, stop=False)
                pe.matmul(dk[:, S:CUT], ident_b[:], neg_ji_b[:], start=False, stop=True)
                pe.matmul(sk[:, 0:S], ctxT[row, i0:i0 + P], xt[row, i0:i0 + S], start=True, stop=True)
                pe.matmul(sk[:, S:CUT], ctxT[row, i0 + P:i0 + S], xt[row, i0 + P:i0 + S], start=True, stop=True).then_inc(b_sc, 1)

            def b_values(b):
                pe.wait_ge(b_ct, NH * (b + 1))
                if b == 0:
                    pe.wait_ge(s_ctx, 16 * NH)
                    pe.wait_ge(pool_const, 1)
                else:
                    pe.wait_ge(b_ov, b)
                for q in range(2):
                    for i in range(2):
                        for f in range(2):
                            h = 2 * q + f
                            at = ((2 * b + i) * NH + h) * (HD + 1)
                            last = pe.matmul(ps[6][HW * f:HW * (f + 1), q * S + i * P:(q + 1) * S], v_room[:, at:at + HW],
                                             cT[:, (NH * b + h) % (2 * NH), i * S:CUT if i else S], start=(i == 0), stop=(i == 1))
                last.then_inc(b_pv, 1)

            def b_turn_values(b):
                pe.wait_ge(b_ov, b + 1)
                if b >= 1:
                    pe.wait_ge(b_num, 2 * b - 1)
                for n in range(4):
                    last = pe.transpose(ps[7][:, n * P:(n + 1) * P], OB[:, n * P:(n + 1) * P], ident)
                last.then_inc(b_ot, 1)

            for r in range(R):
                b_scores(r)
                if r % NH == 1 and r > NH:
                    b_values(r // NH - 1)
                if r % NH == 3 and r > NH:
                    b_turn_values(r // NH - 1)
            b_values(B - 1)
            b_turn_values(B - 1)

            xt = XNT[0]
            for c in range(C):
                if c == 0:
                    pe.wait_ge(b_dec, R)
                    pe.wait_ge(b_ct, R)
                turn_xn(c)
                pe.wait_ge(xnt_ready, 2 * C + c + 1)
                for t in range(c * CT, (c + 1) * CT):
                    last = pe.matmul(ps[2][:, t * E:(t + 1) * E], xt[:, t * P:(t + 1) * P], col("waffT"), start=True, stop=True)
            last.then_inc(c_num, 1)
            pe.wait_ge(c_gb, 1)
            pe.wait_ge(s_w2, 16)
            for e in range(E):
                for k in range(FK):
                    last = pe.matmul(ps[6][0:E, 0:D], gz[:, e, k, :], w2[:, e, k, :], start=(e == 0 and k == 0),
                                     stop=(e == E - 1 and k == FK - 1))
            last.then_inc(c_g0, 1)
            pe.wait_ge(c_sum, 1)
            pe.matmul(ps[7][:, 0:1], ones[:], asum[:], start=True, stop=True).then_inc(c_mean, 1)
            pe.wait_ge(c_oh, 1)
            for c in range(C):
                if c >= 2:
                    pe.wait_ge(c_turned, c - 1)
                for src, bank in ((aff, 2 + 2 * (c % 2)), (oh, 3 + 2 * (c % 2))):
                    for i in range(CT):
                        last = pe.transpose(ps[bank][0:E, i * P:(i + 1) * P], src[:, c * CT + i, :], ident)
                last.then_inc(c_turn, 1)
            for t in range(T):
                if t == 0:
                    pe.wait_ge(c_turned, C)
                if t >= 2:
                    pe.wait_ge(c_cnt, t - 1)
                q0 = (t // 2) * S
                pe.matmul(ps[4 + t % 2][:, 0:S], ohT[:, t * P:(t + 1) * P], affT[:, q0:q0 + S], start=True, stop=True).then_inc(c_row, 1)
            pe.wait_ge(c_nd, 1)
            sent = disp[:].rearrange("p t e -> p (t e)")
            pe.matmul(ps[4][:, 0:T * E], cst("earlier"), sent, start=True, stop=True)
            pe.matmul(ps[5][:, 0:T * E], ones[:], sent, start=True, stop=True).then_inc(c_totals, 1)
            for c in range(C):
                if c >= 2:
                    pe.wait_ge(c_turned, C + c - 1)
                for i in range(CT):
                    last = pe.transpose(ps[2 + c % 2][0:E, i * P:(i + 1) * P], ndisp[:, c * CT + i, :], ident)
                last.then_inc(c_turn, 1)
            pe.wait_ge(c_g0c, 1)
            for c in range(C):
                pe.wait_ge(c_turned, C + c + 1)
                if c >= 2:
                    pe.wait_ge(c_badd, c - 1)
                for i in range(CT):
                    o = ps[6 + c % 2][:, i * P:(i + 1) * P]
                    t = c * CT + i
                    pe.matmul(o, ndT[:, t * P:(t + 1) * P], G0[:], start=True, stop=False)
                    last = pe.matmul(o, ones[0:E, :], col("b2")[0:E, :], start=False, stop=True)
                last.then_inc(c_base, 1)

            def c_turn_group(g):
                pe.wait_ge(slot_load[g], 16)
                if g >= 2:
                    pe.wait_ge(c_xtc, g - 1)
                for t in range(g * CT, min((g + 1) * CT, C_SLOTS)):
                    last = pe.transpose(ps[g % 2][:, (t % CT) * P:(t % CT + 1) * P], xg[:, t, :], ident)
                last.then_inc(c_xt, 1)

            def c_hidden(n):
                pe.wait_ge(c_xtc, n // CT + 1)
                pe.wait_ge(c_w, n + 1)
                if n >= 2:
                    pe.wait_ge(c_act, n - 1)
                for k in range(FK):
                    last = pe.matmul(ps[2 + n % 2][:, k * P:(k + 1) * P], w1_now[:, n % 2, k * P:(k + 1) * P],
                                     xgT[:, (n // CT) % C, (n % CT) * P:(n % CT + 1) * P], start=True, stop=True)
                last.then_inc(c_h, 1)

            def c_down(n):
                g, i = divmod(n, CT)
                e = pe.value_load(expert_of[0:1, n:n + 1], min_val=0, max_val=E - 1)
                pe.wait_ge(c_act, n + 1)
                if i == 0 and g >= 2:
                    pe.wait_ge(c_yc, g - 1)
                for k in range(FK):
                    last = pe.matmul(ps[6 + g % 2][:, i * P:(i + 1) * P], hS[:, n % 2, k, :], w2[:, bass.ds(e, 1), k, :],
                                     start=(k == 0), stop=(k == FK - 1))
                last.then_inc(c_y, 1)

            pe.wait_ge(c_badd, C)
            pe.wait_ge(c_expert, 1)
            c_turn_group(0)
            for n in range(C_SLOTS + 1):
                if n < C_SLOTS:
                    c_hidden(n)
                    if n % CT == 0 and n // CT + 1 < C_GROUPS:
                        c_turn_group(n // CT + 1)
                if n >= 1:
                    c_down(n - 1)

            xt = XNT[1]
            pe.wait_ge(s_lw, 16)

            def d_project(c):
                pe.wait_ge(xnt_ready, 3 * C + c + 1)
                if c >= 1:
                    pe.wait_ge(d_act, c)
                mov = xt[:, c * CW:(c + 1) * CW]
                for k in range(3):
                    last = pe.matmul(ps[2 + k][:], lw[:, k * D:(k + 1) * D], mov, start=True, stop=True)
                last.then_inc(d_proj, 1)

            def d_output(c):
                pe.wait_ge(d_scan, c + 1)
                if c >= 1:
                    pe.wait_ge(d_add, c)
                for i in range(CT):
                    last = pe.transpose(ps[5][:, i * P:(i + 1) * P], drive[:, c % 2, i * P:(i + 1) * P], ident)
                last.then_inc(d_turn, 1)

            def turn_keys(b):
                pe.wait_ge(e_kk, b + 1)
                if b == 0:
                    pe.wait_ge(e_fill, 2)
                    pe.wait_ge(c_yc, C_GROUPS)
                for k in range(2):
                    n = 2 * b + k
                    if n >= 2:
                        pe.wait_ge(e_ktc, n - 1)
                    for q in range(4):
                        for i in range(2):
                            last = pe.transpose(ps_b[6 + n % 2][:, (2 * q + i) * P:(2 * q + i + 1) * P],
                                                KK[:, b % 2, i, 8 * k + 2 * q:8 * k + 2 * q + 2, :].rearrange("p a s -> p (a s)"), ident_b[:])
                    last.then_inc(e_kt, 1)

            for b in range(2):
                turn_keys(b)
            for c in range(C + 1):
                if c < C:
                    turn_xn(c)
                    d_project(c)
                    turn_keys(c + 2)
                if c >= 1:
                    d_output(c - 1)

            xt = XNT[0]
            for c in range(C):
                turn_xn(c)
                pe.wait_ge(xnt_ready, 4 * C + c + 1)
                if c >= 2:
                    pe.wait_ge(e_qc, c - 1)
                for i in range(CT):
                    t = c * CT + i
                    last = pe.matmul(ps[2 + c % 2][:, i * P:(i + 1) * P], xt[:, t * P:(t + 1) * P], aw[:, 0:D], start=True, stop=True)
                last.then_inc(e_q, 1)
                if c % 2 == 1:
                    turn_keys(6 + c // 2)
            pe.wait_ge(e_ktc, 2 * B)
            pe.wait_ge(e_qc, C)
            pe.wait_ge(e_kvc, B)
            pe.wait_ge(e_va, 16 * B)

            def next_fill(kind, which, k):
                f = fill_of[kind, which, k]
                if f >= 2:
                    wait_read(pe, f - 2)
                return f

            def turn_queries(kind, b):
                for k in range(2):
                    f = next_fill(kind, b, k)
                    for q in range(4):
                        for i in range(2):
                            last = pe.transpose(ps_b[f % 2][:, (2 * q + i) * P:(2 * q + i + 1) * P],
                                                QQ[:, b % 2, i, 8 * k + 2 * q:8 * k + 2 * q + 2, :].rearrange("p a s -> p (a s)"), ident_b[:])
                    last.then_inc(e_turn, 1)

            for step in range(FIRST, LAST):
                b = batch_at(step, AT_TURN)
                if b is not None:
                    pe.wait_ge(e_qq, b + 1)
                    turn_queries("q", b)
                b = batch_at(step, AT_TURN2)
                if b is not None:
                    pe.wait_ge(e_mq, b + 1)
                    turn_queries("q2", b)
                n = step
                if 0 <= n < NP:
                    b, a = divmod(n, NA)
                    rows = slice(SL * (a % 2), SL * (a % 2) + 6 * AD)
                    qt, kt = QT[rows, 0, b % 2, a // 2, :], KT[rows, n // 2, :]
                    if a % 8 == 0:
                        wait_read(pe, fill_of["q", b, a // 8])
                    if n >= 2:
                        pe.wait_ge(e_max, n - 1)
                    o = ps[2 + n % 2]
                    pe.matmul(o[:, 0:P], qt[:, 0:P], kt[:, 0:P], start=True, stop=False)
                    pe.matmul(o[:, 0:P], ident_b[:], neg_ij_b[:], start=False, stop=True)
                    pe.matmul(o[:, P:CUT], qt[:, P:S], kt[:, 0:S], start=True, stop=False)
                    pe.matmul(o[:, S:CUT], ident_b[:], neg_ij_b[:], start=False, stop=True).then_inc(e_i, 1)
                n = step - LAG_J
                if 0 <= n < NP:
                    b, a = divmod(n, NA)
                    rows = slice(SL * (a % 2), SL * (a % 2) + 6 * AD + 3)
                    qt, kt = QT[rows, 1, b % 2, a // 2, :], KT[rows, n // 2, :]
                    if a % 8 == 0:
                        wait_read(pe, fill_of["q2", b, a // 8])
                    if n >= 2:
                        pe.wait_ge(e_p, n - 1)
                    o = ps[4 + n % 2]
                    pe.matmul(o[:, 0:S], kt[:, 0:P], qt[:, 0:S], start=True, stop=False)
                    pe.matmul(o[:, 0:P], ident_b[:], neg_ji_b[:], start=False, stop=True)
                    pe.matmul(o[:, S:CUT], kt[:, P:S], qt[:, P:S], start=True, stop=False)
                    pe.matmul(o[:, S:CUT], ident_b[:], neg_ji_b[:], start=False, stop=True).then_inc(e_j, 1)
                g = group_at(step, AT_PV)
                if g is not None:
                    pe.wait_ge(e_p, OG * (g + 1))
                    if g >= 2:
                        pe.wait_ge(e_ov, g - 1)
                    for i in range(2):
                        for j in range(OG):
                            n = g * OG + j
                            o = ps[6 + g % 2][OW * j:OW * (j + 1), i * P:S]
                            v = v_room[:, (2 * n + i) * (AD + 1):(2 * n + i) * (AD + 1) + OW]
                            last = pe.matmul(o, v, pT[:, n % (2 * OG), i * S:CUT if i else S], start=(i == 0), stop=(i == 1))
                    last.then_inc(e_pv, 1)
                g = group_at(step, AT_GROUP)
                if g is not None:
                    f = next_fill("group", g, 0)
                    pe.wait_ge(e_ov, g + 1)
                    for i in range(2):
                        last = pe.transpose(ps[f % 2][:, i * P:(i + 1) * P], OV[:, g % 2, i * P:(i + 1) * P], ident)
                    last.then_inc(e_turn, 1)
                b = batch_at(step, AT_OUT)
                if b is not None:
                    f = next_fill("out", b, 0)
                    pe.wait_ge(e_ot[b % 2], 16 * (b // 2 + 1))
                    for i in range(2):
                        last = pe.transpose(ps[f % 2][:, i * P:(i + 1) * P], Otm[:, b % 2, i, :], ident)
                    last.then_inc(e_turn, 1)
                b = batch_at(step, AT_Y)
                if b is not None:
                    f = next_fill("y", b, 0)
                    wait_read(pe, fill_of["out", b, 0])
                    for i in range(2):
                        last = pe.matmul(ps[f % 2][:, i * P:(i + 1) * P], OT[:, b % 2, i * P:(i + 1) * P], aw[:, 3 * D:4 * D], start=True, stop=True)
                    last.then_inc(e_turn, 1)

                c = chunk_at(step, AT_XT)
                if c is not None:
                    f = next_fill("norm", c, 0)
                    pe.wait_ge(xn_ready, 5 * C + c + 1)
                    for i in range(CT):
                        last = pe.transpose(ps[f % 2][:, i * P:(i + 1) * P], XN[:, c * CT + i, :], ident)
                    last.then_inc(e_turn, 1)
                c = chunk_at(step, AT_GATE)
                if c is not None:
                    f = next_fill("gate", c, 0)
                    wait_read(pe, fill_of["norm", c, 0])
                    for i in range(CT):
                        t = c * CT + i
                        last = pe.matmul(ps[f % 2][:, i * E:(i + 1) * E], XNT[0][:, t * P:(t + 1) * P], col("gateT"), start=True, stop=True)
                    last.then_inc(e_turn, 1)
                h = part_at(step, AT_PLACE)
                if h is not None:
                    f = next_fill("route", h, 0)
                    pe.wait_ge(f_top, h + 1)
                    width = len(PARTS[h]) * E
                    sent = disp[:, PARTS[h].start:PARTS[h].stop, :].rearrange("p t e -> p (t e)")
                    pe.matmul(ps[f % 2][:, 0:width], cst("earlier"), sent, start=True, stop=True)
                    pe.matmul(ps[f % 2][:, width:2 * width], ones[:], sent, start=True, stop=True).then_inc(e_turn, 1)
                turn = turn_at(step)
                if turn is not None:
                    f = next_fill("slots", turn, 0)
                    h, g = turn
                    pe.wait_ge(slot_load[g], 16 * loads_of(h, g))
                    rows = slot_rows_of(h, g)
                    t0, t1 = group_tiles(h, g)
                    for i in range(t1 - t0):
                        last = pe.transpose(ps[f % 2][:, i * P:(i + 1) * P], rows[:, i, :], ident)
                    last.then_inc(e_turn, 1)
                slot = slots_at(step)
                if slot is not None:
                    h, m = slot
                    n = FIRST_SLOT[h] + m
                    wait_read(pe, fill_of["slots", (h, m // CT), 0])
                    pe.wait_ge(f_w, n + 1)
                    if n == 0:
                        pe.wait_ge(e_max, NP)
                    if n >= 2:
                        pe.wait_ge(f_mul, n - 1)
                    turned = f_xgT[:, (FIRST_GROUP[h] + m // CT) % 2, (m % CT) * P:(m % CT + 1) * P]
                    for k in range(2 * GH):
                        last = pe.matmul(ps[2 + n % 2][:, k * P:(k + 1) * P], w12_now[:, n % 2, k * P:(k + 1) * P], turned, start=True, stop=True)
                    last.then_inc(f_h, 1)
                slot = slots_at(step, 1)
                if slot is not None:
                    h, m = slot
                    n = FIRST_SLOT[h] + m
                    group = FIRST_GROUP[h] + m // CT
                    e = pe.value_load(f_expert_of[0:1, n:n + 1], min_val=0, max_val=E - 1)
                    pe.wait_ge(f_mul, n + 1)
                    if n == 0:
                        pe.wait_ge(s_w3, 16)
                        pe.wait_ge(e_p, NP)
                    if m % CT == 0 and group >= 2:
                        pe.wait_ge(f_yc, group - 1)
                    for k in range(GH):
                        last = pe.matmul(ps[4 + group % 2][:, (m % CT) * P:(m % CT + 1) * P], f_hS[:, n % 2, GH + k, :], w3[:, bass.ds(e, 1), k, :],
                                         start=(k == 0), stop=(k == GH - 1))
                    last.then_inc(f_y, 1)

        @block.vector
        def _(dve):
            chain = [0]
            ln_count = [0]

            def link(ins):
                chain[0] += 1
                ins.then_inc(dve_seq, 1)
                dve.wait_ge(dve_seq, chain[0])

            def tile_stats(t0, t1):
                for t in range(t0, t1):
                    last = dve.bn_stats(stats[:, t, :], X[:, t, :])
                link(last)

            def chunk_variance(c):
                t0, t1 = c * CT, (c + 1) * CT
                for t in range(t0, t1):
                    last = dve.bn_aggr(mv[:, t, :], stats[:, t, :])
                link(last)
                dve.tensor_scalar(vareps[:, t0:t1], mv[:, t0:t1, 1], LN_EPS, None, ALU.add).then_inc(var_ready, 1)

            def tile_apply(c, i):
                if i == 0:
                    ln_count[0] += 1
                    dve.wait_ge(rstd_ready, ln_count[0])
                t = c * CT + i
                last = dve.tensor_scalar(XN[:, t, :], X[:, t, :], mv[:, t, 0:1], rstd[:, t:t + 1], ALU.subtract, ALU.mult)
                if i == CT - 1:
                    last.then_inc(xn_ready, 1)

            def norm_stats(c):
                tile_stats(c * CT, (c + 1) * CT)
                chunk_variance(c)

            def norm_apply(c):
                for i in range(CT):
                    tile_apply(c, i)

            def layer_norm(c):
                norm_stats(c)
                norm_apply(c)

            dve.wait_ge(s_x[0], 16)

            def a_scan_chunk(c):
                k = c % 2
                dve.wait_ge(s_small, 16)
                dve.wait_ge(a_gate, c + 1)
                if c >= 2:
                    dve.wait_ge(a_out, c - 1)
                dve.scalar_tensor_tensor(out=drive[:, k, :], in0=ps[4][:], scalar=col("bu"), in1=gate[:, k, :], op0=ALU.add, op1=ALU.mult)
                link(dve.scalar_tensor_tensor(out=decay[:, k, :], in0=tnh[:, k, :], scalar=-1.0, in1=gate[:, k, :], op0=ALU.add, op1=ALU.mult))
                link(dve.tensor_scalar(decay[:, k, :], decay[:, k, :], 1.0, None, ALU.add))
                for b in range(BC):
                    sl = slice(b * S, (b + 1) * S)
                    last = dve.tensor_tensor_scan(state[:, k, sl], decay[:, k, sl], drive[:, k, sl], 0.0, ALU.mult, ALU.add)
                    if b == 0:
                        last.then_inc(a_drive, 1)
                last.then_inc(a_scan, 1)

            def a_residual(c):
                dve.wait_ge(a_out, c + 1)
                dve.wait_ge(a_bias, c + 1)
                ch = X[:, c * CT:(c + 1) * CT, :]
                ins = dve.tensor_tensor(ch, ps[5][:].rearrange("p (t d) -> p t d", d=D), ch, ALU.add)
                ins.then_inc(a_add, 1)

            layer_norm(0)
            dve.wait_ge(s_x[1], 16)
            for c in range(1, C):
                layer_norm(c)
            for c in range(C):
                if c == 0:
                    dve.wait_ge(s_ident, 16)
                    dve.tensor_copy(ident_b[:], ident)
                    dve.wait_ge(s_const, 16)
                    dve.tensor_copy(neg_ji_b[:], cst("neg_ji"))
                    dve.tensor_copy(neg_ij_b[:], cst("neg_ij"))
                a_scan_chunk(c)
                if c >= 1:
                    a_residual(c - 1)
            a_residual(C - 1)

            for c in range(C):
                dve.wait_ge(a_add, c + 1)
                layer_norm(c)
            dve.tensor_tensor(wsq[:], col("waffT"), col("waffT"), ALU.mult).then_inc(c_wsq, 1)
            dve.tensor_scalar(rms1[:], col("rms"), 1.0, None, ALU.add)
            dve.wait_ge(b_gates, 1)
            gb = col("gbias")
            dve.tensor_scalar(g_i[:], ps[6][0:R, 0:S], gb[0:R, :], None, ALU.add)
            link(dve.tensor_scalar(g_f[:], ps[6][R:2 * R, 0:S], gb[R:2 * R, :], None, ALU.add))
            dve.tensor_scalar(g_l[:], g_f[:], 0.0, None, ALU.min)
            dve.scalar_tensor_tensor(out=g_n[:], in0=g_f[:], scalar=-1.0, in1=g_f[:], op0=ALU.mult, op1=ALU.min).then_inc(b_dve, 1)
            dve.wait_ge(b_dve, 1)
            dve.wait_ge(b_exp, 1)
            link(dve.tensor_tensor(g_l[:], g_l[:], g_n[:], ALU.subtract))
            dve.wait_ge(pool_const, 1)
            link(dve.tensor_tensor_scan(g_cs[:], ones[0:R, 0:1].to_broadcast([R, S]), g_l[:], 0.0, ALU.mult, ALU.add))
            link(dve.tensor_tensor(g_b[:], g_i[:], g_cs[:], ALU.subtract))
            link(dve.tensor_tensor_scan(g_g[:], g_b[:], g_b[:], -3.0e38, ALU.max, ALU.max))
            dve.tensor_tensor(g_m[:], g_cs[:], g_g[:], ALU.add).then_inc(b_dve, 1)
            link(dve.tensor_copy(gp[0:R, :], g_g[:]))
            link(dve.tensor_tensor(g_l[:], g_g[:], gp[0:R, :], ALU.subtract))
            link(dve.tensor_copy(g_part[:], g_l[:]))
            dve.tensor_copy(gp[R:2 * R, :], g_part[:])
            link(dve.tensor_tensor(g_f[:], g_l[:], g_part[:], ALU.subtract))
            dve.tensor_copy(gp[2 * R:3 * R, :], g_f[:]).then_inc(b_dve, 1)

            dve.wait_ge(c_wn, 1)
            dve.tensor_copy(wsum[:], ps[3][:, 0:E]).then_inc(c_wsum, 1)

            def b_divide(b):
                o = ps[7][:].rearrange("p (n d) -> p n d", d=HW)
                dve.wait_ge(b_ot, b + 1)
                em = bT[:, 1, :, NH * b:NH * b + NH].rearrange("p i (q f) -> p q i f", q=2)
                link(dve.tensor_tensor(hn[:].rearrange("p (q i f) -> p q i f", q=2, i=2),
                                       o[:, :, HD].rearrange("p (q i f) -> p q i f", q=2, i=2), em, ALU.max))
                link(dve.tensor_scalar(hn[:], hn[:], 1e-6, None, ALU.add))
                link(dve.reciprocal(hr[:], hn[:]))
                dve.tensor_tensor(hh[:], o[:, :, 0:HD], hr[:].unsqueeze(2).to_broadcast([P, 2 * NH, HD]), ALU.mult).then_inc(b_num, 1)
                dve.wait_ge(b_num, 2 * b + 1)
                link(dve.tensor_tensor(hq[:], hh[:], hh[:], ALU.mult))
                link(dve.tensor_reduce(hv[:], hq[:], AX.X, ALU.add))
                dve.tensor_scalar(hv2[:], hv[:], 1.0 / HD, 1e-6, ALU.mult, ALU.add).then_inc(pow_asked, 1)

            def b_norm(b):
                dve.wait_ge(pow_done, b + 1)
                link(dve.tensor_tensor(hq[:], hh[:], hv[:].unsqueeze(2).to_broadcast([P, 2 * NH, HD]), ALU.mult))
                link(dve.tensor_tensor(hh[:], hq[:], rms1[:].unsqueeze(1).to_broadcast([P, 2 * NH, HD]), ALU.mult))
                xx = X[:, 2 * b:2 * b + 2, :].rearrange("p i (q w) -> p q i w", q=2)
                dve.tensor_tensor(xx, xx, hh[:].rearrange("p (q i f) d -> p q i (f d)", q=2, i=2), ALU.add).then_inc(b_num, 1)

            for r in range(R):
                b, h = divmod(r, NH)
                dve.wait_ge(b_dec, r + 1)
                if r >= 2 * NH:
                    dve.wait_ge(b_pv, b - 1)
                dve.scalar_tensor_tensor(out=cT[:, r % (2 * NH), :], in0=ps[SCORE_BANK[r % 3]][:, 0:CUT], scalar=float(HD) ** -0.5,
                                         in1=dec[:, r % 3, :], op0=ALU.mult, op1=ALU.mult).then_inc(b_ct, 1)
                if h == 1 and b >= 2:
                    b_norm(b - 2)
                for c in range(EARLY):
                    k = r - (NH * (BC * c + 3) + 1)
                    if k == 0:
                        dve.wait_ge(b_num, 2 * BC * (c + 1))
                    if k in (0, 1):
                        tile_stats(c * CT + 2 * k, c * CT + 2 * k + 2)
                    if k == 2:
                        chunk_variance(c)
                    if 4 <= k < 4 + CT:
                        if c == 0 and k == 4:
                            dve.wait_ge(e_kvd, 32 * B)
                        tile_apply(c, k - 4)
                if h == 3 and b >= 1:
                    b_divide(b - 1)
            b_norm(B - 2)
            b_divide(B - 1)
            b_norm(B - 1)

            dve.wait_ge(e_kvd, 32 * B)
            for c in range(EARLY, C):
                dve.wait_ge(b_num, 2 * BC * (c + 1))
                layer_norm(c)
            dve.wait_ge(pow_done, B + 1)
            link(dve.tensor_tensor(den[:], xnm[:].unsqueeze(2).to_broadcast([P, T, E]),
                                   wn[:].unsqueeze(1).to_broadcast([P, T, E]), ALU.mult))
            link(dve.tensor_scalar(den[:], den[:], 1e-9, None, ALU.add))
            link(dve.reciprocal(rden[:], den[:]))
            dve.wait_ge(c_num, 1)
            link(dve.tensor_tensor(aff[:], ps[2][:, 0:T * E].rearrange("p (t e) -> p t e", e=E), rden[:], ALU.mult))
            dve.tensor_reduce(asum[:], aff[:], AX.XY, ALU.add).then_inc(c_sum, 1)
            link(dve.tensor_reduce(amax[:], aff[:], AX.X, ALU.max))

            def first_max(dst, scores, best, tiles=slice(0, T)):
                n = tiles.stop - tiles.start
                link(dve.tensor_tensor(eq[:, tiles], scores[:, tiles], best[:, tiles].unsqueeze(2).to_broadcast([P, n, E]), ALU.is_equal))
                link(dve.tensor_tensor(pri[:, tiles], eq[:, tiles], col("prio").unsqueeze(1).to_broadcast([P, n, E]), ALU.mult))
                link(dve.tensor_reduce(pm[:, tiles], pri[:, tiles], AX.X, ALU.max))
                return dve.tensor_tensor(dst[:, tiles], pri[:, tiles], pm[:, tiles].unsqueeze(2).to_broadcast([P, n, E]), ALU.is_equal)

            def slot_places(n, in_tile, in_all):
                total, running, over, place = (sums[:, k * E * T:k * E * T + E * n] for k in range(4))
                total, running, over = (a.rearrange("p (e t) -> p e t", e=E) for a in (total, running, over))
                place = place.rearrange("p (t e) -> p t e", e=E)
                link(dve.tensor_copy(total, in_all.rearrange("p (t e) -> p e t", e=E)))
                link(dve.tensor_tensor_scan(running.rearrange("p e t -> p (e t)"), ones[:, 0:E * n], total.rearrange("p e t -> p (e t)"),
                                            0.0, ALU.mult, ALU.add))
                link(dve.tensor_tensor(running, running, total, ALU.subtract))
                link(dve.tensor_reduce(size[:], total, AX.X, ALU.add))
                link(dve.tensor_tensor(over, size[:].unsqueeze(2).to_broadcast([P, E, n]),
                                       cst("tile_sizes")[:, 0:n].unsqueeze(1).to_broadcast([P, E, n]), ALU.is_gt))
                link(dve.tensor_reduce(tiles_of[:], over, AX.X, ALU.add))
                link(dve.tensor_tensor_scan(tile_end[:], ones[:, 0:E], tiles_of[:], 0.0, ALU.mult, ALU.add))
                link(dve.tensor_tensor(shift[:], tile_end[:], tiles_of[:], ALU.subtract))
                link(dve.scalar_tensor_tensor(out=shift[:], in0=shift[:], scalar=float(P), in1=running[:, :, 0], op0=ALU.mult, op1=ALU.subtract))
                link(dve.tensor_tensor(place, in_tile.rearrange("p (t e) -> p t e", e=E), running.rearrange("p e t -> p t e"), ALU.add))
                return place, dve.tensor_tensor(place, place, shift[:].unsqueeze(1).to_broadcast([P, n, E]), ALU.add)

            def slot_experts(n, dst):
                link(dve.tensor_tensor(passed[:, 0:n], tile_end[:].unsqueeze(1).to_broadcast([P, n, E]),
                                       cst("slot")[:, 0:n].unsqueeze(2).to_broadcast([P, n, E]), ALU.is_le))
                link(dve.tensor_reduce(expert_f[:, 0:n], passed[:, 0:n], AX.X, ALU.add))
                link(dve.tensor_scalar(expert_f[:, 0:n], expert_f[:, 0:n], float(E - 1), None, ALU.min))
                return dve.tensor_copy(dst, expert_f[:, 0:n])

            first_max(oh, aff[:], amax).then_inc(c_oh, 1)
            dve.wait_ge(c_mean, 1)
            dve.scalar_tensor_tensor(out=zc[:], in0=ps[7][:, 0:1], scalar=1.0 / (T * P * E), in1=col("thr"),
                                     op0=ALU.mult, op1=ALU.subtract).then_inc(c_z, 1)
            dve.wait_ge(c_g0, 1)
            dve.tensor_copy(G0[:], ps[6][0:E, 0:D]).then_inc(c_g0c, 1)
            dve.wait_ge(c_sig, 1)
            link(dve.tensor_scalar(cap[:], sg[:], float(S), 4.0, ALU.mult, ALU.max))
            link(dve.tensor_scalar(cap[:], cap[:], float(S), None, ALU.min))
            for t in range(T):
                dve.wait_ge(c_row, t + 1)
                m = (t % 2) * S
                row = ps[4 + t % 2][:, 0:S]
                lo, hi = (slice(0, P), slice(0, S)) if t % 2 == 0 else (slice(0, S), slice(P, S))
                if t >= 1:
                    dve.wait_ge(c_cnt, t)
                own = amax[:, t:t + 1]
                dve.scalar_tensor_tensor(out=cj[:, 0, lo], in0=row[:, lo], scalar=own, in1=cst("before")[:, m:m + S][:, lo],
                                         op0=ALU.is_ge, op1=ALU.mult, accum_out=cnt[:, 0, t:t + 1])
                dve.scalar_tensor_tensor(out=cj[:, 1, hi], in0=row[:, hi], scalar=own, in1=cst("after")[:, m:m + S][:, hi],
                                         op0=ALU.is_gt, op1=ALU.mult, accum_out=cnt[:, 1, t:t + 1]).then_inc(c_cnt, 1)
            dve.wait_ge(c_cnt, T)
            link(dve.scalar_tensor_tensor(out=rank1[:], in0=cnt[:, 0, :], scalar=1.0, in1=cnt[:, 1, :], op0=ALU.add, op1=ALU.add))
            link(dve.tensor_scalar(keep[:], rank1[:], cap[:], None, ALU.is_le))
            link(dve.tensor_tensor(disp[:], oh[:], keep[:].unsqueeze(2).to_broadcast([P, T, E]), ALU.mult))
            dve.tensor_scalar(ndisp[:], disp[:], -1.0, 1.0, ALU.mult, ALU.add).then_inc(c_nd, 1)
            dve.wait_ge(c_totals, 1)
            place, last = slot_places(T, ps[4][:, 0:T * E], ps[5][:, 0:T * E])
            link(last)
            link(dve.tensor_tensor(place, place, disp[:], ALU.mult))
            dve.tensor_scalar(unsent[:], keep[:], -1.0, 1.0, ALU.mult, ALU.add)
            link(dve.tensor_reduce(row_of[:], place, AX.X, ALU.add))
            link(dve.tensor_tensor(unsent[:], unsent[:], cst("spare"), ALU.mult))
            link(dve.tensor_tensor(row_of[:], row_of[:], unsent[:], ALU.add))
            link(dve.tensor_scalar(unsent[:], row_of[:], float(C_ZERO), None, ALU.min))
            dve.tensor_copy(to_row[:], row_of[:]).then_inc(c_rows, 1)
            dve.tensor_copy(from_row[:], unsent[:])
            slot_experts(C_SLOTS, expert_of[:]).then_inc(c_expert, 1)
            dve.wait_ge(c_expert, 1)

            def c_weights(n):
                e = dve.value_load(expert_of[0:1, n:n + 1], min_val=0, max_val=E - 1)
                if n == 0:
                    dve.wait_ge(s_w1, 16)
                if n >= 2:
                    dve.wait_ge(c_act, n - 1)
                dve.tensor_copy(w1_now[:, n % 2, :], w1[:, bass.ds(e, 1), :].rearrange("p a f -> p (a f)"))
                b1 = col("b1").rearrange("p (e k) -> p e k", e=E)
                dve.tensor_copy(b1_now[:, n % 2, :], b1[:, bass.ds(e, 1), :].rearrange("p a k -> p (a k)")).then_inc(c_w, 1)

            for n in range(2):
                c_weights(n)
            for c in range(C):
                dve.wait_ge(c_base, c + 1)
                ch = X[:, c * CT:(c + 1) * CT, :]
                dve.tensor_tensor(ch, ps[6 + c % 2][:].rearrange("p (t d) -> p t d", d=D), ch, ALU.add).then_inc(c_badd, 1)
            for n in range(2, C_SLOTS + 2):
                if n < C_SLOTS:
                    c_weights(n)
                done = n - 1
                if done % CT == 0 or done == C_SLOTS:
                    g = (done - 1) // CT
                    w = (done - g * CT) * P
                    dve.wait_ge(c_y, done)
                    if g >= C:
                        dve.wait_ge(slot_stored[g - C], 16)
                    dve.tensor_copy(yg[:, g % C, 0:w], ps[6 + g % 2][:, 0:w]).then_inc(c_yc, 1)

            def c_residual(c):
                dve.wait_ge(token_back[c], 16 * CT)
                if c == 0:
                    dve.wait_ge(c_badd, C)
                ch = X[:, c * CT:(c + 1) * CT, :]
                dve.tensor_tensor(ch, XN[:, c * CT:(c + 1) * CT, :], ch, ALU.add).then_inc(c_acc, 1)

            def d_scan_chunk(c):
                k = c % 2
                dve.wait_ge(d_act, c + 1)
                if c >= 2:
                    dve.wait_ge(d_turn, c - 1)
                dve.tensor_scalar(decay[:, k, :], state[:, k, :], 0.998, 0.001, ALU.mult, ALU.add)
                link(dve.tensor_tensor(gate[:, k, :], gate[:, k, :], tnh[:, k, :], ALU.mult))
                for b in range(BC):
                    sl = slice(b * S, (b + 1) * S)
                    last = dve.tensor_tensor_scan(drive[:, k, sl], decay[:, k, sl], gate[:, k, sl], 0.0, ALU.mult, ALU.add)
                last.then_inc(d_scan, 1)

            def d_residual(c):
                dve.wait_ge(d_turn, c + 1)
                ch = X[:, c * CT:(c + 1) * CT, :]
                dve.tensor_tensor(ch, ps[5][:].rearrange("p (t d) -> p t d", d=D), ch, ALU.add).then_inc(d_add, 1)

            key_parts = [0]

            def split_keys(b):
                dve.wait_ge(e_ks[b % 2], 16 * (b // 2 + 1))
                if b >= 2:
                    dve.wait_ge(e_kt, 2 * (b - 1))
                src = Ks[:, b % 2].rearrange("p (a i) d -> p i a d", i=2)
                va, vb = (v[:].rearrange("p (a i) d -> p i a d", i=2) for v in (r1, r2))
                slot = [KK[:, b % 2, :, :, AD * j:AD * (j + 1)] for j in range(6)]
                key_parts[0] = split_parts(dve, e_kpart, key_parts[0], src, va, vb, slot[0], slot[2], slot[4])
                dve.tensor_copy(slot[1], slot[0])
                dve.tensor_copy(slot[3], slot[0])
                dve.tensor_copy(slot[5], slot[2]).then_inc(e_kk, 1)

            for b in range(2):
                split_keys(b)
            for c in range(C):
                c_residual(c)
                dve.wait_ge(c_acc, c + 1)
                layer_norm(c)
                split_keys(c + 2)
                if c >= 1:
                    d_scan_chunk(c - 1)
                if c >= 2:
                    d_residual(c - 2)
            d_scan_chunk(C - 1)
            d_residual(C - 2)
            for c in range(C):
                dve.wait_ge(d_add, c + 1)
                layer_norm(c)
                if c == 0:
                    d_residual(C - 1)
                if c % 2 == 1:
                    split_keys(6 + c // 2)

            def best_two(h):
                part = slice(PARTS[h].start, PARTS[h].stop)
                link(dve.tensor_reduce(amax[:, part], aff[:, part], AX.X, ALU.max))
                link(first_max(oh, aff, amax, part))
                link(dve.scalar_tensor_tensor(out=rden[:, part], in0=oh[:, part], scalar=-3.0e38, in1=aff[:, part], op0=ALU.mult, op1=ALU.add))
                link(dve.tensor_reduce(f_m2[:, part], rden[:, part], AX.X, ALU.max))
                dve.tensor_tensor(f_z[:, part], f_m2[:, part], amax[:, part], ALU.subtract).then_inc(f_d, 1)
                link(first_max(ndisp, rden, f_m2, part))
                dve.tensor_tensor(disp[:, part], oh[:, part], ndisp[:, part], ALU.add).then_inc(f_top, 1)

            def route(h):
                part = slice(PARTS[h].start, PARTS[h].stop)
                width = len(PARTS[h]) * E
                f = fill_of["route", h, 0]
                dve.wait_ge(e_turn, f + 1)
                place, last = slot_places(len(PARTS[h]), ps[f % 2][:, 0:width], ps[f % 2][:, width:2 * width])
                last.then_inc(e_read, 1)
                dve.wait_ge(e_read, read_count(f))
                for j, pick in enumerate((oh, ndisp)):
                    link(dve.tensor_tensor(eq[:, part], place, pick[:, part], ALU.mult))
                    link(dve.tensor_reduce(f_row[:, part], eq[:, part], AX.X, ALU.add))
                    last = dve.tensor_copy(f_rows[:, j, part], f_row[:, part])
                    if j == 0:
                        link(last)
                last.then_inc(f_sorted, 1)
                slot_experts(F_SLOTS[h], f_expert_of[:, FIRST_SLOT[h]:FIRST_SLOT[h + 1]]).then_inc(f_expert, 1)
                dve.wait_ge(f_ex, h + 1)
                link(dve.tensor_scalar(f_p[:, part], f_e[:, part], 1.0, None, ALU.add))
                link(dve.reciprocal(f_m2[:, part], f_p[:, part]))
                link(dve.tensor_tensor(f_p2[:, part], f_e[:, part], f_m2[:, part], ALU.mult))

            def f_weights(h, m):
                n = FIRST_SLOT[h] + m
                if m == 0:
                    dve.wait_ge(f_expert, h + 1)
                e = dve.value_load(f_expert_of[0:1, n:n + 1], min_val=0, max_val=E - 1)
                if n == 0:
                    dve.wait_ge(s_w12, 16)
                    dve.wait_ge(e_i, NP)
                if n >= 2:
                    dve.wait_ge(f_h, n - 1)
                dve.tensor_copy(w12_now[:, n % 2, :], w12[:, bass.ds(e, 1), :].rearrange("p a f -> p (a f)")).then_inc(f_w, 1)

            query_parts = [0]

            def part(ins):
                ins.then_inc(e_qpart, 1)
                query_parts[0] += 1

            def split_queries(b, k):
                n = b % 2
                if k == 0:
                    dve.wait_ge(e_fill, 3)
                    dve.wait_ge(e_qs[n], 16 * (b // 2 + 1))
                    if b >= 2:
                        dve.wait_ge(e_turn, fill_of["q2", b - 2, 1] + 1)
                elif k < 6:
                    dve.wait_ge(e_qpart, query_parts[0])
                src = Qs[:, n].rearrange("p (a i) d -> p i a d", i=2)
                left1, left2 = (v[:].rearrange("p (a i) d -> p i a d", i=2) for v in (q1, q2))
                slot = [QQ[:, n, :, :, AD * j:AD * (j + 1)] for j in range(6)]
                if k == 0:
                    part(dve.tensor_copy(slot[0], src))
                elif k == 1:
                    part(dve.tensor_tensor(left1, src, slot[0], ALU.subtract))
                elif k == 2:
                    part(dve.tensor_copy(slot[1], left1))
                elif k == 3:
                    part(dve.tensor_tensor(left2, left1, slot[1], ALU.subtract))
                elif k == 4:
                    part(dve.tensor_copy(slot[3], left2))
                elif k == 5:
                    dve.tensor_copy(slot[2], slot[0])
                elif k == 6:
                    dve.tensor_copy(slot[4], slot[0])
                else:
                    dve.tensor_copy(slot[5], slot[1]).then_inc(e_qq, 1)

            def split_maxima(b, k):
                n = b % 2
                hi, mid, lo = (QQ[:, n, :, :, 6 * AD + j] for j in range(3))
                if k == 0:
                    dve.wait_ge(e_max, NA * (b + 1))
                    dve.tensor_scalar(mx[:, 0, :], mx3[:, n, :, 0], -1.0, None, ALU.mult)
                    link(dve.tensor_tensor(mr[:, 0, :], mx3[:, n, :, 1], mx3[:, n, :, 2], ALU.max))
                    part(dve.tensor_scalar(mx[:, 1, :], mr[:, 0, :], -1.0, None, ALU.mult))
                elif k == 1:
                    dve.wait_ge(e_qpart, query_parts[0])
                    part(dve.tensor_copy(hi, mx[:]))
                    dve.wait_ge(e_qpart, query_parts[0])
                    part(dve.tensor_tensor(mr[:], mx[:], hi, ALU.subtract))
                else:
                    dve.wait_ge(e_qpart, query_parts[0])
                    part(dve.tensor_copy(mid, mr[:]))
                    dve.wait_ge(e_qpart, query_parts[0])
                    part(dve.tensor_tensor(mr2[:], mr[:], mid, ALU.subtract))
                    dve.wait_ge(e_qpart, query_parts[0])
                    dve.tensor_copy(lo, mr2[:]).then_inc(e_mq, 1)

            for step in range(FIRST, LAST):
                for k in range(8):
                    b = batch_at(step, AT_SPLIT + k)
                    if b is not None:
                        split_queries(b, k)
                for k in range(3):
                    b = batch_at(step, AT_MAX + k)
                    if b is not None:
                        split_maxima(b, k)
                g = group_at(step, AT_GROUP)
                if g is not None:
                    b, a = divmod(g * OG, NA)
                    f = fill_of["group", g, 0]
                    dve.wait_ge(e_turn, f + 1)
                    if a == 0 and b >= 2:
                        dve.wait_ge(e_od[b % 2], 16 * (b // 2))
                    o = ps[f % 2][:, 0:2 * P].rearrange("p (i a d) -> p i a d", i=2, d=OW)
                    dve.reciprocal(orec[:], o[:, :, :, AD]).then_inc(e_rec, 1)
                    dve.wait_ge(e_rec, g + 1)
                    dst = Os[:, b % 2, 2 * a:2 * (a + OG), :].rearrange("p (a i) d -> p i a d", i=2)
                    dve.tensor_tensor(dst, o[:, :, :, 0:AD], orec[:].unsqueeze(3).to_broadcast([P, 2, OG, AD]), ALU.mult).then_inc(e_read, 1)
                    dve.wait_ge(e_read, read_count(f))
                    dve.sem_inc(e_o, 1)
                n = step
                if 0 <= n < NP:
                    b, a = divmod(n, NA)
                    dve.wait_ge(e_i, n + 1)
                    dve.tensor_reduce(mx3[:, b % 2, a, :], ps[2 + n % 2][:, 0:CUT].rearrange("p (g j) -> p g j", g=3), AX.X, ALU.max).then_inc(e_max, 1)
                b = batch_at(step, AT_Y)
                if b is not None:
                    f = fill_of["y", b, 0]
                    dve.wait_ge(e_turn, f + 1)
                    xx = X[:, 2 * b:2 * b + 2, :]
                    dve.tensor_tensor(xx, ps[f % 2][:, 0:2 * P].rearrange("p (t d) -> p t d", d=D), xx, ALU.add).then_inc(e_read, 1)
                    dve.wait_ge(e_read, read_count(f))
                    dve.sem_inc(e_add, 1)
                c = chunk_at(step, AT_STATS)
                if c is not None:
                    norm_stats(c)
                c = chunk_at(step, AT_NORM)
                if c is not None:
                    norm_apply(c)
                c = chunk_at(step, AT_GATE)
                if c is not None:
                    f = fill_of["gate", c, 0]
                    dve.wait_ge(e_turn, f + 1)
                    dve.tensor_copy(aff[:, c * CT:(c + 1) * CT], ps[f % 2][:, 0:CT * E].rearrange("p (t e) -> p t e", e=E)).then_inc(e_read, 1)
                h = part_at(step, AT_TOP)
                if h is not None:
                    dve.wait_ge(e_read, read_count(fill_of["gate", PARTS[h].stop // CT - 1, 0]))
                    best_two(h)
                h = part_at(step, AT_PLACE)
                if h is not None:
                    route(h)
                for start in SLOT_START:
                    if step == start - 1:
                        for m in range(2):
                            f_weights(SLOT_START.index(start), m)
                slot = slots_at(step)
                if slot is not None:
                    h, m = slot
                    n = FIRST_SLOT[h] + m
                    dve.wait_ge(f_silu, n + 1)
                    if n >= 2:
                        dve.wait_ge(f_y, n - 1)
                    dve.tensor_tensor(f_hS[:, n % 2, GH:, :], ps[2 + n % 2][:, GH * P:].rearrange("p (k c) -> p k c", k=GH),
                                      f_hS[:, n % 2, 0:GH, :], ALU.mult).then_inc(f_mul, 1)
                    if m + 2 < F_SLOTS[h]:
                        f_weights(h, m + 2)
                slot = slots_at(step, 1)
                if slot is not None and (slot[1] % CT == CT - 1 or slot[1] == F_SLOTS[slot[0]] - 1):
                    h, m = slot
                    group = FIRST_GROUP[h] + m // CT
                    w = (m % CT + 1) * P
                    dve.wait_ge(f_y, FIRST_SLOT[h] + m + 1)
                    if group >= 4:
                        h, g = part_and_group(group - 4)
                        dve.wait_ge(slot_stored[g], 16 * loads_of(h, g))
                    dve.tensor_copy(f_yg[:, group % 4, 0:w], ps[4 + group % 2][:, 0:w]).then_inc(f_yc, 1)

            for c in range(C):
                dve.wait_ge(token_back[c], 16 * CT + 16 * TOP * CT)
                for j, weight in enumerate((f_m2, f_p2)):
                    for t in range(c * CT, (c + 1) * CT):
                        last = dve.scalar_tensor_tensor(out=X[:, t, :], in0=f_back_rows[:, j, t, :], scalar=weight[:, t:t + 1],
                                                        in1=X[:, t, :], op0=ALU.mult, op1=ALU.add)
                    last.then_inc((f_first, f_acc)[j], 1)
                    dve.wait_ge((f_first, f_acc)[j], c + 1)


def _constants():
    c = np.zeros((P, NCONST), np.float32)
    i = np.arange(P)
    c[:, 0:P] = np.eye(P, dtype=np.float32)
    c[:, P:2 * P] = np.where(i[:, None] > i[None, :], NEG, 0.0)
    c[:, 2 * P:3 * P] = np.where(i[None, :] > i[:, None], NEG, 0.0)
    at = CONST["minus3"][0]
    c[0:3 * R, at:at + R] = -np.tile(np.eye(R, dtype=np.float32), (3, 1))
    for name, values in (("earlier", i[:, None] < i[None, :]), ("tile_sizes", P * np.arange(T)[None, :]),
                         ("slot", np.arange(MAX_SLOTS)[None, :]), ("spare", C_ZERO + P * np.arange(T)[None, :] + i[:, None])):
        at, width = CONST[name]
        c[:, at:at + width] = values
    s = np.arange(S)
    for h in range(2):
        before = (s[None, :] < (h * P + i)[:, None]).astype(np.float32)
        c[:, 3 * P + h * S:3 * P + (h + 1) * S] = before
        c[:, 3 * P + 2 * S + h * S:3 * P + 2 * S + (h + 1) * S] = 1.0 - before
    return c


def kernel(**inputs):
    import concourse.bacc as _bacc
    from concourse import mybir as _mybir
    from concourse.bass_utils import run_bass_kernel_spmd as _run

    g = {k: np.asarray(v) for k, v in inputs.items()}
    small = np.zeros((P, NCOLS), np.float32)

    def put(name, a):
        at, w = COLS[name]
        small[0:a.shape[0], at:at + w] = a

    bp = g["L0_attn_bp"].reshape(3, D)
    put("bw", bp[0][:, None])
    put("bk", bp[1][:, None])
    put("bu", g["L0_attn_bu"][:, None])
    put("bg", g["L1_attn_bg"][:, None])
    put("bv", g["L1_attn_bv"][:, None])
    put("bd", g["L1_attn_bd"][:, None])
    put("b1", g["L0_ffn_b1"].reshape(E * FK, P).T)
    gi, gf = g["L0_xattn_igate_kernel"].reshape(3, D, NH), g["L0_xattn_fgate_kernel"].reshape(3, D, NH)
    for n, name in enumerate(("gq", "gk", "gv")):
        put(name, np.concatenate([gi[n], gf[n]], axis=1))
    put("gbias", np.concatenate([np.tile(g["L0_xattn_igate_bias"], B), np.tile(g["L0_xattn_fgate_bias"], B)])[:, None])
    put("thr", np.broadcast_to(g["L0_ffn_affinity_threshold"].reshape(1, 1), (P, 1)))
    put("rms", np.broadcast_to(g["L0_xattn_rms_scale"][None, :], (P, HD)))
    put("bo", np.broadcast_to(g["L0_attn_bo"][None, :], (P, D)))
    put("waffT", g["L0_ffn_waff"].T)
    put("gateT", g["L1_ffn_gate_w"].T)
    put("b2", g["L0_ffn_b2"])
    put("prio", np.broadcast_to(np.arange(E, 0, -1, dtype=np.float32)[None, :], (P, E)))

    arrays = {
        "x": g["x"].reshape(B * S, D),
        "ctx": g["ctx_1024"].reshape(B * S, D),
        "ctxT": g["ctx_1024"].reshape(B * S, D).T,
        "small": small,
        "const": _constants(),
        "wp": g["L0_attn_Wp"],
        "wu": g["L0_attn_Wu"],
        "wo": g["L0_attn_Wo"],
        "w1": g["L0_ffn_W1"].transpose(1, 0, 2),
        "w2": g["L0_ffn_W2"].reshape(E, FK, P, D).transpose(2, 0, 1, 3),
        "lw": np.concatenate([g["L1_attn_Wg"].T, g["L1_attn_Wv"].T, g["L1_attn_Wd"].T], axis=1),
        "aw": np.concatenate([g["L1_xattn_wq"].T, g["L1_xattn_wk"].T, g["L1_xattn_wv"].T, g["L1_xattn_wo"].T], axis=1),
        "w12": g["L1_ffn_w12"].transpose(2, 0, 1),
        "w3": g["L1_ffn_w3"].reshape(E, D, GH, P).transpose(3, 0, 2, 1),
    }
    nc = _bacc.Bacc("TRN2", target_bir_lowering=False, num_devices=1)
    feed, args = {}, []
    for name, a in arrays.items():
        a = np.ascontiguousarray(a)
        feed[f"in_{name}"] = a
        args.append(nc.dram_tensor(f"in_{name}", a.shape, _mybir.dt.from_np(a.dtype), kind="ExternalInput").ap())
    args.append(nc.dram_tensor("out_x", (B * S, D), F32, kind="ExternalOutput").ap())
    build(nc, *args)
    r = _run(nc, [feed], core_ids=[0])
    return r.results[0]["out_x"].reshape(B, S, D)
```
